# Optimizing a Trainium2 kernel written in Bass

```python
import numpy as np
import jax
import jax.numpy as jnp

def _softmax(x, axis=-1):
    return jax.nn.softmax(x, axis=axis)

def _gelu(x):
    return jax.nn.gelu(x, approximate=True)

def _silu(x):
    return jax.nn.silu(x)

def _sigmoid(x):
    return jax.nn.sigmoid(x)

def _layernorm(x, axis=-1, eps=1e-05):
    m = jnp.mean(x, axis=axis, keepdims=True)
    v = jnp.var(x, axis=axis, keepdims=True)
    return (x - m) / jnp.sqrt(v + eps)

def _scatter_add(tgt, idx, src, axis=0):
    return tgt.at[idx].add(src)

def _segment_sum(src, seg, n):
    return jax.ops.segment_sum(src, seg, n)
kernel_name = 'mk_cond_resid_d2_seqx_r8_2ae67f'

def setup_inputs(seed: int=0):
    np.random.seed(seed)
    _w = jnp.asarray

    def _rec_inputs():
        import jax
        import jax.numpy as jnp
        _rk = jax.random.key(seed)
        x = -5.13e-06 + 0.01765 * jax.random.normal(jax.random.fold_in(_rk, 1), (32, 32, 128), jnp.float32)
        _lenS = 32 - jax.random.randint(jax.random.fold_in(_rk, 7), (32,), 0, max(1, 32 // 4) + 1, jnp.int32)
        _lenS2 = 32 - jax.random.randint(jax.random.fold_in(_rk, 8), (32,), 0, max(1, 32 // 4) + 1, jnp.int32)
        cond_1024 = 0.0061147 + 1.02565 * jax.random.normal(jax.random.fold_in(_rk, 11), (32, 128), jnp.float32)
        return (x, cond_1024)
    x, cond_1024 = _rec_inputs()

    def _L0_cond_setup():
        import math
        import jax, jax.numpy as jnp
        import numpy as np
        EPS = 1e-07
        MAX_TANH_ARG = 1.0 - 1e-05

        def _norm(x):
            return jnp.sqrt(jnp.sum(x * x, axis=-1, keepdims=True)).clip(EPS)

        def logmap0(x):
            n = _norm(x)
            return jnp.arctanh(jnp.clip(n, EPS, MAX_TANH_ARG)) * x / n

        def expmap0(v):
            n = _norm(v)
            return jnp.tanh(n) * v / n

        def mobius_add(x, y):
            x2 = jnp.sum(x * x, -1, keepdims=True)
            y2 = jnp.sum(y * y, -1, keepdims=True)
            xy = jnp.sum(x * y, -1, keepdims=True)
            num = (1 + 2 * xy + y2) * x + (1 - x2) * y
            den = (1 + 2 * xy + x2 * y2).clip(EPS)
            return num / den

        def plin(x, w, b):
            return expmap0(logmap0(x) @ w + b)

        def layer_norm(x, eps=1e-06):
            m = x.mean(-1, keepdims=True)
            v = ((x - m) ** 2).mean(-1, keepdims=True)
            return (x - m) / jnp.sqrt(v + eps)

        def _beta(a, b):
            return math.exp(math.lgamma(a) + math.lgamma(b) - math.lgamma(a + b))
        D, H, FF = (128, 16, 512)
        HD = D // H
        BETA_N = _beta(D / 2, 0.5)
        BETA_H = _beta(HD / 2, 0.5)

        def _to_heads(p):
            B, S, _ = p.shape
            t = logmap0(p).reshape(B, S, H, HD) * (BETA_H / BETA_N)
            return expmap0(jnp.transpose(t, (0, 2, 1, 3)))

        def _from_heads(ph):
            B, _, S, _ = ph.shape
            t = logmap0(ph) * (BETA_N / BETA_H)
            t = jnp.transpose(t, (0, 2, 1, 3)).reshape(B, S, D)
            return expmap0(t)
        key = jax.random.key(seed)
        ks = jax.random.split(key, 20)
        B, S = (4, 128)
        x = expmap0(0.02 * jax.random.normal(ks[0], (B, S, D), jnp.float32))
        t_emb = jax.random.normal(ks[1], (B, 1, D), jnp.float32)
        g = lambda k, sh: 0.02 * jax.random.normal(k, sh, jnp.float32)
        return {'x': x, 't_emb': t_emb, 'w_q': g(ks[2], (D, D)), 'b_q': jnp.zeros((D,), jnp.float32), 'w_k': g(ks[3], (D, D)), 'b_k': jnp.zeros((D,), jnp.float32), 'w_v': g(ks[4], (D, D)), 'b_v': jnp.zeros((D,), jnp.float32), 'w_o': g(ks[5], (D, D)), 'b_o': jnp.zeros((D,), jnp.float32), 'w_f1': g(ks[6], (D, FF)), 'b_f1': jnp.zeros((FF,), jnp.float32), 'w_f2': g(ks[7], (FF, D)), 'b_f2': jnp.zeros((D,), jnp.float32), 'w_ada': g(ks[8], (D, 6 * D)), 'b_ada': jnp.zeros((6 * D,), jnp.float32)}
    _L0_cond_all = _L0_cond_setup()
    _L0_cond_in = {k: v for k, v in _L0_cond_all.items() if k in ('w_q', 'b_q', 'w_k', 'b_k', 'w_v', 'b_v', 'w_o', 'b_o', 'w_f1', 'b_f1', 'w_f2', 'b_f2', 'w_ada', 'b_ada')}
    del _L0_cond_all

    def _L1_cond_setup():
        import jax, jax.numpy as jnp
        import numpy as np
        NUM_EXPERTS = 4
        TOP_K = 2
        key = jax.random.key(seed)
        ks = jax.random.split(key, 16)
        B, L, D, E, H = (8, 96, 128, NUM_EXPERTS, 512)
        s = 0.02
        return {'context_c': jax.random.normal(ks[0], (B, L, D), jnp.float32), 'time_cond': jax.random.normal(ks[1], (B, D), jnp.float32), 'gate_w': jax.random.normal(ks[2], (3 * D, E), jnp.float32) * s, 'gate_b': jnp.zeros((E,), jnp.float32), 'time_w': jax.random.normal(ks[3], (D, 2 * E), jnp.float32) * s, 'time_b': jnp.zeros((2 * E,), jnp.float32), 'ew1': jax.random.normal(ks[4], (E, D, H), jnp.float32) * s, 'eb1': jnp.zeros((E, H), jnp.float32), 'ew2': jax.random.normal(ks[5], (E, H, D), jnp.float32) * s, 'eb2': jnp.zeros((E, D), jnp.float32), 'sw1': jax.random.normal(ks[6], (D, H), jnp.float32) * s, 'sb1': jnp.zeros((H,), jnp.float32), 'sw2': jax.random.normal(ks[7], (H, D), jnp.float32) * s, 'sb2': jnp.zeros((D,), jnp.float32)}
    _L1_cond_all = _L1_cond_setup()
    _L1_cond_in = {k: v for k, v in _L1_cond_all.items() if k in ('gate_w', 'gate_b', 'time_w', 'time_b', 'ew1', 'eb1', 'ew2', 'eb2', 'sw1', 'sb1', 'sw2', 'sb2')}
    del _L1_cond_all
    return {'x': x, 'cond_1024': cond_1024, 'L0_cond_w_q': _L0_cond_in['w_q'], 'L0_cond_b_q': _L0_cond_in['b_q'], 'L0_cond_w_k': _L0_cond_in['w_k'], 'L0_cond_b_k': _L0_cond_in['b_k'], 'L0_cond_w_v': _L0_cond_in['w_v'], 'L0_cond_b_v': _L0_cond_in['b_v'], 'L0_cond_w_o': _L0_cond_in['w_o'], 'L0_cond_b_o': _L0_cond_in['b_o'], 'L0_cond_w_f1': _L0_cond_in['w_f1'], 'L0_cond_b_f1': _L0_cond_in['b_f1'], 'L0_cond_w_f2': _L0_cond_in['w_f2'], 'L0_cond_b_f2': _L0_cond_in['b_f2'], 'L0_cond_w_ada': _L0_cond_in['w_ada'], 'L0_cond_b_ada': _L0_cond_in['b_ada'], 'L1_cond_gate_w': _L1_cond_in['gate_w'], 'L1_cond_gate_b': _L1_cond_in['gate_b'], 'L1_cond_time_w': _L1_cond_in['time_w'], 'L1_cond_time_b': _L1_cond_in['time_b'], 'L1_cond_ew1': _L1_cond_in['ew1'], 'L1_cond_eb1': _L1_cond_in['eb1'], 'L1_cond_ew2': _L1_cond_in['ew2'], 'L1_cond_eb2': _L1_cond_in['eb2'], 'L1_cond_sw1': _L1_cond_in['sw1'], 'L1_cond_sb1': _L1_cond_in['sb1'], 'L1_cond_sw2': _L1_cond_in['sw2'], 'L1_cond_sb2': _L1_cond_in['sb2']}

def reference(x, cond_1024, L0_cond_w_q, L0_cond_b_q, L0_cond_w_k, L0_cond_b_k, L0_cond_w_v, L0_cond_b_v, L0_cond_w_o, L0_cond_b_o, L0_cond_w_f1, L0_cond_b_f1, L0_cond_w_f2, L0_cond_b_f2, L0_cond_w_ada, L0_cond_b_ada, L1_cond_gate_w, L1_cond_gate_b, L1_cond_time_w, L1_cond_time_b, L1_cond_ew1, L1_cond_eb1, L1_cond_ew2, L1_cond_eb2, L1_cond_sw1, L1_cond_sb1, L1_cond_sw2, L1_cond_sb2):
    import jax
    import jax.numpy as jnp

    def _L0_cond_ref(x, t_emb, w_q, b_q, w_k, b_k, w_v, b_v, w_o, b_o, w_f1, b_f1, w_f2, b_f2, w_ada, b_ada):
        import math
        import jax, jax.numpy as jnp
        import numpy as np
        EPS = 1e-07
        MAX_TANH_ARG = 1.0 - 1e-05

        def _norm(x):
            return jnp.sqrt(jnp.sum(x * x, axis=-1, keepdims=True)).clip(EPS)

        def logmap0(x):
            n = _norm(x)
            return jnp.arctanh(jnp.clip(n, EPS, MAX_TANH_ARG)) * x / n

        def expmap0(v):
            n = _norm(v)
            return jnp.tanh(n) * v / n

        def mobius_add(x, y):
            x2 = jnp.sum(x * x, -1, keepdims=True)
            y2 = jnp.sum(y * y, -1, keepdims=True)
            xy = jnp.sum(x * y, -1, keepdims=True)
            num = (1 + 2 * xy + y2) * x + (1 - x2) * y
            den = (1 + 2 * xy + x2 * y2).clip(EPS)
            return num / den

        def plin(x, w, b):
            return expmap0(logmap0(x) @ w + b)

        def layer_norm(x, eps=1e-06):
            m = x.mean(-1, keepdims=True)
            v = ((x - m) ** 2).mean(-1, keepdims=True)
            return (x - m) / jnp.sqrt(v + eps)

        def _beta(a, b):
            return math.exp(math.lgamma(a) + math.lgamma(b) - math.lgamma(a + b))
        D, H, FF = (128, 16, 512)
        HD = D // H
        BETA_N = _beta(D / 2, 0.5)
        BETA_H = _beta(HD / 2, 0.5)

        def _to_heads(p):
            B, S, _ = p.shape
            t = logmap0(p).reshape(B, S, H, HD) * (BETA_H / BETA_N)
            return expmap0(jnp.transpose(t, (0, 2, 1, 3)))

        def _from_heads(ph):
            B, _, S, _ = ph.shape
            t = logmap0(ph) * (BETA_N / BETA_H)
            t = jnp.transpose(t, (0, 2, 1, 3)).reshape(B, S, D)
            return expmap0(t)
        ada = t_emb @ w_ada + b_ada
        sh_msa, sc_msa, g_msa, sh_mlp, sc_mlp, g_mlp = jnp.split(ada, 6, axis=-1)
        residual = x
        xn = layer_norm(logmap0(x))
        xm = expmap0(xn * (1 + sc_msa) + sh_msa)
        q = _to_heads(plin(xm, w_q, b_q))
        k = _to_heads(plin(xm, w_k, b_k))
        v = _to_heads(plin(xm, w_v, b_v))
        qt, kt, vt = (logmap0(q), logmap0(k), logmap0(v))
        scores = jnp.einsum('bhqd,bhkd->bhqk', qt, kt) / math.sqrt(HD)
        attn = jax.nn.softmax(scores, axis=-1)
        out_h = expmap0(jnp.einsum('bhqk,bhkd->bhqd', attn, vt))
        attn_out = plin(_from_heads(out_h), w_o, b_o)
        attn_t = g_msa * logmap0(attn_out)
        x = mobius_add(residual, expmap0(attn_t))
        residual = x
        xn = layer_norm(logmap0(x))
        xm = expmap0(xn * (1 + sc_mlp) + sh_mlp)
        ff = plin(plin(xm, w_f1, b_f1), w_f2, b_f2)
        ff_t = g_mlp * logmap0(ff)
        return mobius_add(residual, expmap0(ff_t))

    def _L1_cond_ref(context_c, time_cond, gate_w, gate_b, time_w, time_b, ew1, eb1, ew2, eb2, sw1, sb1, sw2, sb2):
        import jax, jax.numpy as jnp
        import numpy as np
        NUM_EXPERTS = 4
        TOP_K = 2
        B, L, D = context_c.shape
        E, K = (NUM_EXPERTS, TOP_K)
        L_head = L_wrist = L // 3
        head = context_c[:, :L_head]
        wrist = context_c[:, L_head:L_head + L_wrist]
        proprio = context_c[:, L_head + L_wrist:]
        full_agg = context_c.mean(axis=1)
        hp_agg = jnp.concatenate([head, proprio], axis=1).mean(axis=1)
        wp_agg = jnp.concatenate([wrist, proprio], axis=1).mean(axis=1)
        gate_in = jnp.concatenate([full_agg, hp_agg, wp_agg], axis=-1)
        gate_logits = gate_in @ gate_w + gate_b
        mod = jax.nn.silu(time_cond) @ time_w + time_b
        scale, shift = jnp.split(mod, 2, axis=-1)
        gate_logits = gate_logits * (1.0 + scale) + shift
        gate_scores = jax.nn.softmax(gate_logits, axis=-1)
        topk_w, topk_i = jax.lax.top_k(gate_scores, K)
        topk_w = topk_w / (topk_w.sum(axis=-1, keepdims=True) + 1e-08)
        onehot = (topk_i[..., None] == jnp.arange(E)[None, None, :]).astype(context_c.dtype)
        w_be = jnp.sum(topk_w[..., None] * onehot, axis=1)
        mask = np.ones((E, L), dtype=np.float32)
        mask[1, L_head:L_head + L_wrist] = 0.0
        mask[2, :L_head] = 0.0
        mask = jnp.asarray(mask)
        out = jnp.zeros_like(context_c)
        for e in range(E):
            h = jax.nn.gelu(context_c @ ew1[e] + eb1[e], approximate=True)
            y = h @ ew2[e] + eb2[e]
            out = out + w_be[:, e][:, None, None] * mask[e][None, :, None] * y
        shared = jax.nn.gelu(context_c @ sw1 + sb1, approximate=True) @ sw2 + sb2
        return out + shared
    x = x + _L0_cond_ref(x, cond_1024[:, None, :], L0_cond_w_q, L0_cond_b_q, L0_cond_w_k, L0_cond_b_k, L0_cond_w_v, L0_cond_b_v, L0_cond_w_o, L0_cond_b_o, L0_cond_w_f1, L0_cond_b_f1, L0_cond_w_f2, L0_cond_b_f2, L0_cond_w_ada, L0_cond_b_ada)
    x = x + _L1_cond_ref(x, cond_1024, L1_cond_gate_w, L1_cond_gate_b, L1_cond_time_w, L1_cond_time_b, L1_cond_ew1, L1_cond_eb1, L1_cond_ew2, L1_cond_eb2, L1_cond_sw1, L1_cond_sb1, L1_cond_sw2, L1_cond_sb2)
    return x

_drawn_inputs = setup_inputs


def setup_inputs(seed=0):
    import zlib

    import numpy as np

    out = dict(_drawn_inputs(seed))
    spreads = {'L0_cond_b_q': (0.0, 0.8),
     'L0_cond_b_k': (0.0, 0.8),
     'L0_cond_b_v': (0.0, 0.1),
     'L0_cond_b_o': (0.0, 0.1),
     'L0_cond_b_f1': (0.0, 0.1),
     'L0_cond_b_f2': (0.0, 0.1),
     'L0_cond_b_ada': (0.0, 0.1),
     'L1_cond_gate_b': (0.0, 0.1),
     'L1_cond_time_b': (0.0, 0.1),
     'L1_cond_eb1': (0.0, 0.1),
     'L1_cond_eb2': (0.0, 0.1),
     'L1_cond_sb1': (0.0, 0.1),
     'L1_cond_sb2': (0.0, 0.1)}
    factors = {'L0_cond_w_q': 8.0,
     'L0_cond_w_k': 8.0,
     'L0_cond_w_v': 3.154,
     'L1_cond_gate_w': 5.657,
     'L1_cond_ew1': 4.019}
    for name, (base, spread) in spreads.items():
        noise = np.random.default_rng([zlib.crc32(name.encode()), seed]).standard_normal(out[name].shape)
        drawn = base * np.exp(spread * noise) if base else spread * noise
        out[name] = jnp.asarray(drawn.astype(out[name].dtype))
    for name, factor in factors.items():
        out[name] = (out[name] * factor).astype(out[name].dtype)
    return out
```

```python
import math

import concourse.bass as bass
from concourse import mybir
from contextlib import ExitStack

B, S, D = 32, 32, 128
H, HD, FF = 16, 8, 512
E = 4
P = 128
TILES = B * S // P
BT = P // S
NG = 2
TG = TILES // NG
GT = TG * P
GB = B // NG
HG = 4
NHG = H // HG
FC = FF // P
VW = HG * HD + HG
SEG = 10
TAIL = S - 2 * SEG

C_ID, C_HM, C_VM, C_WM, C_TRI, C_SEL, C_MT = 0, 128, 132, 136, 140, 156, 668
C_END = 1181
K_COND, K_BADA, K_BF1, K_EB1, K_GW, K_TW = 0, 32, 36, 40, 60, 72
K_END = 80
R_QKV, R_BO, R_BF2, R_BG, R_GB, R_TB = 0, 384, 512, 640, 896, 900
R_END = 908


def _beta(a, b):
    return math.exp(math.lgamma(a) + math.lgamma(b) - math.lgamma(a + b))


RATIO = _beta(HD / 2, 0.5) / _beta(D / 2, 0.5)
MAX_ARG = 0.9999899864196777
A = math.atanh(MAX_ARG)
TINY = 1e-30
EPS = 1e-7


def cond_resid_kernel(nc, x, consts, cols, rows, w_ada, w_qkv, w_o, w_f1, w_f2, w_up, w_down, b_down, out):
    f32 = mybir.dt.float32
    u32 = mybir.dt.uint32
    ALU = mybir.AluOpType
    ACT = mybir.ActivationFunctionType
    X = mybir.AxisListType.X

    ctx = ExitStack()
    with ctx:
        def sb(name, shape):
            return ctx.enter_context(nc.sbuf_tensor(name, shape, f32))

        def sem(name):
            return ctx.enter_context(nc.semaphore(name))

        cst = sb("cst", [P, C_END])
        col = sb("col", [P, K_END])
        row = sb("row", [P, R_END])
        wada = sb("wada", [P, 6 * D])
        wqkv = sb("wqkv", [P, 3 * D])
        wo = sb("wo", [P, D])
        wf1 = sb("wf1", [P, FF])
        wf2 = sb("wf2", [P, FC, D])
        wup = sb("wup", [P, 2, FF])
        wdn = sb("wdn", [P, 2, FC, D])
        bdn = sb("bdn", [E + 1, D])
        ident = cst[:, C_ID:C_ID + P]
        ones = sb("ones", [P, 1])
        warm = sb("warm", [P, 1])
        adaT = sb("adaT", [P, 4, B])
        adag = sb("adag", [GB, NG, 2 * D])
        gain = sb("gain", [P, TILES, 2 * D])
        silu = sb("silu", [P, B])
        mod = sb("mod", [GB, NG, 2 * E])
        xin = sb("xin", [P, TILES, D])
        x1 = sb("x1", [P, TILES, D])
        x3 = sb("x3", [P, TILES, D])
        xn = sb("xn", [P, TILES, D])
        yT = sb("yT", [P, NG, GT])
        ysq = sb("ysq", [P, NG, GT])
        qkv = sb("qkv", [P, TILES, 3 * D])
        qk = sb("qk", [P, TILES, 2 * D])
        vs = sb("vs", [P, TILES, D])
        vrep = sb("vrep", [P, NG, TG * BT, D])
        qsq = [vrep[:, g].rearrange("p r d -> p (r d)")[:, 0:TG * 3 * D] for g in range(NG)]
        vexp = sb("vexp", [P, NG, TG * BT, NHG, VW])
        qT = sb("qT", [P, NG, GT])
        kexp = sb("kexp", [P, NG, TG * BT, HG, S])
        prob = sb("prob", [P, NG, NHG, GT])
        probT = sb("probT", [P, NG, NHG, GT])
        o = sb("o", [P, TILES, NHG, VW])
        osq = xn
        ain = ysq[:].rearrange("p g (t d) -> p (g t) d", d=D)
        ainT = sb("ainT", [P, NG, GT])
        ap, gt, tmp = (qkv[:, :, i * D:(i + 1) * D] for i in range(3))
        junk = sb("junk", [P, NG, 3, D])
        rsb = sb("rsb", [P, NG, GT])
        hf = prob
        hsq = kexp[:].rearrange("p g r h s -> p g (r h s)").rearrange("p g (c t) -> p g c t", c=FC)
        x3T = sb("x3T", [P, NG, GT])
        hT = probT
        bst = sb("bst", [P, 2, TILES, 6])
        mv = sb("mv", [P, 2, TILES, 2])
        st = sb("st", [P, 2, 24, TILES])
        heads = sb("heads", [P, NG, 4, 204])
        oh = sb("oh", [P, NG, 6, TG * H])
        onrm = sb("onrm", [P, NG, 4, TG])
        seg = sb("seg", [P, NG, 3, GB])
        agg = sb("agg", [P, NG, 3, GB])
        gl = sb("gl", [GB, NG, 8, E])
        gp = sb("gp", [GB, NG, 3, E * E])
        gs = sb("gs", [GB, NG, 8])
        wtok = sb("wtok", [P, NG, E, TG])
        wT = sb("wT", [E + 1, NG, GT])

        bank = [ctx.enter_context(nc.psum_tensor(f"bank{i}", [P, 512], f32)) for i in range(8)]

        names = """x_in consts_in rows_in wada_in wqkv_in wo_in wf1_in wf2_in bdn_in
        ones_ready vones_ready ada_mm mod_mm adat_ready adag_ready gain_mm gain_ready silu_e silu_ready
        mod_ready meansq norm0 m_ready ln_ready lnvar rstd xn_ready xnT_mm yT_ready ysq_ready yss_mm yn_ready
        qkv_mm qkv_ready qsq_ready hss_ready hnorm c_ready v_ready vexp_ready qk_ready qT_mm kT_mm
        qT_ready kexp_ready sc_mm p_ready pT_mm pTd_ready pTa_ready o_mm o_ready osq_ready oss_ready on_ready
        oc_ready onn_ready ain_ready ainT_mm ainT_ready ap_mm ap_ready asq_ready gt_ready an_ready n_ready
        th_ready rs_ready rsb_mm rsb_ready up_mm hf_ready hsq_ready hss2_mm hn_ready f_mm x3_ready x3T_mm
        x3T_ready agg_ready gate_mm logit_ready gexp_ready w_ready wtok_mm wtok_ready moe_up moe_h moe_y
        moe_acc stored vec_step act_step pool_step""".split()
        s = {n: sem(n) for n in names}
        vrep_in = [sem(f"vrep_in{g}") for g in range(NG)]
        wup_in, wdn_in = ([sem(f"{n}{i}") for i in range(2)] for n in ("wup_in", "wdn_in"))

        nc_v, nc_a, nc_t, nc_p = nc.vector, nc.scalar, nc.tensor, nc.gpsimd

        def T(g):
            return slice(g * TG, (g + 1) * TG)

        def bk(g, i):
            return bank[4 * g + i]

        UPB = [3, 0, 2, 1]

        block = ctx.enter_context(nc.Block())

        @block.sync
        def _(sp):
            for g in range(NG):
                sp.dma_start(xin[:, T(g), :], x[T(g)].rearrange("t p d -> p t d")).then_inc(s["x_in"], 16)
            sp.dma_start(col[:], cols).then_inc(s["consts_in"], 16)
            sp.dma_start(cst[:], consts).then_inc(s["consts_in"], 16)
            sp.dma_start(wada[:], w_ada).then_inc(s["wada_in"], 16)
            sp.dma_start(row[:], rows.broadcast_to([P, R_END])).then_inc(s["rows_in"], 16)
            sp.dma_start(wqkv[:], w_qkv).then_inc(s["wqkv_in"], 16)
            sp.dma_start(wo[:], w_o).then_inc(s["wo_in"], 16)
            sp.dma_start(wf1[:], w_f1).then_inc(s["wf1_in"], 16)
            sp.dma_start(wf2[:], w_f2.rearrange("p (c d) -> p c d", c=FC)).then_inc(s["wf2_in"], 16)
            sp.dma_start(bdn[:], b_down).then_inc(s["bdn_in"], 16)
            for e in range(2):
                sp.dma_start(wup[:, e, :], w_up[e]).then_inc(wup_in[e % 2], 16)
                sp.dma_start(wdn[:, e, :, :], w_down[e].rearrange("p (c d) -> p c d", c=FC)).then_inc(wdn_in[e % 2], 16)
            for g in range(NG):
                sp.wait_ge(s["v_ready"], g + 1)
                for b in range(BT):
                    for h in range(HG):
                        sp.dma_start(vrep[h * S:(h + 1) * S, g, b::BT, :], vs[b * S:(b + 1) * S, T(g), :]) \
                            .then_inc(vrep_in[g], 16)
            for e in range(2, E + 1):
                sp.wait_ge(s["moe_up"], FC * NG * (e - 1))
                sp.dma_start(wup[:, e % 2, :], w_up[e]).then_inc(wup_in[e % 2], 16)
                sp.wait_ge(s["moe_y"], NG * (e - 1))
                sp.dma_start(wdn[:, e % 2, :, :], w_down[e].rearrange("p (c d) -> p c d", c=FC)).then_inc(wdn_in[e % 2], 16)
            for g in range(NG):
                sp.wait_ge(s["moe_acc"], NG * E + g + 1)
                sp.dma_start(out[T(g)].rearrange("t p d -> p t d"), x3[:, T(g), :]).then_inc(s["stored"], 16)
            sp.wait_ge(s["stored"], 16 * NG)

        @block.vector
        def _(v):
            steps = [0]

            def step(ins):
                ins.then_inc(s["vec_step"], 1)
                steps[0] += 1

            def settle():
                v.wait_ge(s["vec_step"], steps[0])

            def link(ins):
                step(ins)
                settle()

            def conditioning():
                nc_v.memset(ones[:], 1.0).then_inc(s["ones_ready"], 1)
                step(nc_v.memset(wT[:], 1.0))
                v.wait_ge(s["silu_e"], 1)
                link(nc_v.tensor_scalar(silu[:], silu[:], 1.0, None, ALU.add))
                link(nc_v.reciprocal(silu[:], silu[:]))
                nc_v.tensor_tensor(silu[:], silu[:], col[:, K_COND:K_COND + B], ALU.mult).then_inc(s["silu_ready"], 1)
                v.wait_ge(s["ada_mm"], 1)
                for j in range(4):
                    step(nc_v.tensor_scalar(adaT[:, j, :], bank[0][:, j * B:(j + 1) * B],
                                            col[:, K_BADA + j:K_BADA + j + 1], float(j % 2), ALU.add, ALU.add))
                settle()
                v.wait_ge(s["rows_in"], 16)
                for g in range(NG):
                    v.wait_ge(s["ada_mm"], 2 + g)
                    nc_v.tensor_tensor(adag[:, g, :], bank[4 + g][0:GB, 0:2 * D], row[0:GB, R_BG:R_BG + 2 * D],
                                       ALU.add).then_inc(s["adag_ready"], 1)
                v.wait_ge(s["mod_mm"], 1)
                for g in range(NG):
                    step(nc_v.tensor_tensor(mod[:, g, :], bank[1][0:GB, g * 2 * E:(g + 1) * 2 * E],
                                            row[0:GB, R_TB:R_TB + 2 * E], ALU.add))
                settle()
                for g in range(NG):
                    last = nc_v.tensor_scalar(mod[:, g, 0:E], mod[:, g, 0:E], 1.0, None, ALU.add)
                last.then_inc(s["mod_ready"], 1)

            def normalise(g, j, src):
                t4 = T(g)
                k = j * NG + g
                q = lambda i: st[:, j, i, t4]
                for t in range(g * TG, (g + 1) * TG):
                    step(nc_v.bn_stats(bst[:, j, t, :], src[:, t, :]))
                settle()
                for t in range(g * TG, (g + 1) * TG):
                    step(nc_v.bn_aggr(mv[:, j, t, :], bst[:, j, t, :]))
                settle()
                mu, var = mv[:, j, t4, 0], mv[:, j, t4, 1]
                link(nc_v.tensor_tensor(q(0), mu, mu, ALU.mult))
                nc_v.tensor_tensor(q(1), q(0), var, ALU.add).then_inc(s["meansq"], 1)
                v.wait_ge(s["norm0"], k + 1)
                nc_v.tensor_scalar(q(3), q(2), MAX_ARG, None, ALU.min).then_inc(s["m_ready"], 1)
                link(nc_v.reciprocal(q(4), q(2)))
                v.wait_ge(s["m_ready"], k + 1)
                link(nc_v.tensor_tensor(q(5), q(3), q(3), ALU.mult))
                link(nc_v.tensor_scalar(q(6), q(5), 1.0 / 13, None, ALU.mult))
                for i in (11, 9, 7, 5, 3):
                    link(nc_v.scalar_tensor_tensor(q(6), q(6), 1.0 / i, q(5), ALU.add, ALU.mult))
                step(nc_v.tensor_scalar(q(6), q(6), 1.0, None, ALU.add))
                step(nc_v.tensor_scalar(q(7), q(3), 0.25, None, ALU.is_lt))
                settle()
                v.wait_ge(s["ln_ready"], k + 1)
                link(nc_v.tensor_tensor(q(10), q(8), q(9), ALU.subtract))
                link(nc_v.scalar_tensor_tensor(q(11), q(10), 0.5, q(4), ALU.mult, ALU.mult))
                link(nc_v.copy_predicated(q(11), q(7).bitcast(u32), q(6)))
                link(nc_v.reciprocal(q(12), q(11)))
                link(nc_v.tensor_tensor(q(12), q(12), q(12), ALU.mult))
                nc_v.scalar_tensor_tensor(q(13), q(12), 1e-6, var, ALU.mult, ALU.add).then_inc(s["lnvar"], 1)
                v.wait_ge(s["rstd"], k + 1)
                link(nc_v.reciprocal(q(15), q(14)))
                for t in range(g * TG, (g + 1) * TG):
                    nc_v.tensor_scalar(xn[:, t, :], src[:, t, :], mv[:, j, t, 0:1], st[:, j, 15, t:t + 1],
                                       ALU.subtract, ALU.mult).then_inc(s["xn_ready"], 1)

            def modulate(g, j):
                v.wait_ge(s["xnT_mm"], j * NG + g + 1)
                b0 = g * GB
                y3 = yT[:, g, :].rearrange("p (b s) -> p b s", s=S)
                sc = adaT[:, 2 * j + 1, b0:b0 + GB].unsqueeze(2).broadcast_to([P, GB, S])
                sh = adaT[:, 2 * j, b0:b0 + GB].unsqueeze(2).broadcast_to([P, GB, S])
                link(nc_v.tensor_tensor(y3, bk(g, 0)[:, :].rearrange("p (b s) -> p b s", s=S), sc, ALU.mult))
                nc_v.tensor_tensor(y3, y3, sh, ALU.add).then_inc(s["yT_ready"], 1)

            def clamp_y(g, j):
                q = lambda i: st[:, j, i, T(g)]
                v.wait_ge(s["yn_ready"], j * NG + g + 1)
                if j == 1:
                    nc_v.tensor_scalar(q(18), q(16), 1.0 / A, 1.0, ALU.mult, ALU.max).then_inc(s["rs_ready"], 1)
                link(nc_v.reciprocal(q(17), q(16)))
                link(nc_v.tensor_scalar(q(17), q(17), A, 1.0, ALU.mult, ALU.min))

            def project(g):
                for t in range(g * TG, (g + 1) * TG):
                    v.wait_ge(s["qkv_mm"], t + 1)
                    nc_v.scalar_tensor_tensor(qkv[:, t, :], bk(g, (t + 2) % 4)[:, 0:3 * D], st[:, 0, 17, t:t + 1],
                                              row[:, R_QKV:R_QKV + 3 * D], ALU.mult, ALU.add).then_inc(s["qkv_ready"], 1)
                hh = lambda i: heads[:, g, i, :]
                n = TG * 3 * H
                v.wait_ge(s["qsq_ready"], (g + 1) * TG)
                link(nc_v.tensor_reduce(hh(0)[:, 0:n], qsq[g].rearrange("p (h d) -> p h d", d=HD),
                                        X, ALU.add))
                nc_v.tensor_reduce(hh(0)[:, n:n + 3 * TG], hh(0)[:, 0:n].rearrange("p (w h) -> p w h", h=H),
                                   X, ALU.add).then_inc(s["hss_ready"], 1)
                v.wait_ge(s["hnorm"], g + 1)
                link(nc_v.reciprocal(hh(2), hh(1)))
                link(nc_v.tensor_scalar(hh(3)[:, n:n + 3 * TG], hh(2)[:, n:n + 3 * TG], A * RATIO, RATIO,
                                        ALU.mult, ALU.min))
                w3 = lambda z: z[:, 0:n].rearrange("p (w h) -> p w h", h=H)
                nc_v.scalar_tensor_tensor(w3(hh(3)), w3(hh(2)), A,
                                          hh(3)[:, n:n + 3 * TG].unsqueeze(2).broadcast_to([P, 3 * TG, H]),
                                          ALU.mult, ALU.min).then_inc(s["c_ready"], 1)
                v.wait_ge(s["c_ready"], g + 1)
                c4 = hh(3)[:, 0:n].rearrange("p (t h) -> p t h", t=TG)[:, :, 0:2 * H]
                nc_v.tensor_tensor(qk[:, T(g), :].rearrange("p t (h d) -> p t h d", d=HD),
                                   qkv[:, T(g), 0:2 * D].rearrange("p t (h d) -> p t h d", d=HD),
                                   c4.unsqueeze(3).broadcast_to([P, TG, 2 * H, HD]), ALU.mult).then_inc(s["qk_ready"], 1)

            def expand_k(g):
                v.wait_ge(s["kT_mm"], g + 1)
                n = TG * BT
                kk = bk(g, 1)[:, :].rearrange("p (r s) -> p r s", s=S).unsqueeze(2).broadcast_to([P, n, HG, S])
                hm = cst[:, C_HM:C_HM + HG].unsqueeze(1).broadcast_to([P, n, HG]).unsqueeze(3).broadcast_to([P, n, HG, S])
                nc_v.tensor_tensor(kexp[:, g], kk, hm, ALU.mult).then_inc(s["kexp_ready"], 1)

            def copy_probs(g):
                for i in (0, 2):
                    v.wait_ge(s["pT_mm"], g * NHG + i + 1)
                    nc_v.tensor_copy(probT[:, g, i, :], bk(g, i)[:, :]).then_inc(s["pTd_ready"], 1)

            def heads_out(g):
                t4 = T(g)
                oo = lambda i: oh[:, g, i, :]
                ov = o[:, t4].rearrange("p t n w -> p (t n) w")
                n = TG * NHG
                v.wait_ge(s["o_ready"], 2 * (g + 1))
                step(nc_v.reciprocal(oo(0).rearrange("p (n h) -> p n h", h=HG), ov[:, :, HG * HD:VW]))
                v.wait_ge(s["osq_ready"], g + 1)
                nc_v.tensor_reduce(oo(1), osq[:, t4, :].rearrange("p t (h d) -> p (t h) d", d=HD), X,
                                   ALU.add).then_inc(s["oss_ready"], 1)
                v.wait_ge(s["on_ready"], g + 1)
                link(nc_v.reciprocal(oo(3), oo(2)))
                link(nc_v.scalar_tensor_tensor(oo(3), oo(3), A, oo(0), ALU.mult, ALU.min))
                link(nc_v.tensor_scalar(oo(3), oo(3), 1.0 / RATIO, None, ALU.mult))
                c = oo(3).rearrange("p (n h) -> p n h", h=HG).unsqueeze(3).broadcast_to([P, n, HG, HD])
                nc_v.tensor_tensor(ain[:, t4, :].rearrange("p t (n h d) -> p (t n) h d", h=HG, d=HD),
                                   ov[:, :, 0:HG * HD].rearrange("p n (h d) -> p n h d", d=HD), c,
                                   ALU.mult).then_inc(s["ain_ready"], 1)
                link(nc_v.tensor_tensor(oo(4), oo(3), oo(3), ALU.mult))
                link(nc_v.tensor_tensor(oo(4), oo(4), oo(1), ALU.mult))
                nc_v.tensor_reduce(onrm[:, g, 0, :], oo(4).rearrange("p (t h) -> p t h", t=TG), X,
                                   ALU.add).then_inc(s["oc_ready"], 1)
                v.wait_ge(s["onn_ready"], g + 1)
                link(nc_v.reciprocal(onrm[:, g, 2, :], onrm[:, g, 1, :]))
                link(nc_v.tensor_scalar(onrm[:, g, 2, :], onrm[:, g, 2, :], A, 1.0, ALU.mult, ALU.min))

            def residual(g, j, ps, scale, bias, res, dst):
                t4 = T(g)
                k = j * NG + g
                q = lambda i: st[:, j, i, t4]
                for t in range(TG):
                    last = nc_v.scalar_tensor_tensor(ap[:, g * TG + t, :], ps[:, t * D:(t + 1) * D], scale[:, t:t + 1],
                                                     row[:, bias:bias + D], ALU.mult, ALU.add)
                last.then_inc(s["ap_ready"], 1)
                v.wait_ge(s["ap_ready"], k + 1)
                nc_v.tensor_tensor(gt[:, t4, :], ap[:, t4, :], gain[:, t4, j * D:(j + 1) * D],
                                   ALU.mult).then_inc(s["gt_ready"], 1)
                v.wait_ge(s["gt_ready"], k + 1)
                for t in range(TG):
                    step(nc_v.tensor_tensor_reduce(out=tmp[:, g * TG + t, :], in0=res[:, g * TG + t, :],
                                                   in1=gt[:, g * TG + t, :], scale=1.0, scalar=0.0, op0=ALU.mult,
                                                   op1=ALU.add, accum_out=st[:, j, 19, g * TG + t:g * TG + t + 1]))
                step(nc_v.tensor_scalar(q(0), q(1), float(D), None, ALU.mult))
                v.wait_ge(s["an_ready"], k + 1)
                step(nc_v.reciprocal(q(22), q(20)))
                step(nc_v.reciprocal(q(23), q(21)))
                settle()
                link(nc_v.tensor_scalar(q(22), q(22), A, 1.0, ALU.mult, ALU.min))
                nc_v.tensor_tensor(q(20), q(22), q(21), ALU.mult).then_inc(s["n_ready"], 1)
                step(nc_v.tensor_scalar(q(3), q(0), -1.0, 1.0, ALU.mult, ALU.add))
                v.wait_ge(s["th_ready"], k + 1)
                step(nc_v.tensor_tensor(q(4), q(22), q(23), ALU.mult))
                step(nc_v.tensor_tensor(q(5), q(22), q(22), ALU.mult))
                settle()
                step(nc_v.tensor_tensor(q(6), q(4), q(19), ALU.mult))
                step(nc_v.tensor_tensor(q(3), q(3), q(4), ALU.mult))
                step(nc_v.tensor_tensor(q(8), q(0), q(5), ALU.mult))
                settle()
                link(nc_v.tensor_scalar(q(6), q(6), 2.0, 1.0, ALU.mult, ALU.add))
                step(nc_v.tensor_tensor(q(8), q(6), q(8), ALU.add))
                step(nc_v.tensor_tensor(q(5), q(6), q(5), ALU.add))
                settle()
                link(nc_v.tensor_scalar(q(8), q(8), EPS, None, ALU.max))
                link(nc_v.reciprocal(q(8), q(8)))
                step(nc_v.tensor_tensor(q(3), q(3), q(8), ALU.mult))
                step(nc_v.tensor_tensor(q(5), q(5), q(8), ALU.mult))
                settle()
                for t in range(g * TG, (g + 1) * TG):
                    sc = st[:, j, 3, t:t + 1]
                    if j == 0:
                        step(nc_v.tensor_scalar(tmp[:, t, :], gt[:, t, :], sc, None, ALU.mult))
                    else:
                        step(nc_v.scalar_tensor_tensor(tmp[:, t, :], gt[:, t, :], sc, xin[:, t, :], ALU.mult, ALU.add))
                settle()
                for t in range(g * TG, (g + 1) * TG):
                    ins = nc_v.scalar_tensor_tensor(dst[:, t, :], res[:, t, :], st[:, j, 5, t:t + 1], tmp[:, t, :],
                                                    ALU.mult, ALU.add)
                    ins.then_inc(s["x3_ready"], 1) if j else step(ins)
                if j:
                    v.wait_ge(s["x3_ready"], (g + 1) * TG)
                else:
                    settle()

            def hidden(g):
                v.wait_ge(s["rsb_ready"], g + 1)
                for i, c in enumerate(UPB):
                    v.wait_ge(s["up_mm"], g * FC + i + 1)
                    nc_v.scalar_tensor_tensor(hf[:, g, i, :], rsb[:, g, :], col[:, K_BF1 + i:K_BF1 + i + 1], bk(g, c)[:, :],
                                              ALU.mult, ALU.add).then_inc(s["hf_ready"], 1)

            def hidden_clamp(g):
                t4 = T(g)
                v.wait_ge(s["hn_ready"], g + 1)
                link(nc_v.reciprocal(onrm[:, g, 2, :], onrm[:, g, 3, :]))
                link(nc_v.scalar_tensor_tensor(onrm[:, g, 2, :], onrm[:, g, 2, :], A, st[:, 1, 17, t4], ALU.mult, ALU.min))

            def gate_inputs(g):
                v.wait_ge(s["x3T_ready"], g + 1)
                xt = x3T[:, g, :].rearrange("p (b s) -> p b s", s=S)
                for i, (a, b) in enumerate(((0, SEG), (SEG, 2 * SEG), (2 * SEG, S))):
                    step(nc_v.tensor_reduce(seg[:, g, i, :], xt[:, :, a:b], X, ALU.add))
                settle()
                step(nc_v.tensor_tensor(agg[:, g, 1, :], seg[:, g, 0, :], seg[:, g, 2, :], ALU.add))
                step(nc_v.tensor_tensor(agg[:, g, 2, :], seg[:, g, 1, :], seg[:, g, 2, :], ALU.add))
                settle()
                link(nc_v.tensor_tensor(agg[:, g, 0, :], agg[:, g, 1, :], seg[:, g, 1, :], ALU.add))
                step(nc_v.tensor_scalar(agg[:, g, 0, :], agg[:, g, 0, :], 1.0 / S, None, ALU.mult))
                nc_v.tensor_scalar(agg[:, g, 1:3, :], agg[:, g, 1:3, :], 1.0 / (SEG + TAIL), None,
                                   ALU.mult).then_inc(s["agg_ready"], 1)

            def gate(g):
                L = lambda i: gl[:, g, i, :]
                v.wait_ge(s["gate_mm"], g + 1)
                link(nc_v.tensor_tensor(L(0), bk(g, 3)[0:GB, 0:E], row[0:GB, R_GB:R_GB + E], ALU.add))
                link(nc_v.tensor_tensor(L(0), L(0), mod[:, g, 0:E], ALU.mult))
                link(nc_v.tensor_tensor(L(0), L(0), mod[:, g, E:2 * E], ALU.add))
                nc_v.tensor_reduce(gs[:, g, 0:1], L(0), X, ALU.max, negate=True).then_inc(s["logit_ready"], 1)
                v.wait_ge(s["gexp_ready"], g + 1)
                link(nc_v.tensor_reduce(gs[:, g, 1:2], L(1), X, ALU.add))
                link(nc_v.reciprocal(gs[:, g, 2:3], gs[:, g, 1:2]))
                link(nc_v.tensor_scalar(L(2), L(1), gs[:, g, 2:3], None, ALU.mult))
                pj = L(2).unsqueeze(1).broadcast_to([GB, E, E])
                pi = L(2).unsqueeze(2).broadcast_to([GB, E, E])
                m = lambda i: gp[:, g, i, :].rearrange("p (i j) -> p i j", i=E)
                step(nc_v.tensor_tensor(m(0), pj, pi, ALU.is_gt))
                step(nc_v.tensor_tensor(m(1), pj, pi, ALU.is_equal))
                settle()
                link(nc_v.tensor_tensor(m(1), m(1), cst[0:GB, C_TRI:C_TRI + E * E].rearrange("p (i j) -> p i j", i=E),
                                        ALU.mult))
                link(nc_v.tensor_tensor(m(0), m(0), m(1), ALU.add))
                link(nc_v.tensor_reduce(L(3), m(0), X, ALU.add))
                link(nc_v.scalar_tensor_tensor(L(4), L(3), 1.5, L(2), ALU.is_lt, ALU.mult))
                link(nc_v.tensor_reduce(gs[:, g, 3:4], L(4), X, ALU.add))
                link(nc_v.tensor_scalar(gs[:, g, 3:4], gs[:, g, 3:4], 1e-8, None, ALU.add))
                link(nc_v.reciprocal(gs[:, g, 4:5], gs[:, g, 3:4]))
                nc_v.tensor_scalar(L(5), L(4), gs[:, g, 4:5], None, ALU.mult).then_inc(s["w_ready"], 1)
                v.wait_ge(s["wtok_mm"], g + 1)
                nc_v.tensor_tensor(wtok[:, g].rearrange("p e t -> p t e"),
                                   bk(g, 3)[:, 8:8 + E * TG].rearrange("p (t e) -> p t e", e=E),
                                   cst[:, C_WM:C_WM + E].unsqueeze(1).broadcast_to([P, TG, E]), ALU.mult)
                nc_v.tensor_tensor(wT[0:E, g, :], bk(g, 1)[0:E, :], cst[0:E, C_MT:C_MT + GT],
                                   ALU.mult).then_inc(s["wtok_ready"], 1)

            v.wait_ge(s["x_in"], 32)
            v.wait_ge(s["consts_in"], 32)
            normalise(0, 0, xin)
            conditioning()
            normalise(1, 0, xin)
            for g in range(NG):
                modulate(g, 0)
            for g in range(NG):
                clamp_y(g, 0)
                project(g)
            for g in range(NG):
                expand_k(g)
            for g in range(NG):
                copy_probs(g)
            for g in range(NG):
                heads_out(g)
            for g in range(NG):
                v.wait_ge(s["ap_mm"], g + 1)
                residual(g, 0, bk(g, 3), onrm[:, g, 2, :], R_BO, xin, x1)
                normalise(g, 1, x1)
            for g in range(NG):
                modulate(g, 1)
            for g in range(NG):
                clamp_y(g, 1)
                hidden(g)
            for g in range(NG):
                hidden_clamp(g)
                v.wait_ge(s["f_mm"], g + 1)
                residual(g, 1, bk(g, 0), onrm[:, g, 2, :], R_BF2, x1, x3)
            for g in range(NG):
                gate_inputs(g)
            for g in range(NG):
                gate(g)
            v.wait_ge(s["wtok_ready"], NG)

            for e in range(E):
                for g in range(NG):
                    v.wait_ge(s["moe_y"], NG * e + g + 1)
                    if e:
                        v.wait_ge(s["moe_acc"], NG * (e - 1) + g + 1)
                    for t in range(TG):
                        last = nc_v.scalar_tensor_tensor(x3[:, g * TG + t, :], bk(g, 3)[:, t * D:(t + 1) * D],
                                                         wtok[:, g, e, t:t + 1], x3[:, g * TG + t, :], ALU.mult, ALU.add)
                    last.then_inc(s["moe_acc"], 1)
            for g in range(NG):
                v.wait_ge(s["moe_y"], NG * E + g + 1)
                v.wait_ge(s["moe_acc"], NG * (E - 1) + g + 1)
                nc_v.tensor_tensor(x3[:, T(g), :].rearrange("p t d -> p (t d)"), bk(g, 3)[:, :],
                                   x3[:, T(g), :].rearrange("p t d -> p (t d)"), ALU.add).then_inc(s["moe_acc"], 1)

        @block.scalar
        def _(a):
            act = nc_a.activation

            def norm_log(g, j):
                q = lambda i: st[:, j, i, T(g)]
                k = j * NG + g
                a.wait_ge(s["meansq"], k + 1)
                act(q(2), q(1), ACT.Sqrt, scale=float(D), bias=tiny).then_inc(s["norm0"], 1)
                a.wait_ge(s["m_ready"], k + 1)
                act(q(8), q(3), ACT.Ln, scale=1.0, bias=1.0)
                act(q(9), q(3), ACT.Ln, scale=-1.0, bias=1.0).then_inc(s["ln_ready"], 1)
                a.wait_ge(s["lnvar"], k + 1)
                act(q(14), q(13), ACT.Sqrt).then_inc(s["rstd"], 1)

            def square_y(g, j):
                a.wait_ge(s["yT_ready"], j * NG + g + 1)
                act(ysq[:, g, :], yT[:, g, :], ACT.Square).then_inc(s["ysq_ready"], 1)

            def norm_y(g, j):
                a.wait_ge(s["yss_mm"], j * NG + g + 1)
                act(st[:, j, 16, T(g)], bk(g, 1)[:, 0:TG], ACT.Sqrt, bias=tiny).then_inc(s["yn_ready"], 1)

            def gains(g):
                for i in range(2):
                    a.wait_ge(s["gain_mm"], 2 * g + i + 1)
                    t = g * TG + 2 * i
                    act(gain[:, t:t + 2, :].rearrange("p t d -> p (t d)"), bk(g, 2 + i)[:, :],
                        ACT.Copy).then_inc(s["gain_ready"], 1)

            def residual_norms(g, j):
                k = j * NG + g
                a.wait_ge(s["ap_ready"], k + 1)
                for t in range(TG):
                    act(junk[:, g, 0, :], ap[:, g * TG + t, :], ACT.Square,
                        accum_out=st[:, j, 20, g * TG + t:g * TG + t + 1]).then_inc(s["act_step"], 1)
                    a.wait_ge(s["act_step"], (k * 2) * TG + t + 1)
                a.wait_ge(s["gt_ready"], k + 1)
                for t in range(TG):
                    act(junk[:, g, 1, :], gt[:, g * TG + t, :], ACT.Square,
                        accum_out=st[:, j, 21, g * TG + t:g * TG + t + 1]).then_inc(s["act_step"], 1)
                    a.wait_ge(s["act_step"], (k * 2 + 1) * TG + t + 1)
                both = st[:, j, 20:22, T(g)]
                act(both, both, ACT.Sqrt, bias=tiny).then_inc(s["an_ready"], 1)
                a.wait_ge(s["n_ready"], k + 1)
                act(st[:, j, 22, T(g)], st[:, j, 20, T(g)], ACT.Tanh).then_inc(s["th_ready"], 1)

            tiny = cst[:, C_END - 1:C_END]
            a.wait_ge(s["consts_in"], 32)
            norm_log(0, 0)
            act(silu[:], col[:, K_COND:K_COND + B], ACT.Exp, scale=-1.0).then_inc(s["silu_e"], 1)
            norm_log(1, 0)
            for g in range(NG):
                gains(g)
            for g in range(NG):
                square_y(g, 0)
            for g in range(NG):
                norm_y(g, 0)
            for g in range(NG):
                for t in range(g * TG, (g + 1) * TG):
                    a.wait_ge(s["qkv_ready"], t + 1)
                    act(qsq[g][:, (t % TG) * 3 * D:(t % TG + 1) * 3 * D], qkv[:, t, :], ACT.Square).then_inc(s["qsq_ready"], 1)
                a.wait_ge(s["hss_ready"], g + 1)
                act(heads[:, g, 1, :], heads[:, g, 0, :], ACT.Sqrt, bias=tiny).then_inc(s["hnorm"], 1)
            for g in range(NG):
                a.wait_ge(s["qT_mm"], g + 1)
                act(qT[:, g, :], bk(g, 0)[:, :], ACT.Copy).then_inc(s["qT_ready"], 1)
            for g in range(NG):
                a.wait_ge(s["sc_mm"], g + 1)
                for i in range(NHG):
                    act(prob[:, g, i, :], bk(g, i)[:, :], ACT.Exp, scale=HD ** -0.5).then_inc(s["p_ready"], 1)
                for i in (1, 3):
                    a.wait_ge(s["pT_mm"], g * NHG + i + 1)
                    act(probT[:, g, i, :], bk(g, i)[:, :], ACT.Copy).then_inc(s["pTa_ready"], 1)
            for g in range(NG):
                a.wait_ge(s["o_mm"], g + 1)
                for i in range(2):
                    t = g * TG + 2 * i
                    act(o[:, t:t + 2].rearrange("p t n w -> p (t n w)"), bk(g, i)[:, 0:2 * NHG * VW],
                        ACT.Copy).then_inc(s["o_ready"], 1)
                a.wait_ge(s["o_ready"], 2 * (g + 1))
                act(osq[:, T(g), :].rearrange("p t (n w) -> p (t n) w", w=HG * HD),
                    o[:, T(g)].rearrange("p t n w -> p (t n) w")[:, :, 0:HG * HD], ACT.Square).then_inc(s["osq_ready"], 1)
                a.wait_ge(s["oss_ready"], g + 1)
                act(oh[:, g, 2, :], oh[:, g, 1, :], ACT.Sqrt, bias=tiny).then_inc(s["on_ready"], 1)
                a.wait_ge(s["oc_ready"], g + 1)
                act(onrm[:, g, 1, :], onrm[:, g, 0, :], ACT.Sqrt, bias=tiny).then_inc(s["onn_ready"], 1)
                a.wait_ge(s["ainT_mm"], g + 1)
                act(ainT[:, g, :], bk(g, 2)[:, :], ACT.Copy).then_inc(s["ainT_ready"], 1)
            for g in range(NG):
                residual_norms(g, 0)
                norm_log(g, 1)
            for g in range(NG):
                square_y(g, 1)
            for g in range(NG):
                norm_y(g, 1)
                a.wait_ge(s["rsb_mm"], g + 1)
                act(rsb[:, g, :], bk(g, 2)[:, :], ACT.Copy).then_inc(s["rsb_ready"], 1)
                for c in range(FC):
                    a.wait_ge(s["hf_ready"], g * FC + c + 1)
                    act(hsq[:, g, c, :], hf[:, g, c, :], ACT.Square).then_inc(s["hsq_ready"], 1)
            for g in range(NG):
                a.wait_ge(s["hss2_mm"], g + 1)
                act(onrm[:, g, 3, :], bk(g, 1)[:, 0:TG], ACT.Sqrt, bias=tiny).then_inc(s["hn_ready"], 1)
                residual_norms(g, 1)
            for g in range(NG):
                a.wait_ge(s["x3T_mm"], g + 1)
                act(x3T[:, g, :], bk(g, 2)[:, :], ACT.Copy).then_inc(s["x3T_ready"], 1)
            for g in range(NG):
                a.wait_ge(s["logit_ready"], g + 1)
                act(gl[:, g, 1, :], gl[:, g, 0, :], ACT.Exp, bias=gs[:, g, 0:1]).then_inc(s["gexp_ready"], 1)
            for e in range(E + 1):
                for g in range(NG):
                    n = e * NG + g
                    if e:
                        a.wait_ge(s["moe_y"], n - NG + 1)
                    for c in range(FC):
                        a.wait_ge(s["moe_up"], n * FC + c + 1)
                        act(hT[:, g, c, :], bk(g, c % 3)[:, :], ACT.Gelu_apprx_tanh,
                            bias=col[:, K_EB1 + e * FC + c:K_EB1 + e * FC + c + 1]).then_inc(s["moe_h"], 1)

        @block.gpsimd
        def _(p):
            p.wait_ge(s["consts_in"], 32)
            vm = cst[:, C_VM:C_VM + HG]
            n = TG * BT * NHG
            for g in range(NG):
                vd = vexp[:, g].rearrange("p r n w -> p (r n) w")
                nc_p.tensor_copy(vd[:, :, HG * HD:VW], vm.unsqueeze(1).broadcast_to([P, n, HG]))
            for g in range(NG):
                p.wait_ge(s["c_ready"], g + 1)
                c = heads[:, g, 3, 0:TG * 3 * H].rearrange("p (t h) -> p t h", t=TG)[:, :, 2 * H:3 * H]
                nc_p.tensor_tensor(vs[:, T(g), :].rearrange("p t (h d) -> p t h d", d=HD),
                                   qkv[:, T(g), 2 * D:3 * D].rearrange("p t (h d) -> p t h d", d=HD),
                                   c.unsqueeze(3).broadcast_to([P, TG, H, HD]), ALU.mult).then_inc(s["v_ready"], 1)
            for g in range(NG):
                vd = vexp[:, g].rearrange("p r n w -> p (r n) w")
                p.wait_ge(vrep_in[g], 16 * BT * HG)
                nc_p.tensor_tensor(vd[:, :, 0:HG * HD].rearrange("p n (h d) -> p n h d", d=HD),
                                   vrep[:, g].rearrange("p r (n h d) -> p (r n) h d", h=HG, d=HD),
                                   vm.unsqueeze(1).broadcast_to([P, n, HG]).unsqueeze(3).broadcast_to([P, n, HG, HD]),
                                   ALU.mult).then_inc(s["vexp_ready"], 1)

        @block.tensor
        def _(pe):
            mm, tr = nc_t.matmul, nc_t.transpose

            def conditioning():
                cond = col[:, K_COND:K_COND + B]
                pe.wait_ge(s["consts_in"], 32)
                pe.wait_ge(s["wada_in"], 16)
                for j, c in enumerate((0, 1, 3, 4)):
                    last = mm(bank[0][:, j * B:(j + 1) * B], wada[:, c * D:(c + 1) * D], cond, start=True, stop=True)
                last.then_inc(s["ada_mm"], 1)
                for g in range(NG):
                    for i, c in enumerate((2, 5)):
                        last = mm(bank[4 + g][0:GB, i * D:(i + 1) * D], cond[:, g * GB:(g + 1) * GB],
                                  wada[:, c * D:(c + 1) * D], start=True, stop=True)
                    last.then_inc(s["ada_mm"], 1)
                pe.wait_ge(s["silu_ready"], 1)
                for g in range(NG):
                    last = mm(bank[1][0:GB, g * 2 * E:(g + 1) * 2 * E], silu[:, g * GB:(g + 1) * GB],
                              col[:, K_TW:K_TW + 2 * E], start=True, stop=True)
                last.then_inc(s["mod_mm"], 1)
                for g in range(NG):
                    pe.wait_ge(s["adag_ready"], g + 1)
                    for i in range(2):
                        for t in range(2):
                            tt = 2 * i + t
                            last = mm(bk(g, 2 + i)[:, t * 2 * D:(t + 1) * 2 * D],
                                      cst[0:GB, C_SEL + tt * P:C_SEL + (tt + 1) * P], adag[:, g, :], start=True, stop=True)
                        last.then_inc(s["gain_mm"], 1)

            def transpose_group(dst, src, g):
                for t in range(TG):
                    last = tr(dst[:, t * P:(t + 1) * P], src[:, g * TG + t, :], ident)
                return last

            def norm_rows(g, j):
                pe.wait_ge(s["ysq_ready"], j * NG + g + 1)
                for t in range(TG):
                    last = mm(bk(g, 1)[:, t:t + 1], ysq[:, g, t * P:(t + 1) * P], ones[:], start=True, stop=True)
                last.then_inc(s["yss_mm"], 1)

            def xn_transposed(g, j):
                k = j * NG + g
                pe.wait_ge(s["xn_ready"], (k + 1) * TG)
                transpose_group(bk(g, 0), xn, g).then_inc(s["xnT_mm"], 1)

            pe.wait_ge(s["ones_ready"], 1)
            conditioning()
            pe.wait_ge(s["adag_ready"], NG)
            pe.wait_ge(s["mod_ready"], 1)
            for g in range(NG):
                xn_transposed(g, 0)
            for g in range(NG):
                norm_rows(g, 0)
            pe.wait_ge(s["wqkv_in"], 16)
            for g in range(NG):
                pe.wait_ge(s["gain_ready"], 2 * (g + 1))
                pe.wait_ge(s["yn_ready"], g + 1)
                for t in range(TG):
                    mm(bk(g, (t + 2) % 4)[:, 0:3 * D], yT[:, g, t * P:(t + 1) * P], wqkv[:],
                       start=True, stop=True).then_inc(s["qkv_mm"], 1)
            for g in range(NG):
                pe.wait_ge(s["qk_ready"], g + 1)
                for half, name in ((0, "qT_mm"), (1, "kT_mm")):
                    for t in range(TG):
                        last = tr(bk(g, half)[:, t * P:(t + 1) * P], qk[:, g * TG + t, half * D:(half + 1) * D], ident)
                    last.then_inc(s[name], 1)
            for g in range(NG):
                pe.wait_ge(s["qT_ready"], g + 1)
                pe.wait_ge(s["kexp_ready"], g + 1)
                for r in range(TG * BT):
                    t, b = divmod(r, BT)
                    for n in range(NHG):
                        last = mm(bk(g, n)[b * S:(b + 1) * S, t * P:(t + 1) * P],
                                  qT[n * 32:(n + 1) * 32, g, r * S:(r + 1) * S],
                                  kexp[n * 32:(n + 1) * 32, g, r].rearrange("p h s -> p (h s)"), start=True, stop=True)
                last.then_inc(s["sc_mm"], 1)
            for g in range(NG):
                for n in range(NHG):
                    pe.wait_ge(s["p_ready"], g * NHG + n + 1)
                    for t in range(TG):
                        last = tr(bk(g, n)[:, t * P:(t + 1) * P], prob[:, g, n, t * P:(t + 1) * P], ident)
                    last.then_inc(s["pT_mm"], 1)
            for g in range(NG):
                pe.wait_ge(s["pTd_ready"], 2 * (g + 1))
                pe.wait_ge(s["pTa_ready"], 2 * (g + 1))
                pe.wait_ge(s["vexp_ready"], g + 1)
                for t in range(TG):
                    for n in range(NHG):
                        c = ((t % 2) * NHG + n) * VW
                        for b in range(BT):
                            last = mm(bk(g, t // 2)[b * S:(b + 1) * S, c:c + VW],
                                      probT[:, g, n, t * P + b * S:t * P + (b + 1) * S],
                                      vexp[:, g, t * BT + b, n, :], start=True, stop=True)
                last.then_inc(s["o_mm"], 1)
            pe.wait_ge(s["wo_in"], 16)
            for g in range(NG):
                pe.wait_ge(s["ain_ready"], g + 1)
                transpose_group(bk(g, 2), ain, g).then_inc(s["ainT_mm"], 1)
                pe.wait_ge(s["ainT_ready"], g + 1)
                for t in range(TG):
                    last = mm(bk(g, 3)[:, t * D:(t + 1) * D], ainT[:, g, t * P:(t + 1) * P], wo[:], start=True, stop=True)
                last.then_inc(s["ap_mm"], 1)
            for g in range(NG):
                xn_transposed(g, 1)
            pe.wait_ge(s["wf1_in"], 16)
            pe.wait_ge(s["wf2_in"], 16)
            for g in range(NG):
                norm_rows(g, 1)
                pe.wait_ge(s["rs_ready"], g + 1)
                for t in range(TG):
                    tt = g * TG + t
                    last = mm(bk(g, 2)[:, t * P:(t + 1) * P], st[:, 1, 18, tt:tt + 1].broadcast_to([P, P]), ident,
                              start=True, stop=True)
                last.then_inc(s["rsb_mm"], 1)
                for i, c in enumerate(UPB):
                    if c == 2:
                        pe.wait_ge(s["rsb_ready"], g + 1)
                    mm(bk(g, c)[:, :], wf1[:, i * P:(i + 1) * P], yT[:, g, :], start=True, stop=True) \
                        .then_inc(s["up_mm"], 1)
            for g in range(NG):
                pe.wait_ge(s["hsq_ready"], FC * (g + 1))
                for t in range(TG):
                    for c in range(FC):
                        last = mm(bk(g, 1)[:, t:t + 1], hsq[:, g, c, t * P:(t + 1) * P], ones[:],
                                  start=c == 0, stop=c == FC - 1)
                last.then_inc(s["hss2_mm"], 1)
                for t in range(TG):
                    for c in range(FC):
                        last = mm(bk(g, 0)[:, t * D:(t + 1) * D], hf[:, g, c, t * P:(t + 1) * P], wf2[:, c, :],
                                  start=c == 0, stop=c == FC - 1)
                last.then_inc(s["f_mm"], 1)
            for g in range(NG):
                pe.wait_ge(s["x3_ready"], TG * (g + 1))
                transpose_group(bk(g, 2), x3, g).then_inc(s["x3T_mm"], 1)
            for g in range(NG):
                pe.wait_ge(s["agg_ready"], g + 1)
                for j in range(3):
                    last = mm(bk(g, 3)[0:GB, 0:E], agg[:, g, j, :], col[:, K_GW + j * E:K_GW + (j + 1) * E],
                              start=j == 0, stop=j == 2)
                last.then_inc(s["gate_mm"], 1)
            for g in range(NG):
                pe.wait_ge(s["w_ready"], g + 1)
                for t in range(TG):
                    mm(bk(g, 3)[:, 8 + E * t:8 + E * (t + 1)], cst[0:GB, C_SEL + t * P:C_SEL + (t + 1) * P],
                       gl[:, g, 5, :], start=True, stop=True)
                mm(bk(g, 1)[0:E, :], gl[:, g, 5, :], cst[0:GB, C_SEL:C_SEL + GT], start=True, stop=True) \
                    .then_inc(s["wtok_mm"], 1)

            def up(n):
                e, g = divmod(n, NG)
                if g == 0:
                    pe.wait_ge(wup_in[e % 2], 16 * (e // 2 + 1))
                for c in range(FC):
                    if n >= NG or c == 3:
                        pe.wait_ge(s["moe_h"], n * FC + 1 if c == 3 else (n - NG) * FC + (4 if c == 0 else c + 1))
                    mm(bk(g, c % 3)[:, :], wup[:, e % 2, c * P:(c + 1) * P], x3T[:, g, :], start=True, stop=True) \
                        .then_inc(s["moe_up"], 1)

            def down(n):
                e, g = divmod(n, NG)
                if g == 0:
                    pe.wait_ge(wdn_in[e % 2], 16 * (e // 2 + 1))
                pe.wait_ge(s["moe_h"], FC * (n + 1))
                if n >= NG:
                    pe.wait_ge(s["moe_acc"], n - NG + 1)
                for t in range(TG):
                    d = bk(g, 3)[:, t * D:(t + 1) * D]
                    if e == E:
                        mm(d, wT[:, g, t * P:(t + 1) * P], bdn[:], start=True, stop=False)
                    for c in range(FC):
                        last = mm(d, hT[:, g, c, t * P:(t + 1) * P], wdn[:, e % 2, c, :],
                                  start=c == 0 and e < E, stop=c == FC - 1)
                last.then_inc(s["moe_y"], 1)

            pe.wait_ge(s["wtok_ready"], NG)
            pe.wait_ge(s["bdn_in"], 16)
            up(0)
            for n in range(NG * (E + 1)):
                if n + 1 < NG * (E + 1):
                    up(n + 1)
                down(n)


_OUT = (B, S, D)


def _constants(np):
    c = np.zeros((P, C_END - 1), np.float32)
    i = np.arange(P)
    c[:, C_ID:C_ID + P] = np.eye(P)
    c[:, C_HM:C_HM + HG] = (i[:, None] // HD) % HG == np.arange(HG)
    c[:, C_VM:C_VM + HG] = i[:, None] // S == np.arange(HG)
    keep = np.ones((S, E))
    keep[SEG:2 * SEG, 1] = 0
    keep[0:SEG, 2] = 0
    c[:, C_WM:C_WM + E] = np.tile(keep, (BT, 1))
    c[:, C_TRI:C_TRI + E * E] = np.tril(np.ones((E, E)), -1).reshape(1, -1)
    tok = np.arange(GT)
    c[0:GB, C_SEL:C_SEL + GT] = tok[None, :] // S == np.arange(GB)[:, None]
    c[0:E, C_MT:C_MT + GT] = np.tile(keep, (GB, 1)).T
    return c


def kernel(**inputs):
    import numpy as np
    import concourse.bacc as bacc
    from concourse.bass_utils import run_bass_kernel_spmd

    a = {k: np.asarray(v) for k, v in inputs.items()}
    L0 = lambda n: a["L0_cond_" + n]
    L1 = lambda n: a["L1_cond_" + n]
    chunks = lambda w: np.ascontiguousarray(w.reshape(FC, P, D).transpose(1, 0, 2).reshape(P, FC * D))
    bada = L0("b_ada").reshape(6, D)
    eb1 = np.concatenate([L1("eb1"), L1("sb1")[None]]).reshape((E + 1) * FC, P)
    tiny = np.full((P, 1), TINY, np.float32)
    arrays = {
        "x": a["x"].reshape(TILES, P, D),
        "consts": np.concatenate([_constants(np), tiny], axis=1),
        "cols": np.concatenate([a["cond_1024"].T, bada[[0, 1, 3, 4]].T, L0("b_f1").reshape(FC, P).T, eb1.T,
                                L1("gate_w").reshape(3, D, E).transpose(1, 0, 2).reshape(D, 3 * E), L1("time_w")], axis=1),
        "rows": np.concatenate([L0("b_q"), L0("b_k"), L0("b_v"), L0("b_o"), L0("b_f2"), bada[2], bada[5],
                                L1("gate_b"), L1("time_b")])[None],
        "w_ada": L0("w_ada"),
        "w_qkv": np.concatenate([L0("w_q"), L0("w_k"), L0("w_v")], axis=1),
        "w_o": L0("w_o"),
        "w_f1": L0("w_f1"),
        "w_f2": chunks(L0("w_f2")),
        "w_up": np.concatenate([L1("ew1"), L1("sw1")[None]]),
        "w_down": np.stack([chunks(w) for w in [*L1("ew2"), L1("sw2")]]),
        "b_down": np.concatenate([L1("eb2"), L1("sb2")[None]]),
    }
    nc = bacc.Bacc("TRN2", target_bir_lowering=False, num_devices=1)
    aps = []
    for name in arrays:
        arrays[name] = np.ascontiguousarray(arrays[name])
        aps.append(nc.dram_tensor(name, arrays[name].shape, mybir.dt.from_np(arrays[name].dtype),
                                  kind="ExternalInput").ap())
    out = nc.dram_tensor("out", (TILES, P, D), mybir.dt.float32, kind="ExternalOutput").ap()
    cond_resid_kernel(nc, *aps, out)
    r = run_bass_kernel_spmd(nc, [arrays], core_ids=[0])
    return r.results[0]["out"].reshape(_OUT)
```

```python
import math

import concourse.bass as bass
from concourse import mybir
from contextlib import ExitStack

B, S, D = 32, 32, 128
H, HD, FF = 16, 8, 512
E = 4
P = 128
TILES = B * S // P
BT = P // S
NG = 2
TG = TILES // NG
GT = TG * P
GB = B // NG
HG = 4
NHG = H // HG
FC = FF // P
VW = HG * HD + HG
SEG = 10
TAIL = S - 2 * SEG

C_ID, C_HM, C_VM, C_WM, C_TRI, C_TINY, C_END = 0, 128, 132, 136, 140, 156, 157
S_SEL, S_MT, S_END = 0, 1024, 1536
K_COND, K_BADA, K_BF1, K_EB1, K_GW, K_TW = 0, 32, 36, 40, 60, 72
K_END = 80
R_QKV, R_BO, R_BF2, R_BG, R_GB, R_TB = 0, 384, 512, 640, 896, 900
R_END = 908


def _beta(a, b):
    return math.exp(math.lgamma(a) + math.lgamma(b) - math.lgamma(a + b))


RATIO = _beta(HD / 2, 0.5) / _beta(D / 2, 0.5)
MAX_ARG = 0.9999899864196777
A = math.atanh(MAX_ARG)
TINY = 1e-30
EPS = 1e-7


def cond_resid_kernel(nc, x, consts, sels, cols, rows, w_ada, w_qkv, w_o, w_f1, w_f2, w_up, w_down, b_down, out):
    f32 = mybir.dt.float32
    u32 = mybir.dt.uint32
    f32r = mybir.dt.float32r
    ALU = mybir.AluOpType
    ACT = mybir.ActivationFunctionType
    X = mybir.AxisListType.X

    ctx = ExitStack()
    with ctx:
        def sb(name, shape, dt=f32):
            return ctx.enter_context(nc.sbuf_tensor(name, shape, dt))

        def sem(name):
            return ctx.enter_context(nc.semaphore(name))

        cst = sb("cst", [P, C_END])
        sel = sb("sel", [B, S_END])
        col = sb("col", [P, K_END])
        row = sb("row", [P, R_END])
        wqkv = sb("wqkv", [P, 3 * D])
        wo = sb("wo", [P, D])
        wf1 = sb("wf1", [P, FF])
        wf2 = sb("wf2", [P, FC, D])
        wdn0 = sb("wdn0", [P, FC, D])
        whi = sb("whi", [P, E + 1, FF], f32r)
        wlo = sb("wlo", [P, E + 1, FF], f32r)
        bdn = sb("bdn", [E + 1, D])
        ident = cst[:, C_ID:C_ID + P]
        ones = sb("ones", [P, 1])
        adaT = sb("adaT", [P, 4, B])
        adag = sb("adag", [B, 2 * D])
        gain = sb("gain", [P, TILES, 2 * D])
        silu = sb("silu", [P, B])
        mod = sb("mod", [GB, NG, 2 * E])
        xin = sb("xin", [P, TILES, D])
        x1 = sb("x1", [P, TILES, D])
        xn = sb("xn", [P, TILES, D])
        x3 = xn
        yT = sb("yT", [P, NG, GT])
        ysq = sb("ysq", [P, NG, GT])
        qkv = sb("qkv", [P, TILES, 3 * D])
        qk = sb("qk", [P, TILES, 2 * D])
        vs = sb("vs", [P, TILES, D])
        vrep = sb("vrep", [P, NG, TG * BT, D])
        qsq = [vrep[:, g].rearrange("p r d -> p (r d)")[:, 0:TG * 3 * D] for g in range(NG)]
        vexp = sb("vexp", [P, NG, TG * BT, NHG, VW])
        qT = sb("qT", [P, NG, GT])
        kexp = sb("kexp", [P, NG, TG * BT, HG, S])
        prob = sb("prob", [P, NG, NHG, GT])
        wada = prob[:, 1].rearrange("p n t -> p (n t)")[:, 0:6 * D]
        probT = sb("probT", [P, NG, NHG, GT])
        o = sb("o", [P, TILES, NHG, VW])
        osq = xn
        ain = ysq[:].rearrange("p g (t d) -> p (g t) d", d=D)
        ainT = sb("ainT", [P, NG, GT])
        ap, gt, tmp = (qkv[:, :, i * D:(i + 1) * D] for i in range(3))
        rsb = ainT
        hf = prob
        hsq = kexp[:].rearrange("p g r h s -> p g (r h s)").rearrange("p g (c t) -> p g c t", c=FC)
        hT = (probT, prob)
        x3hi = sb("x3hi", [P, NG, GT], f32r)
        x3lo = sb("x3lo", [P, NG, GT], f32r)
        bst = sb("bst", [P, 2, TILES, 6])
        mv = sb("mv", [P, 2, TILES, 2])
        st = sb("st", [P, 2, 24, TILES])
        heads = sb("heads", [P, NG, 4, 204])
        onrm = sb("onrm", [P, 4, TILES])
        seg = sb("seg", [P, NG, 3, GB])
        agg = sb("agg", [P, NG, 3, GB])
        gl = sb("gl", [GB, NG, 6, E])
        gp = sb("gp", [GB, NG, 2, E * E])
        gs = sb("gs", [GB, NG, 5])
        wtok = sb("wtok", [P, E, TILES])
        wT = qT[0:E + 1]

        bank = [ctx.enter_context(nc.psum_tensor(f"bank{i}", [P, 512], f32)) for i in range(8)]

        v_dram = nc.dram_tensor("v_dram", (NG, P, TG, D), f32, kind="Internal").ap()

        both = """trans_mm xn_even xn_odd vals funcs yT_ready ysq_ready yss_mm
        qkv_mm qkv_ready qsq_ready c_ready v_ready vexp_ready qk_ready qT_ready kexp_ready sc_mm p_ready
        pT_mm pT_even pT_odd o_mm o_ready osq_ready ain_ready ainT_ready ap_mm ap_ready gt_ready sq_done
        xtmp_mid xtmp_even xtmp_odd x1_ready x3_ready rs_ready rsb_mm rsb_ready up_mm hf_ready
        hsq_ready hpair_ready hsum_ready hss_mm f_mm x3hi_ready x3lo_ready agg_ready mod_ready gate_mm
        w_ready wtok_ready wT_ready moe_up moe_h moe_y moe_acc v_out""".split()
        s = {n: [sem(f"{n}{g}") for g in range(NG)] for n in both}
        once = """consts_in wada_in sels_in rows_in wqkv_in wmlp_in ones_ready ada_mm adaT_ready adag_ready
        gain_mm gain_ready silu_e silu_ready split stored vec_step pool_step row_ready""".split()
        s.update({n: sem(n) for n in once})
        x_in = [sem(f"x_in{g}") for g in range(NG)]
        vrep_in = [sem(f"vrep_in{g}") for g in range(NG)]
        w_in = [sem(f"w_in{e}") for e in range(E + 1)]

        TRANS = "xnT0 qT kT ainT xnT1 x3T".split()
        VALS = "mean0 m0 var0 nb0 head out tok n0 beta0 mean1 m1 var1 nb1 n1 beta1 logit".split()
        FUNCS = "src0 ln0 rstd0 y0 head out tok a0 th0 src1 ln1 rstd1 y1 h a1 th1 gexp".split()
        GATES = "logit token transposed".split()

        def nth(names, name):
            return names.index(name) + 1

        nc_v, nc_a, nc_t, nc_p = nc.vector, nc.scalar, nc.tensor, nc.gpsimd

        def T(g):
            return slice(g * TG, (g + 1) * TG)

        def tiles(g):
            return range(g * TG, (g + 1) * TG)

        def bk(g, i):
            return bank[4 * g + i]

        UPB = [3, 0, 2, 1]

        def oo(g, i):
            return heads[:, g].rearrange("p i w -> p (i w)")[:, i * TG * H:(i + 1) * TG * H]

        vslot = lambda i: vrep[:, i // 4].rearrange("p r d -> p (r d)")[:, (i % 4) * FF:(i % 4 + 1) * FF]
        wup = [vslot(i) for i in range(E + 1)]
        vflat = vexp[:, 0].rearrange("p r n w -> p (r n w)")
        wdn = [wdn0[:]] + [vflat[:, i * FF:(i + 1) * FF].rearrange("p (c d) -> p c d", c=FC) for i in range(E)]

        def chunk_seq(e, c):
            return e * FC + c + (e >= 2)

        WT_SEQ = 2 * FC

        block = ctx.enter_context(nc.Block())

        @block.sync
        def _(sp):
            for g in range(NG):
                sp.dma_start(xin[:, T(g), :], x[T(g)].rearrange("t p d -> p t d")).then_inc(x_in[g], 16)
            sp.dma_start(row[:], rows.broadcast_to([P, R_END])).then_inc(s["rows_in"], 16)
            sp.dma_start(wqkv[:], w_qkv).then_inc(s["wqkv_in"], 16)
            sp.dma_start(wo[:], w_o).then_inc(s["wmlp_in"], 16)
            sp.dma_start(wf1[:], w_f1).then_inc(s["wmlp_in"], 16)
            sp.dma_start(wf2[:], w_f2.rearrange("p (c d) -> p c d", c=FC)).then_inc(s["wmlp_in"], 16)
            sp.dma_start(bdn[:], b_down).then_inc(s["wmlp_in"], 16)

            def load_up(e):
                sp.dma_start(wup[e], w_up[e]).then_inc(w_in[e], 16)

            def load_down(e):
                sp.dma_start(wdn[e], w_down[e].rearrange("p (c d) -> p c d", c=FC)).then_inc(w_in[e], 16)

            load_down(0)
            for g in range(NG):
                sp.wait_ge(s["v_ready"][g], 1)
                sp.dma_start(v_dram[g], vs[:, T(g), :]).then_inc(s["v_out"][g], 16)
                sp.wait_ge(s["v_out"][g], 16)
                for h in range(HG):
                    sp.dma_start(vrep[h * S:(h + 1) * S, g, :, :].rearrange("s (t b) d -> s t b d", b=BT),
                                 v_dram[g].rearrange("(b s) t d -> s t b d", b=BT)).then_inc(vrep_in[g], 16)
            sp.wait_ge(s["vexp_ready"][0], 1)
            for e in range(E):
                load_up(e)
            sp.wait_ge(s["o_mm"][0], 1)
            for e in range(1, E + 1):
                load_down(e)
            sp.wait_ge(s["vexp_ready"][1], 1)
            load_up(E)
            for g in range(NG):
                sp.wait_ge(s["moe_acc"][g], E + 1)
                sp.dma_start(out[T(g)].rearrange("t p d -> p t d"), x3[:, T(g), :]).then_inc(s["stored"], 16)
            sp.wait_ge(s["stored"], 16 * NG)

        @block.vector
        def _(v):
            steps = [0]

            def step(ins):
                ins.then_inc(s["vec_step"], 1)
                steps[0] += 1

            def settle():
                v.wait_ge(s["vec_step"], steps[0])

            def link(ins):
                step(ins)
                settle()

            def once_ones(_):
                nc_v.memset(ones[:], 1.0).then_inc(s["ones_ready"], 1)
                v.wait_ge(s["consts_in"], 32)

            def adaT_out(_):
                v.wait_ge(s["ada_mm"], 1)
                for j in range(4):
                    nc_v.tensor_scalar(adaT[:, j, :], bank[0][:, j * B:(j + 1) * B],
                                       col[:, K_BADA + j:K_BADA + j + 1], float(j % 2), ALU.add,
                                       ALU.add).then_inc(s["adaT_ready"], 1)

            def adag_out(_):
                v.wait_ge(s["rows_in"], 16)
                v.wait_ge(s["ada_mm"], 2)
                nc_v.tensor_tensor(adag[:], bank[4][0:B, 0:2 * D], row[0:B, R_BG:R_BG + 2 * D],
                                   ALU.add).then_inc(s["adag_ready"], 1)

            def silu_out(_):
                v.wait_ge(s["silu_e"], 1)
                link(nc_v.tensor_scalar(silu[:], silu[:], 1.0, None, ALU.add))
                link(nc_v.reciprocal(silu[:], silu[:]))
                nc_v.tensor_tensor(silu[:], silu[:], col[:, K_COND:K_COND + B], ALU.mult).then_inc(s["silu_ready"], 1)

            def stats(g, j, src):
                for t in tiles(g):
                    step(nc_v.bn_stats(bst[:, j, t, :], src[:, t, :]))

            def mean_square(g, j):
                q = lambda i: st[:, j, i, T(g)]
                settle()
                for t in tiles(g):
                    step(nc_v.bn_aggr(mv[:, j, t, :], bst[:, j, t, :]))
                settle()
                link(nc_v.tensor_tensor(q(0), mv[:, j, T(g), 0], mv[:, j, T(g), 0], ALU.mult))
                nc_v.tensor_tensor(q(1), q(0), mv[:, j, T(g), 1], ALU.add).then_inc(s["vals"][g], 1)

            def log_small(g, j):
                q = lambda i: st[:, j, i, T(g)]
                v.wait_ge(s["funcs"][g], nth(FUNCS, f"src{j}"))
                nc_v.tensor_scalar(q(3), q(2), MAX_ARG, None, ALU.min).then_inc(s["vals"][g], 1)
                link(nc_v.reciprocal(q(4), q(2)))
                v.wait_ge(s["vals"][g], nth(VALS, f"m{j}"))
                link(nc_v.tensor_tensor(q(5), q(3), q(3), ALU.mult))
                link(nc_v.tensor_scalar(q(6), q(5), 1.0 / 13, None, ALU.mult))
                for i in (11, 9, 7, 5, 3):
                    link(nc_v.scalar_tensor_tensor(q(6), q(6), 1.0 / i, q(5), ALU.add, ALU.mult))
                step(nc_v.tensor_scalar(q(6), q(6), 1.0, None, ALU.add))
                step(nc_v.tensor_scalar(q(7), q(3), 0.25, None, ALU.is_lt))

            def log_factor(g, j):
                q = lambda i: st[:, j, i, T(g)]
                v.wait_ge(s["funcs"][g], nth(FUNCS, f"ln{j}"))
                link(nc_v.tensor_tensor(q(10), q(8), q(9), ALU.subtract))
                link(nc_v.scalar_tensor_tensor(q(11), q(10), 0.5, q(4), ALU.mult, ALU.mult))
                link(nc_v.copy_predicated(q(11), q(7).bitcast(u32), q(6)))
                link(nc_v.reciprocal(q(12), q(11)))
                link(nc_v.tensor_tensor(q(12), q(12), q(12), ALU.mult))
                nc_v.scalar_tensor_tensor(q(13), q(12), 1e-6, mv[:, j, T(g), 1], ALU.mult,
                                          ALU.add).then_inc(s["vals"][g], 1)

            def normalise(g, j, src):
                q = lambda i: st[:, j, i, T(g)]
                v.wait_ge(s["funcs"][g], nth(FUNCS, f"rstd{j}"))
                link(nc_v.reciprocal(q(15), q(14)))
                nc_v.scalar_tensor_tensor(q(16), mv[:, j, T(g), 0], -1.0, q(15), ALU.mult,
                                          ALU.mult).then_inc(s["vals"][g], 1)
                for t in tiles(g)[::2]:
                    nc_v.tensor_scalar(xn[:, t, :], src[:, t, :], mv[:, j, t, 0:1], st[:, j, 15, t:t + 1],
                                       ALU.subtract, ALU.mult).then_inc(s["xn_even"][g], 1)

            def modulate(g, j):
                v.wait_ge(s["trans_mm"][g], nth(TRANS, f"xnT{j}"))
                v.wait_ge(s["adaT_ready"], 4)
                b0 = g * GB
                y3 = yT[:, g, :].rearrange("p (b s) -> p b s", s=S)
                sc = adaT[:, 2 * j + 1, b0:b0 + GB].unsqueeze(2).broadcast_to([P, GB, S])
                sh = adaT[:, 2 * j, b0:b0 + GB].unsqueeze(2).broadcast_to([P, GB, S])
                link(nc_v.tensor_tensor(y3, bk(g, 0)[:, :].rearrange("p (b s) -> p b s", s=S), sc, ALU.mult))
                nc_v.tensor_tensor(y3, y3, sh, ALU.add).then_inc(s["yT_ready"][g], 1)

            def clamp_y(g, j):
                q = lambda i: st[:, j, i, T(g)]
                v.wait_ge(s["funcs"][g], nth(FUNCS, f"y{j}"))
                if j == 1:
                    nc_v.tensor_scalar(q(18), q(0), 1.0 / A, 1.0, ALU.mult, ALU.max).then_inc(s["rs_ready"][g], 1)
                link(nc_v.reciprocal(q(17), q(0)))
                link(nc_v.tensor_scalar(q(17), q(17), A, 1.0, ALU.mult, ALU.min))

            n_hd = TG * 3 * H

            def project(g):
                v.wait_ge(s["rows_in"], 16)
                for i, t in enumerate(tiles(g)):
                    v.wait_ge(s["qkv_mm"][g], i + 1)
                    nc_v.scalar_tensor_tensor(qkv[:, t, :], bk(g, (i + 2) % 4)[:, 0:3 * D], st[:, 0, 17, t:t + 1],
                                              row[:, R_QKV:R_QKV + 3 * D], ALU.mult, ALU.add).then_inc(s["qkv_ready"][g], 1)

            def head_sums(g):
                v.wait_ge(s["qsq_ready"][g], TG)
                h0 = heads[:, g, 0, :]
                link(nc_v.tensor_reduce(h0[:, 0:n_hd], qsq[g].rearrange("p (h d) -> p h d", d=HD), X, ALU.add))
                nc_v.tensor_reduce(h0[:, n_hd:n_hd + 3 * TG], h0[:, 0:n_hd].rearrange("p (w h) -> p w h", h=H),
                                   X, ALU.add).then_inc(s["vals"][g], 1)

            def head_clamps(g):
                hh = lambda i: heads[:, g, i, :]
                v.wait_ge(s["funcs"][g], nth(FUNCS, "head"))
                link(nc_v.reciprocal(hh(2), hh(1)))
                link(nc_v.tensor_scalar(hh(3)[:, n_hd:n_hd + 3 * TG], hh(2)[:, n_hd:n_hd + 3 * TG], A * RATIO, RATIO,
                                        ALU.mult, ALU.min))
                w3 = lambda z: z[:, 0:n_hd].rearrange("p (w h) -> p w h", h=H)
                nc_v.scalar_tensor_tensor(w3(hh(3)), w3(hh(2)), A,
                                          hh(3)[:, n_hd:n_hd + 3 * TG].unsqueeze(2).broadcast_to([P, 3 * TG, H]),
                                          ALU.mult, ALU.min).then_inc(s["c_ready"][g], 1)
                v.wait_ge(s["c_ready"][g], 1)
                c4 = hh(3)[:, 0:n_hd].rearrange("p (t h) -> p t h", t=TG)[:, :, 0:2 * H]
                nc_v.tensor_tensor(qk[:, T(g), :].rearrange("p t (h d) -> p t h d", d=HD),
                                   qkv[:, T(g), 0:2 * D].rearrange("p t (h d) -> p t h d", d=HD),
                                   c4.unsqueeze(3).broadcast_to([P, TG, 2 * H, HD]), ALU.mult).then_inc(s["qk_ready"][g], 1)

            def expand_k(g):
                v.wait_ge(s["trans_mm"][g], nth(TRANS, "kT"))
                n = TG * BT
                kk = bk(g, 1)[:, :].rearrange("p (r s) -> p r s", s=S).unsqueeze(2).broadcast_to([P, n, HG, S])
                hm = cst[:, C_HM:C_HM + HG].unsqueeze(1).broadcast_to([P, n, HG]).unsqueeze(3).broadcast_to([P, n, HG, S])
                nc_v.tensor_tensor(kexp[:, g], kk, hm, ALU.mult).then_inc(s["kexp_ready"][g], 1)

            def copy_probs(g):
                for i in (0, 2):
                    v.wait_ge(s["pT_mm"][g], i + 1)
                    nc_v.tensor_copy(probT[:, g, i, :], bk(g, i)[:, :]).then_inc(s["pT_even"][g], 1)

            def head_squares(g):
                ov = o[:, T(g)].rearrange("p t n w -> p (t n) w")
                v.wait_ge(s["o_ready"][g], 2)
                step(nc_v.reciprocal(oo(g, 0).rearrange("p (n h) -> p n h", h=HG), ov[:, :, HG * HD:VW]))
                v.wait_ge(s["osq_ready"][g], 1)
                nc_v.tensor_reduce(oo(g, 1), osq[:, T(g), :].rearrange("p t (h d) -> p (t h) d", d=HD), X,
                                   ALU.add).then_inc(s["vals"][g], 1)

            def heads_out(g):
                v.wait_ge(s["funcs"][g], nth(FUNCS, "out"))
                link(nc_v.reciprocal(oo(g, 3), oo(g, 2)))
                link(nc_v.scalar_tensor_tensor(oo(g, 3), oo(g, 3), A, oo(g, 0), ALU.mult, ALU.min))
                n = TG * NHG
                c = oo(g, 3).rearrange("p (n h) -> p n h", h=HG).unsqueeze(3).broadcast_to([P, n, HG, HD])
                nc_v.tensor_tensor(ain[:, T(g), :].rearrange("p t (n h d) -> p (t n) h d", h=HG, d=HD),
                                   o[:, T(g)].rearrange("p t n w -> p (t n) w")[:, :, 0:HG * HD]
                                   .rearrange("p n (h d) -> p n h d", d=HD), c, ALU.mult).then_inc(s["ain_ready"][g], 1)
                link(nc_v.tensor_tensor(oo(g, 4), oo(g, 3), oo(g, 3), ALU.mult))
                link(nc_v.tensor_tensor(oo(g, 4), oo(g, 4), oo(g, 1), ALU.mult))
                nc_v.tensor_reduce(onrm[:, 0, T(g)], oo(g, 4).rearrange("p (t h) -> p t h", t=TG), X,
                                   ALU.add).then_inc(s["vals"][g], 1)

            def token_clamp(g):
                v.wait_ge(s["funcs"][g], nth(FUNCS, "tok"))
                link(nc_v.reciprocal(onrm[:, 2, T(g)], onrm[:, 1, T(g)]))
                link(nc_v.tensor_scalar(onrm[:, 2, T(g)], onrm[:, 2, T(g)], A, 1.0 / RATIO, ALU.mult, ALU.min))

            def branch_out(g, j, bnk, mm_done, bias, res):
                n0 = j * TG

                def project_out(t):
                    nc_v.scalar_tensor_tensor(ap[:, t, :], bk(g, bnk)[:, (t % TG) * D:(t % TG + 1) * D],
                                              onrm[:, 2, t:t + 1], row[:, bias:bias + D],
                                              ALU.mult, ALU.add).then_inc(s["ap_ready"][g], 1)

                def gained(t, i):
                    v.wait_ge(s["ap_ready"][g], n0 + i + 1)
                    nc_v.tensor_tensor(gt[:, t, :], ap[:, t, :], gain[:, t, j * D:(j + 1) * D],
                                       ALU.mult).then_inc(s["gt_ready"][g], 1)

                def dot(t, i):
                    v.wait_ge(s["gt_ready"][g], n0 + i + 1)
                    step(nc_v.tensor_tensor_reduce(out=tmp[:, t, :], in0=res[:, t, :], in1=gt[:, t, :], scale=1.0,
                                                   scalar=0.0, op0=ALU.mult, op1=ALU.add, accum_out=st[:, j, 19, t:t + 1]))

                v.wait_ge(s[mm_done][g], 1)
                v.wait_ge(s["gain_ready"], 2 * (g + 1))
                for i in range(TG + 2):
                    t = g * TG + i
                    if i < TG:
                        project_out(t)
                    if 0 <= i - 1 < TG:
                        gained(t - 1, i - 1)
                    if 0 <= i - 2:
                        dot(t - 2, i - 2)
                q = lambda i: st[:, j, i, T(g)]
                link(nc_v.tensor_scalar(q(0), q(1), float(D), None, ALU.mult))
                step(nc_v.tensor_scalar(q(3), q(0), -1.0, 1.0, ALU.mult, ALU.add))

            def branch_norm(g, j):
                q = lambda i: st[:, j, i, T(g)]
                v.wait_ge(s["funcs"][g], nth(FUNCS, f"a{j}"))
                step(nc_v.reciprocal(q(22), q(20)))
                step(nc_v.reciprocal(q(23), q(21)))
                settle()
                link(nc_v.tensor_scalar(q(22), q(22), A, 1.0, ALU.mult, ALU.min))
                nc_v.tensor_tensor(q(20), q(22), q(21), ALU.mult).then_inc(s["vals"][g], 1)

            def mobius(g, j, res, dst):
                q = lambda i: st[:, j, i, T(g)]
                v.wait_ge(s["funcs"][g], nth(FUNCS, f"th{j}"))
                step(nc_v.tensor_tensor(q(4), q(22), q(23), ALU.mult))
                step(nc_v.tensor_tensor(q(5), q(22), q(22), ALU.mult))
                settle()
                step(nc_v.tensor_tensor(q(6), q(4), q(19), ALU.mult))
                step(nc_v.tensor_tensor(q(3), q(3), q(4), ALU.mult))
                step(nc_v.tensor_tensor(q(8), q(0), q(5), ALU.mult))
                settle()
                link(nc_v.tensor_scalar(q(6), q(6), 2.0, 1.0, ALU.mult, ALU.add))
                step(nc_v.tensor_tensor(q(8), q(6), q(8), ALU.add))
                step(nc_v.tensor_tensor(q(5), q(6), q(5), ALU.add))
                settle()
                link(nc_v.tensor_scalar(q(8), q(8), EPS, None, ALU.max))
                link(nc_v.reciprocal(q(8), q(8)))
                nc_v.tensor_tensor(q(3), q(3), q(8), ALU.mult).then_inc(s["vals"][g], 1)
                link(nc_v.tensor_tensor(q(5), q(5), q(8), ALU.mult))
                if j == 1:
                    for t in tiles(g)[::2]:
                        nc_v.scalar_tensor_tensor(tmp[:, t, :], gt[:, t, :], st[:, j, 3, t:t + 1], xin[:, t, :],
                                                  ALU.mult, ALU.add).then_inc(s["xtmp_even"][g], 1)
                for i in range(TG + 1):
                    t = g * TG + i
                    if i < TG:
                        if j == 0:
                            v.wait_ge(s["xtmp_mid"][g], i + 1)
                        elif i % 2:
                            v.wait_ge(s["xtmp_odd"][g], i // 2 + 1)
                        else:
                            v.wait_ge(s["xtmp_even"][g], i // 2 + 1)
                        nc_v.scalar_tensor_tensor(dst[:, t, :], res[:, t, :], st[:, j, 5, t:t + 1], tmp[:, t, :],
                                                  ALU.mult, ALU.add).then_inc(s["x3_ready" if j else "x1_ready"][g], 1)
                    if j == 0 and i:
                        v.wait_ge(s["x1_ready"][g], i)
                        step(nc_v.bn_stats(bst[:, 1, t - 1, :], x1[:, t - 1, :]))

            def hidden(g):
                v.wait_ge(s["rsb_ready"][g], 1)
                for i, c in enumerate(UPB):
                    v.wait_ge(s["up_mm"][g], i + 1)
                    nc_v.scalar_tensor_tensor(hf[:, g, i, :], rsb[:, g, :], col[:, K_BF1 + i:K_BF1 + i + 1], bk(g, c)[:, :],
                                              ALU.mult, ALU.add).then_inc(s["hf_ready"][g], 1)

            def sum_hidden(g):
                v.wait_ge(s["hsq_ready"][g], FC)
                step(nc_v.tensor_tensor(hsq[:, g, 2, :], hsq[:, g, 2, :], hsq[:, g, 3, :], ALU.add))
                v.wait_ge(s["hpair_ready"][g], 1)
                settle()
                nc_v.tensor_tensor(hsq[:, g, 0, :], hsq[:, g, 0, :], hsq[:, g, 2, :], ALU.add).then_inc(s["hsum_ready"][g], 1)

            def hidden_clamp(g):
                v.wait_ge(s["funcs"][g], nth(FUNCS, "h"))
                link(nc_v.reciprocal(onrm[:, 1, T(g)], onrm[:, 3, T(g)]))
                link(nc_v.scalar_tensor_tensor(onrm[:, 2, T(g)], onrm[:, 1, T(g)], A, st[:, 1, 17, T(g)], ALU.mult, ALU.min))

            def modulation(g):
                link(nc_v.tensor_tensor(mod[:, g, :], bk(g, 1)[0:GB, 8:8 + 2 * E], row[0:GB, R_TB:R_TB + 2 * E], ALU.add))
                nc_v.tensor_scalar(mod[:, g, 0:E], mod[:, g, 0:E], 1.0, None, ALU.add).then_inc(s["mod_ready"][g], 1)

            def x3_low(g):
                v.wait_ge(s["x3hi_ready"][g], 1)
                nc_v.tensor_tensor(x3lo[:, g, :], bk(g, 3)[:, :], x3hi[:, g, :].bitcast(f32),
                                   ALU.subtract).then_inc(s["x3lo_ready"][g], 1)

            def gate_inputs(g):
                xt = bk(g, 3)[:, :].rearrange("p (b s) -> p b s", s=S)
                for i, (a, b) in enumerate(((0, SEG), (SEG, 2 * SEG), (2 * SEG, S))):
                    step(nc_v.tensor_reduce(seg[:, g, i, :], xt[:, :, a:b], X, ALU.add))
                settle()
                step(nc_v.tensor_tensor(agg[:, g, 1, :], seg[:, g, 0, :], seg[:, g, 2, :], ALU.add))
                step(nc_v.tensor_tensor(agg[:, g, 2, :], seg[:, g, 1, :], seg[:, g, 2, :], ALU.add))
                settle()
                link(nc_v.tensor_tensor(agg[:, g, 0, :], agg[:, g, 1, :], seg[:, g, 1, :], ALU.add))
                step(nc_v.tensor_scalar(agg[:, g, 0, :], agg[:, g, 0, :], 1.0 / S, None, ALU.mult))
                nc_v.tensor_scalar(agg[:, g, 1:3, :], agg[:, g, 1:3, :], 1.0 / (SEG + TAIL), None,
                                   ALU.mult).then_inc(s["agg_ready"][g], 1)

            def gate_logits(g):
                L = lambda i: gl[:, g, i, :]
                v.wait_ge(s["gate_mm"][g], nth(GATES, "logit"))
                v.wait_ge(s["mod_ready"][g], 1)
                link(nc_v.tensor_tensor(L(0), bk(g, 3)[0:GB, 0:E], row[0:GB, R_GB:R_GB + E], ALU.add))
                link(nc_v.tensor_tensor(L(0), L(0), mod[:, g, 0:E], ALU.mult))
                link(nc_v.tensor_tensor(L(0), L(0), mod[:, g, E:2 * E], ALU.add))
                nc_v.tensor_reduce(gs[:, g, 0:1], L(0), X, ALU.max, negate=True).then_inc(s["vals"][g], 1)

            def gate_weights(g):
                L = lambda i: gl[:, g, i, :]
                v.wait_ge(s["funcs"][g], nth(FUNCS, "gexp"))
                link(nc_v.tensor_reduce(gs[:, g, 1:2], L(1), X, ALU.add))
                link(nc_v.reciprocal(gs[:, g, 2:3], gs[:, g, 1:2]))
                link(nc_v.tensor_scalar(L(2), L(1), gs[:, g, 2:3], None, ALU.mult))
                pj = L(2).unsqueeze(1).broadcast_to([GB, E, E])
                pi = L(2).unsqueeze(2).broadcast_to([GB, E, E])
                m = lambda i: gp[:, g, i, :].rearrange("p (i j) -> p i j", i=E)
                step(nc_v.tensor_tensor(m(0), pj, pi, ALU.is_gt))
                step(nc_v.tensor_tensor(m(1), pj, pi, ALU.is_equal))
                settle()
                link(nc_v.tensor_tensor(m(1), m(1), cst[0:GB, C_TRI:C_TRI + E * E].rearrange("p (i j) -> p i j", i=E),
                                        ALU.mult))
                link(nc_v.tensor_tensor(m(0), m(0), m(1), ALU.add))
                link(nc_v.tensor_reduce(L(3), m(0), X, ALU.add))
                link(nc_v.scalar_tensor_tensor(L(4), L(3), 1.5, L(2), ALU.is_lt, ALU.mult))
                link(nc_v.tensor_reduce(gs[:, g, 3:4], L(4), X, ALU.add))
                link(nc_v.tensor_scalar(gs[:, g, 3:4], gs[:, g, 3:4], 1e-8, None, ALU.add))
                link(nc_v.reciprocal(gs[:, g, 4:5], gs[:, g, 3:4]))
                nc_v.tensor_scalar(L(5), L(4), gs[:, g, 4:5], None, ALU.mult).then_inc(s["w_ready"][g], 1)

            def token_weights(g):
                v.wait_ge(s["gate_mm"][g], nth(GATES, "token"))
                nc_v.tensor_tensor(wtok[:, :, T(g)].rearrange("p e t -> p t e"),
                                   bk(g, 3)[:, 8:8 + E * TG].rearrange("p (t e) -> p t e", e=E),
                                   cst[:, C_WM:C_WM + E].unsqueeze(1).broadcast_to([P, TG, E]),
                                   ALU.mult).then_inc(s["wtok_ready"][g], 1)
                v.wait_ge(s["gate_mm"][g], nth(GATES, "transposed"))
                v.wait_ge(s["row_ready"], NG)
                nc_v.tensor_tensor(wT[0:E, g, :], bk(g, WT_SEQ % 3)[0:E, :], sel[0:E, S_MT:S_MT + GT],
                                   ALU.mult).then_inc(s["wT_ready"][g], 1)

            def accumulate(g, e):
                v.wait_ge(s["moe_y"][g], e + 1)
                if e == 0:
                    v.wait_ge(s["wtok_ready"][g], 1)
                else:
                    v.wait_ge(s["moe_acc"][g], e)
                if e < E:
                    for i, t in enumerate(tiles(g)):
                        last = nc_v.scalar_tensor_tensor(x3[:, t, :], bk(g, 3)[:, i * D:(i + 1) * D],
                                                         wtok[:, e, t:t + 1], x3[:, t, :], ALU.mult, ALU.add)
                else:
                    x3g = x3[:, T(g), :].rearrange("p t d -> p (t d)")
                    last = nc_v.tensor_tensor(x3g, bk(g, 3)[:, :], x3g, ALU.add)
                last.then_inc(s["moe_acc"][g], 1)

            def x_stats(g):
                v.wait_ge(x_in[g], 16)
                stats(g, 0, xin)

            def mean_square0(g): mean_square(g, 0)
            def log_small0(g): log_small(g, 0)
            def log_factor0(g): log_factor(g, 0)
            def normalise0(g): normalise(g, 0, xin)
            def modulate0(g): modulate(g, 0)
            def clamp_y0(g): clamp_y(g, 0)
            def branch_out0(g): branch_out(g, 0, 3, "ap_mm", R_BO, xin)
            def branch_norm0(g): branch_norm(g, 0)
            def mobius0(g): mobius(g, 0, xin, x1)
            def mean_square1(g): mean_square(g, 1)
            def log_small1(g): log_small(g, 1)
            def log_factor1(g): log_factor(g, 1)
            def normalise1(g): normalise(g, 1, x1)
            def modulate1(g): modulate(g, 1)
            def clamp_y1(g): clamp_y(g, 1)
            def branch_out1(g): branch_out(g, 1, 0, "f_mm", R_BF2, x1)
            def branch_norm1(g): branch_norm(g, 1)
            def mobius1(g): mobius(g, 1, x1, x3)
            def acc0(g): accumulate(g, 0)
            def acc1(g): accumulate(g, 1)
            def acc2(g): accumulate(g, 2)
            def acc3(g): accumulate(g, 3)
            def acc4(g): accumulate(g, 4)

            once_ones(0)
            x_stats(1)
            mean_square0(1)
            log_small0(1)
            x_stats(0)
            adaT_out(0)
            adag_out(0)
            log_factor0(1)
            normalise0(1)
            mean_square0(0)
            log_small0(0)
            log_factor0(0)
            normalise0(0)
            modulate0(0)
            clamp_y0(0)
            modulate0(1)
            project(0)
            head_sums(0)
            head_clamps(0)
            expand_k(0)
            clamp_y0(1)
            project(1)
            head_sums(1)
            head_clamps(1)
            copy_probs(0)
            expand_k(1)
            head_squares(0)
            heads_out(0)
            token_clamp(0)
            branch_out0(0)
            branch_norm0(0)
            mobius0(0)
            mean_square1(0)
            silu_out(0)
            log_small1(0)
            log_factor1(0)
            copy_probs(1)
            normalise1(0)
            head_squares(1)
            modulate1(0)
            heads_out(1)
            token_clamp(1)
            branch_out0(1)
            clamp_y1(0)
            branch_norm0(1)
            modulation(0)
            hidden(0)
            sum_hidden(0)
            mobius0(1)
            mean_square1(1)
            log_small1(1)
            log_factor1(1)
            normalise1(1)
            modulate1(1)
            hidden_clamp(0)
            branch_out1(0)
            branch_norm1(0)
            clamp_y1(1)
            modulation(1)
            mobius1(0)
            hidden(1)
            sum_hidden(1)
            x3_low(0)
            gate_inputs(0)
            gate_logits(0)
            gate_weights(0)
            token_weights(0)
            hidden_clamp(1)
            branch_out1(1)
            branch_norm1(1)
            acc0(0)
            mobius1(1)
            x3_low(1)
            acc1(0)
            gate_inputs(1)
            gate_logits(1)
            acc2(0)
            gate_weights(1)
            token_weights(1)
            acc3(0)
            acc0(1)
            acc1(1)
            acc2(1)
            acc3(1)
            acc4(0)
            acc4(1)

        @block.scalar
        def _(a):
            act = nc_a.activation
            tiny = cst[:, C_TINY:C_TINY + 1]

            def src_norm(g, j):
                q = lambda i: st[:, j, i, T(g)]
                a.wait_ge(s["vals"][g], nth(VALS, f"mean{j}"))
                act(q(2), q(1), ACT.Sqrt, scale=float(D), bias=tiny).then_inc(s["funcs"][g], 1)

            def logs(g, j):
                q = lambda i: st[:, j, i, T(g)]
                a.wait_ge(s["vals"][g], nth(VALS, f"m{j}"))
                act(q(8), q(3), ACT.Ln, scale=1.0, bias=1.0)
                act(q(9), q(3), ACT.Ln, scale=-1.0, bias=1.0).then_inc(s["funcs"][g], 1)

            def rstd(g, j):
                q = lambda i: st[:, j, i, T(g)]
                a.wait_ge(s["vals"][g], nth(VALS, f"var{j}"))
                act(q(14), q(13), ACT.Sqrt).then_inc(s["funcs"][g], 1)

            def normalise(g, j, src):
                a.wait_ge(s["vals"][g], nth(VALS, f"nb{j}"))
                for t in tiles(g)[1::2]:
                    act(xn[:, t, :], src[:, t, :], ACT.Identity, scale=st[:, j, 15, t:t + 1],
                        bias=st[:, j, 16, t:t + 1]).then_inc(s["xn_odd"][g], 1)

            def square_y(g, j):
                a.wait_ge(s["yT_ready"][g], j + 1)
                act(ysq[:, g, :], yT[:, g, :], ACT.Square).then_inc(s["ysq_ready"][g], 1)

            def norm_y(g, j):
                a.wait_ge(s["yss_mm"][g], j + 1)
                act(st[:, j, 0, T(g)], bk(g, 1)[:, 0:TG], ACT.Sqrt, bias=tiny).then_inc(s["funcs"][g], 1)

            def gains(g):
                for i in range(2):
                    a.wait_ge(s["gain_mm"], 2 * g + i + 1)
                    t = g * TG + 2 * i
                    act(gain[:, t:t + 2, :].rearrange("p t d -> p (t d)"), bk(g, 2 + i)[:, :],
                        ACT.Copy).then_inc(s["gain_ready"], 1)

            def square_qkv(g):
                for i, t in enumerate(tiles(g)):
                    a.wait_ge(s["qkv_ready"][g], i + 1)
                    act(qsq[g][:, i * 3 * D:(i + 1) * 3 * D], qkv[:, t, :], ACT.Square).then_inc(s["qsq_ready"][g], 1)

            def head_norms(g):
                a.wait_ge(s["vals"][g], nth(VALS, "head"))
                act(heads[:, g, 1, :], heads[:, g, 0, :], ACT.Sqrt, bias=tiny).then_inc(s["funcs"][g], 1)

            def copy_qT(g):
                a.wait_ge(s["trans_mm"][g], nth(TRANS, "qT"))
                act(qT[:, g, :], bk(g, 0)[:, :], ACT.Copy).then_inc(s["qT_ready"][g], 1)

            def exps(g):
                a.wait_ge(s["sc_mm"][g], 1)
                for i in range(NHG):
                    act(prob[:, g, i, :], bk(g, i)[:, :], ACT.Exp, scale=HD ** -0.5).then_inc(s["p_ready"][g], 1)

            def silu_exp(_):
                act(silu[:], col[:, K_COND:K_COND + B], ACT.Exp, scale=-1.0).then_inc(s["silu_e"], 1)

            def copy_probs(g):
                for i in (1, 3):
                    a.wait_ge(s["pT_mm"][g], i + 1)
                    act(probT[:, g, i, :], bk(g, i)[:, :], ACT.Copy).then_inc(s["pT_odd"][g], 1)

            def copy_o(g):
                a.wait_ge(s["o_mm"][g], 1)
                for i in range(2):
                    t = g * TG + 2 * i
                    act(o[:, t:t + 2].rearrange("p t n w -> p (t n w)"), bk(g, i)[:, 0:2 * NHG * VW],
                        ACT.Copy).then_inc(s["o_ready"][g], 1)
                a.wait_ge(s["o_ready"][g], 2)
                act(osq[:, T(g), :].rearrange("p t (n w) -> p (t n) w", w=HG * HD),
                    o[:, T(g)].rearrange("p t n w -> p (t n) w")[:, :, 0:HG * HD], ACT.Square).then_inc(s["osq_ready"][g], 1)

            def out_norms(g):
                a.wait_ge(s["vals"][g], nth(VALS, "out"))
                act(oo(g, 2), oo(g, 1), ACT.Sqrt, bias=tiny).then_inc(s["funcs"][g], 1)

            def copy_ainT(g):
                a.wait_ge(s["trans_mm"][g], nth(TRANS, "ainT"))
                act(ainT[:, g, :], bk(g, 2)[:, :], ACT.Copy).then_inc(s["ainT_ready"][g], 1)

            def token_norms(g):
                a.wait_ge(s["vals"][g], nth(VALS, "tok"))
                act(onrm[:, 1, T(g)], onrm[:, 0, T(g)], ACT.Sqrt, bias=tiny).then_inc(s["funcs"][g], 1)

            def branch_squares(g, j):
                n0 = j * TG

                def square(i, src, ready, lane, q):
                    t = g * TG + i
                    a.wait_ge(s[ready][g], n0 + i + 1)
                    act(qk[:, t, lane * D:(lane + 1) * D], src[:, t, :], ACT.Square,
                        accum_out=st[:, j, q, t:t + 1]).then_inc(s["sq_done"][g], 1)

                for i in range(TG + 1):
                    if i < TG:
                        square(i, ap, "ap_ready", 0, 20)
                    if i:
                        square(i - 1, gt, "gt_ready", 1, 21)
                a.wait_ge(s["sq_done"][g], 2 * (n0 + TG))
                act(st[:, j, 20:22, T(g)], st[:, j, 20:22, T(g)], ACT.Sqrt, bias=tiny).then_inc(s["funcs"][g], 1)

            def tanh_norm(g, j):
                a.wait_ge(s["vals"][g], nth(VALS, f"n{j}"))
                act(st[:, j, 22, T(g)], st[:, j, 20, T(g)], ACT.Tanh).then_inc(s["funcs"][g], 1)

            def branch_scaled(g, j):
                a.wait_ge(s["vals"][g], nth(VALS, f"beta{j}"))
                for t in tiles(g) if j == 0 else tiles(g)[1::2]:
                    act(tmp[:, t, :], gt[:, t, :], ACT.Copy, scale=st[:, j, 3, t:t + 1]).then_inc(s["xtmp_mid"][g], 1)

            def copy_rsb(g):
                a.wait_ge(s["rsb_mm"][g], 1)
                act(rsb[:, g, :], bk(g, 2)[:, :], ACT.Copy).then_inc(s["rsb_ready"][g], 1)

            def square_hidden(g):
                for c in range(FC):
                    a.wait_ge(s["hf_ready"][g], c + 1)
                    act(hsq[:, g, c, :], hf[:, g, c, :], ACT.Square).then_inc(s["hsq_ready"][g], 1)

            def hidden_norms(g):
                a.wait_ge(s["hss_mm"][g], 1)
                act(onrm[:, 3, T(g)], bk(g, 1)[:, 0:TG], ACT.Sqrt, bias=tiny).then_inc(s["funcs"][g], 1)

            def x3_high(g):
                a.wait_ge(s["trans_mm"][g], nth(TRANS, "x3T"))
                act(x3hi[:, g, :], bk(g, 3)[:, :], ACT.Copy).then_inc(s["x3hi_ready"][g], 1)

            def gate_exp(g):
                a.wait_ge(s["vals"][g], nth(VALS, "logit"))
                act(gl[:, g, 1, :], gl[:, g, 0, :], ACT.Exp, bias=gs[:, g, 0:1]).then_inc(s["funcs"][g], 1)

            def gelu(g, e):
                if e >= 2:
                    a.wait_ge(s["moe_y"][g], e - 1)
                for c in range(FC):
                    a.wait_ge(s["moe_up"][g], e * FC + c + 1)
                    act(hT[e % 2][:, g, c, :], bk(g, chunk_seq(e, c) % 3)[:, :], ACT.Gelu_apprx_tanh,
                        bias=col[:, K_EB1 + e * FC + c:K_EB1 + e * FC + c + 1]).then_inc(s["moe_h"][g], 1)

            def src_norm0(g): src_norm(g, 0)
            def logs0(g): logs(g, 0)
            def rstd0(g): rstd(g, 0)
            def normalise0(g): normalise(g, 0, xin)
            def square_y0(g): square_y(g, 0)
            def norm_y0(g): norm_y(g, 0)
            def branch_squares0(g): branch_squares(g, 0)
            def tanh_norm0(g): tanh_norm(g, 0)
            def branch_scaled0(g): branch_scaled(g, 0)
            def src_norm1(g): src_norm(g, 1)
            def logs1(g): logs(g, 1)
            def rstd1(g): rstd(g, 1)
            def normalise1(g): normalise(g, 1, x1)
            def square_y1(g): square_y(g, 1)
            def norm_y1(g): norm_y(g, 1)
            def branch_squares1(g): branch_squares(g, 1)
            def tanh_norm1(g): tanh_norm(g, 1)
            def branch_scaled1(g): branch_scaled(g, 1)
            def gelu0(g): gelu(g, 0)
            def gelu1(g): gelu(g, 1)
            def gelu2(g): gelu(g, 2)
            def gelu3(g): gelu(g, 3)
            def gelu4(g): gelu(g, 4)

            a.dma_start(cst[:], consts).then_inc(s["consts_in"], 16)
            a.dma_start(col[:], cols).then_inc(s["consts_in"], 16)
            a.dma_start(wada, w_ada).then_inc(s["wada_in"], 16)
            a.dma_start(sel[:], sels).then_inc(s["sels_in"], 16)
            a.wait_ge(s["consts_in"], 32)
            src_norm0(1)
            logs0(1)
            rstd0(1)
            normalise0(1)
            src_norm0(0)
            logs0(0)
            rstd0(0)
            normalise0(0)
            square_y0(0)
            gains(0)
            gains(1)
            norm_y0(0)
            silu_exp(0)
            square_y0(1)
            square_qkv(0)
            norm_y0(1)
            head_norms(0)
            copy_qT(0)
            square_qkv(1)
            head_norms(1)
            exps(0)
            copy_qT(1)
            copy_probs(0)
            copy_o(0)
            out_norms(0)
            copy_ainT(0)
            token_norms(0)
            branch_squares0(0)
            tanh_norm0(0)
            branch_scaled0(0)
            src_norm1(0)
            exps(1)
            logs1(0)
            copy_probs(1)
            rstd1(0)
            normalise1(0)
            copy_o(1)
            out_norms(1)
            square_y1(0)
            copy_ainT(1)
            token_norms(1)
            norm_y1(0)
            branch_squares0(1)
            copy_rsb(0)
            tanh_norm0(1)
            square_hidden(0)
            branch_scaled0(1)
            src_norm1(1)
            logs1(1)
            hidden_norms(0)
            rstd1(1)
            normalise1(1)
            square_y1(1)
            norm_y1(1)
            branch_squares1(0)
            tanh_norm1(0)
            branch_scaled1(0)
            copy_rsb(1)
            square_hidden(1)
            x3_high(0)
            gate_exp(0)
            gelu0(0)
            gelu1(0)
            hidden_norms(1)
            branch_squares1(1)
            tanh_norm1(1)
            gelu2(0)
            branch_scaled1(1)
            x3_high(1)
            gelu3(0)
            gate_exp(1)
            gelu0(1)
            gelu1(1)
            gelu4(0)
            gelu2(1)
            gelu3(1)
            gelu4(1)

        @block.gpsimd
        def _(p):
            vm = cst[:, C_VM:C_VM + HG]
            n = TG * BT * NHG

            def start(_):
                p.wait_ge(s["consts_in"], 32)
                for g in range(NG):
                    vd = vexp[:, g].rearrange("p r n w -> p (r n) w")
                    nc_p.tensor_copy(vd[:, :, HG * HD:VW], vm.unsqueeze(1).broadcast_to([P, n, HG]))

            def ones_row(g):
                p.wait_ge(s["sc_mm"][g], 1)
                nc_p.memset(wT[:, g, :], 1.0).then_inc(s["row_ready"], 1)

            def clamp_v(g):
                p.wait_ge(s["c_ready"][g], 1)
                c = heads[:, g, 3, 0:TG * 3 * H].rearrange("p (t h) -> p t h", t=TG)[:, :, 2 * H:3 * H]
                nc_p.tensor_tensor(vs[:, T(g), :].rearrange("p t (h d) -> p t h d", d=HD),
                                   qkv[:, T(g), 2 * D:3 * D].rearrange("p t (h d) -> p t h d", d=HD),
                                   c.unsqueeze(3).broadcast_to([P, TG, H, HD]), ALU.mult).then_inc(s["v_ready"][g], 1)

            def expand_v(g):
                vd = vexp[:, g].rearrange("p r n w -> p (r n) w")
                p.wait_ge(vrep_in[g], 16 * HG)
                nc_p.tensor_tensor(vd[:, :, 0:HG * HD].rearrange("p n (h d) -> p n h d", d=HD),
                                   vrep[:, g].rearrange("p r (n h d) -> p (r n) h d", h=HG, d=HD),
                                   vm.unsqueeze(1).broadcast_to([P, n, HG]).unsqueeze(3).broadcast_to([P, n, HG, HD]),
                                   ALU.mult).then_inc(s["vexp_ready"][g], 1)

            def split_up(e):
                p.wait_ge(w_in[e], 32)
                nc_p.tensor_copy(whi[:, e, :], wup[e]).then_inc(s["pool_step"], 1)
                p.wait_ge(s["pool_step"], e + 1)
                nc_p.tensor_tensor(wlo[:, e, :], wup[e], whi[:, e, :].bitcast(f32), ALU.subtract).then_inc(s["split"], 1)

            def pair_squares(g):
                p.wait_ge(s["hsq_ready"][g], 2)
                nc_p.tensor_tensor(hsq[:, g, 0, :], hsq[:, g, 0, :], hsq[:, g, 1, :], ALU.add).then_inc(s["hpair_ready"][g], 1)

            def add_x(g):
                for i, t in enumerate(tiles(g)[1::2]):
                    p.wait_ge(s["xtmp_mid"][g], TG + i + 1)
                    nc_p.tensor_tensor(tmp[:, t, :], tmp[:, t, :], xin[:, t, :], ALU.add).then_inc(s["xtmp_odd"][g], 1)

            start(0)
            clamp_v(0)
            clamp_v(1)
            expand_v(0)
            expand_v(1)
            ones_row(0)
            ones_row(1)
            split_up(0)
            split_up(1)
            split_up(2)
            split_up(3)
            split_up(4)
            pair_squares(0)
            add_x(0)
            pair_squares(1)
            add_x(1)

        @block.tensor
        def _(pe):
            mm, tr = nc_t.matmul, nc_t.transpose

            def ada(_):
                cond = col[:, K_COND:K_COND + B]
                pe.wait_ge(s["consts_in"], 32)
                pe.wait_ge(s["wada_in"], 16)
                for j, c in enumerate((0, 1, 3, 4)):
                    last = mm(bank[0][:, j * B:(j + 1) * B], wada[:, c * D:(c + 1) * D], cond, start=True, stop=True)
                last.then_inc(s["ada_mm"], 1)
                for i, c in enumerate((2, 5)):
                    last = mm(bank[4][0:B, i * D:(i + 1) * D], cond, wada[:, c * D:(c + 1) * D], start=True, stop=True)
                last.then_inc(s["ada_mm"], 1)

            def gains(g):
                pe.wait_ge(s["adag_ready"], 1)
                pe.wait_ge(s["sels_in"], 16)
                for i, t in enumerate(tiles(g)):
                    last = mm(bk(g, 2 + i // 2)[:, i % 2 * 2 * D:(i % 2 + 1) * 2 * D],
                              sel[:, S_SEL + t * P:S_SEL + (t + 1) * P], adag[:], start=True, stop=True)
                    if i % 2:
                        last.then_inc(s["gain_mm"], 1)

            def transpose_group(dst, src, g):
                for i, t in enumerate(tiles(g)):
                    last = tr(dst[:, i * P:(i + 1) * P], src[:, t, :], ident)
                last.then_inc(s["trans_mm"][g], 1)

            def norm_rows(g, j):
                pe.wait_ge(s["ones_ready"], 1)
                pe.wait_ge(s["ysq_ready"][g], j + 1)
                if j == 1:
                    pe.wait_ge(s["silu_ready"], 1)
                    mm(bk(g, 1)[0:GB, 8:8 + 2 * E], silu[:, g * GB:(g + 1) * GB], col[:, K_TW:K_TW + 2 * E],
                       start=True, stop=True)
                for i in range(TG):
                    last = mm(bk(g, 1)[:, i:i + 1], ysq[:, g, i * P:(i + 1) * P], ones[:], start=True, stop=True)
                last.then_inc(s["yss_mm"][g], 1)

            def xn_transposed(g, j):
                pe.wait_ge(s["xn_even"][g], (j + 1) * TG // 2)
                pe.wait_ge(s["xn_odd"][g], (j + 1) * TG // 2)
                if j == 0:
                    if g == 0:
                        pe.wait_ge(s["adaT_ready"], 4)
                    else:
                        pe.wait_ge(s["adag_ready"], 1)
                transpose_group(bk(g, 0), xn, g)

            def project(g):
                pe.wait_ge(s["wqkv_in"], 16)
                pe.wait_ge(s["gain_ready"], 2 * (g + 1))
                pe.wait_ge(s["funcs"][g], nth(FUNCS, "y0"))
                for t in range(TG):
                    mm(bk(g, (t + 2) % 4)[:, 0:3 * D], yT[:, g, t * P:(t + 1) * P], wqkv[:],
                       start=True, stop=True).then_inc(s["qkv_mm"][g], 1)

            def transpose_qk(g):
                pe.wait_ge(s["qk_ready"][g], 1)
                for half in range(2):
                    transpose_group(bk(g, half), qk[:, :, half * D:(half + 1) * D], g)

            def scores(g):
                pe.wait_ge(s["qT_ready"][g], 1)
                pe.wait_ge(s["kexp_ready"][g], 1)
                for r in range(TG * BT):
                    t, b = divmod(r, BT)
                    for n in range(NHG):
                        last = mm(bk(g, n)[b * S:(b + 1) * S, t * P:(t + 1) * P],
                                  qT[n * 32:(n + 1) * 32, g, r * S:(r + 1) * S],
                                  kexp[n * 32:(n + 1) * 32, g, r].rearrange("p h s -> p (h s)"), start=True, stop=True)
                last.then_inc(s["sc_mm"][g], 1)

            def transpose_probs(g):
                for n in range(NHG):
                    pe.wait_ge(s["p_ready"][g], n + 1)
                    for t in range(TG):
                        last = tr(bk(g, n)[:, t * P:(t + 1) * P], prob[:, g, n, t * P:(t + 1) * P], ident)
                    last.then_inc(s["pT_mm"][g], 1)

            def weigh_v(g):
                pe.wait_ge(s["pT_even"][g], 2)
                pe.wait_ge(s["pT_odd"][g], 2)
                pe.wait_ge(s["vexp_ready"][g], 1)
                for t in range(TG):
                    for n in range(NHG):
                        c = ((t % 2) * NHG + n) * VW
                        for b in range(BT):
                            last = mm(bk(g, t // 2)[b * S:(b + 1) * S, c:c + VW],
                                      probT[:, g, n, t * P + b * S:t * P + (b + 1) * S],
                                      vexp[:, g, t * BT + b, n, :], start=True, stop=True)
                last.then_inc(s["o_mm"][g], 1)

            def transpose_ain(g):
                pe.wait_ge(s["ain_ready"][g], 1)
                transpose_group(bk(g, 2), ain, g)

            def project_out(g):
                pe.wait_ge(s["wmlp_in"], 64)
                pe.wait_ge(s["ainT_ready"][g], 1)
                for t in range(TG):
                    last = mm(bk(g, 3)[:, t * D:(t + 1) * D], ainT[:, g, t * P:(t + 1) * P], wo[:], start=True, stop=True)
                last.then_inc(s["ap_mm"][g], 1)

            def hidden(g):
                pe.wait_ge(s["yT_ready"][g], 2)
                for i, c in enumerate(UPB):
                    if i == 2:
                        pe.wait_ge(s["rs_ready"][g], 1)
                        for t in range(TG):
                            tt = g * TG + t
                            last = mm(bk(g, 2)[:, t * P:(t + 1) * P], st[:, 1, 18, tt:tt + 1].broadcast_to([P, P]), ident,
                                      start=True, stop=True)
                        last.then_inc(s["rsb_mm"][g], 1)
                        pe.wait_ge(s["rsb_ready"][g], 1)
                    if c == 1:
                        pe.wait_ge(s["mod_ready"][g], 1)
                    mm(bk(g, c)[:, :], wf1[:, i * P:(i + 1) * P], yT[:, g, :], start=True, stop=True) \
                        .then_inc(s["up_mm"][g], 1)

            def hidden_norms(g):
                pe.wait_ge(s["hsum_ready"][g], 1)
                for t in range(TG):
                    last = mm(bk(g, 1)[:, t:t + 1], hsq[:, g, 0, t * P:(t + 1) * P], ones[:], start=True, stop=True)
                last.then_inc(s["hss_mm"][g], 1)

            def mlp_out(g):
                pe.wait_ge(s["hf_ready"][g], FC)
                for t in range(TG):
                    for c in range(FC):
                        last = mm(bk(g, 0)[:, t * D:(t + 1) * D], hf[:, g, c, t * P:(t + 1) * P], wf2[:, c, :],
                                  start=c == 0, stop=c == FC - 1)
                last.then_inc(s["f_mm"][g], 1)

            def transpose_x3(g):
                pe.wait_ge(s["x3_ready"][g], TG)
                transpose_group(bk(g, 3), x3, g)

            def gate(g):
                pe.wait_ge(s["agg_ready"][g], 1)
                for j in range(3):
                    last = mm(bk(g, 3)[0:GB, 0:E], agg[:, g, j, :], col[:, K_GW + j * E:K_GW + (j + 1) * E],
                              start=j == 0, stop=j == 2)
                last.then_inc(s["gate_mm"][g], 1)

            def token_weights(g):
                pe.wait_ge(s["w_ready"][g], 1)
                for t in range(TG):
                    last = mm(bk(g, 3)[:, 8 + E * t:8 + E * (t + 1)], sel[0:GB, S_SEL + t * P:S_SEL + (t + 1) * P],
                              gl[:, g, 5, :], start=True, stop=True)
                last.then_inc(s["gate_mm"][g], 1)
                bank_read(g, WT_SEQ)
                mm(bk(g, WT_SEQ % 3)[0:E, :], gl[:, g, 5, :], sel[0:GB, S_SEL:S_SEL + GT],
                   start=True, stop=True).then_inc(s["gate_mm"][g], 1)

            def bank_read(g, k):
                r = k - 3
                if r == WT_SEQ:
                    pe.wait_ge(s["wT_ready"][g], 1)
                elif r >= 0:
                    pe.wait_ge(s["moe_h"][g], r + 1 - (r > WT_SEQ))

            def up(g, e):
                pe.wait_ge(s["x3lo_ready"][g], 1)
                pe.wait_ge(s["split"], e + 1)
                lo, hi, xlo, xhi = wlo[:, e, :], whi[:, e, :], x3lo[:, g, :], x3hi[:, g, :]
                for c in range(FC):
                    k = chunk_seq(e, c)
                    bank_read(g, k)
                    z = bk(g, k % 3)[:, :]
                    mm(z, hi[:, c * P:(c + 1) * P], xhi, start=True, stop=False)
                    mm(z, lo[:, c * P:(c + 1) * P], xhi, start=False, stop=False)
                    mm(z, hi[:, c * P:(c + 1) * P], xlo, start=False, stop=True).then_inc(s["moe_up"][g], 1)

            def down(g, e):
                pe.wait_ge(s["moe_h"][g], FC * (e + 1))
                pe.wait_ge(w_in[e], 32)
                if e == 0:
                    pe.wait_ge(s["wtok_ready"][g], 1)
                else:
                    pe.wait_ge(s["moe_acc"][g], e)
                if e == E:
                    pe.wait_ge(s["wT_ready"][g], 1)
                for t in range(TG):
                    d = bk(g, 3)[:, t * D:(t + 1) * D]
                    if e == E:
                        mm(d, wT[:, g, t * P:(t + 1) * P], bdn[:], start=True, stop=False)
                    for c in range(FC):
                        last = mm(d, hT[e % 2][:, g, c, t * P:(t + 1) * P], wdn[e][:, c, :],
                                  start=c == 0 and e < E, stop=c == FC - 1)
                last.then_inc(s["moe_y"][g], 1)

            def xn_transposed0(g): xn_transposed(g, 0)
            def norm_rows0(g): norm_rows(g, 0)
            def xn_transposed1(g): xn_transposed(g, 1)
            def norm_rows1(g): norm_rows(g, 1)
            def up0(g): up(g, 0)
            def up1(g): up(g, 1)
            def up2(g): up(g, 2)
            def up3(g): up(g, 3)
            def up4(g): up(g, 4)
            def down0(g): down(g, 0)
            def down1(g): down(g, 1)
            def down2(g): down(g, 2)
            def down3(g): down(g, 3)
            def down4(g): down(g, 4)

            ada(0)
            gains(0)
            gains(1)
            xn_transposed0(0)
            norm_rows0(0)
            xn_transposed0(1)
            project(0)
            norm_rows0(1)
            project(1)
            transpose_qk(0)
            scores(0)
            transpose_qk(1)
            transpose_probs(0)
            weigh_v(0)
            transpose_ain(0)
            project_out(0)
            scores(1)
            transpose_probs(1)
            weigh_v(1)
            xn_transposed1(0)
            norm_rows1(0)
            transpose_ain(1)
            project_out(1)
            hidden(0)
            hidden_norms(0)
            mlp_out(0)
            xn_transposed1(1)
            norm_rows1(1)
            hidden(1)
            transpose_x3(0)
            hidden_norms(1)
            gate(0)
            up0(0)
            up1(0)
            token_weights(0)
            mlp_out(1)
            down0(0)
            up2(0)
            down1(0)
            transpose_x3(1)
            up3(0)
            down2(0)
            gate(1)
            up0(1)
            up1(1)
            token_weights(1)
            up4(0)
            down0(1)
            down3(0)
            up2(1)
            down1(1)
            up3(1)
            down2(1)
            up4(1)
            down3(1)
            down4(0)
            down4(1)


_OUT = (B, S, D)


def _constants(np):
    c = np.zeros((P, C_END), np.float32)
    i = np.arange(P)
    c[:, C_ID:C_ID + P] = np.eye(P)
    c[:, C_HM:C_HM + HG] = (i[:, None] // HD) % HG == np.arange(HG)
    c[:, C_VM:C_VM + HG] = i[:, None] // S == np.arange(HG)
    keep = np.ones((S, E))
    keep[SEG:2 * SEG, 1] = 0
    keep[0:SEG, 2] = 0
    c[:, C_WM:C_WM + E] = np.tile(keep, (BT, 1))
    c[:, C_TRI:C_TRI + E * E] = np.tril(np.ones((E, E)), -1).reshape(1, -1)
    c[:, C_TINY] = TINY
    m = np.zeros((B, S_END), np.float32)
    m[:, S_SEL:S_SEL + B * S] = np.arange(B * S)[None, :] // S == np.arange(B)[:, None]
    m[0:E, S_MT:S_MT + GT] = np.tile(keep, (GB, 1)).T
    return c, m


def kernel(**inputs):
    import numpy as np
    import concourse.bacc as bacc
    from concourse.bass_utils import run_bass_kernel_spmd

    a = {k: np.asarray(v) for k, v in inputs.items()}
    L0 = lambda n: a["L0_cond_" + n]
    L1 = lambda n: a["L1_cond_" + n]
    chunks = lambda w: np.ascontiguousarray(w.reshape(FC, P, D).transpose(1, 0, 2).reshape(P, FC * D))
    bada = L0("b_ada").reshape(6, D)
    eb1 = np.concatenate([L1("eb1"), L1("sb1")[None]]).reshape((E + 1) * FC, P)
    consts, sels = _constants(np)
    arrays = {
        "x": a["x"].reshape(TILES, P, D),
        "consts": consts,
        "sels": sels,
        "cols": np.concatenate([a["cond_1024"].T, bada[[0, 1, 3, 4]].T, L0("b_f1").reshape(FC, P).T, eb1.T,
                                L1("gate_w").reshape(3, D, E).transpose(1, 0, 2).reshape(D, 3 * E), L1("time_w")], axis=1),
        "rows": np.concatenate([L0("b_q"), L0("b_k"), L0("b_v"), L0("b_o"), L0("b_f2"), bada[2], bada[5],
                                L1("gate_b"), L1("time_b")])[None],
        "w_ada": L0("w_ada"),
        "w_qkv": np.concatenate([L0("w_q"), L0("w_k"), L0("w_v")], axis=1),
        "w_o": L0("w_o"),
        "w_f1": L0("w_f1"),
        "w_f2": chunks(L0("w_f2")),
        "w_up": np.concatenate([L1("ew1"), L1("sw1")[None]]),
        "w_down": np.stack([chunks(w) for w in [*L1("ew2"), L1("sw2")]]),
        "b_down": np.concatenate([L1("eb2"), L1("sb2")[None]]),
    }
    nc = bacc.Bacc("TRN2", target_bir_lowering=False, num_devices=1)
    aps = []
    for name in arrays:
        arrays[name] = np.ascontiguousarray(arrays[name])
        aps.append(nc.dram_tensor(name, arrays[name].shape, mybir.dt.from_np(arrays[name].dtype),
                                  kind="ExternalInput").ap())
    out = nc.dram_tensor("out", (TILES, P, D), mybir.dt.float32, kind="ExternalOutput").ap()
    cond_resid_kernel(nc, *aps, out)
    r = run_bass_kernel_spmd(nc, [arrays], core_ids=[0])
    return r.results[0]["out"].reshape(_OUT)
```

```python
import math

import concourse.bass as bass
from concourse import mybir
from contextlib import ExitStack

B, S, D = 32, 32, 128
H, HD, FF = 16, 8, 512
E = 4
P = 128
TILES = B * S // P
BT = P // S
NG = 2
TG = TILES // NG
GT = TG * P
GB = B // NG
HG = 4
NHG = H // HG
FC = FF // P
VW = HG * HD + HG
SEG = 10
TAIL = S - 2 * SEG

C_ID, C_HM, C_VM, C_WM, C_TRI, C_TINY, C_END = 0, 128, 132, 136, 140, 156, 157
S_SEL, S_END = 0, 512
K_COND, K_BADA, K_BF1, K_EB1, K_GW, K_TW = 0, 32, 36, 40, 60, 72
K_END = 80
R_QKV, R_BO, R_BF2, R_BG, R_GB, R_TB, R_B2 = 0, 384, 512, 640, 896, 900, 908
R_END = 908 + (E + 1) * D


def _beta(a, b):
    return math.exp(math.lgamma(a) + math.lgamma(b) - math.lgamma(a + b))


RATIO = _beta(HD / 2, 0.5) / _beta(D / 2, 0.5)
MAX_ARG = 0.9999899864196777
A = math.atanh(MAX_ARG)
TINY = 1e-30
EPS = 1e-7


def cond_resid_kernel(nc, x, consts, sels, cols, rows, w_ada, w_qkv, w_o, w_f1, w_f2, w_up, w_down, out):
    f32 = mybir.dt.float32
    u32 = mybir.dt.uint32
    f32r = mybir.dt.float32r
    ALU = mybir.AluOpType
    ACT = mybir.ActivationFunctionType
    X = mybir.AxisListType.X

    ctx = ExitStack()
    with ctx:
        def sb(name, shape, dt=f32):
            return ctx.enter_context(nc.sbuf_tensor(name, shape, dt))

        def sem(name):
            return ctx.enter_context(nc.semaphore(name))

        cst = sb("cst", [P, C_END])
        sel = sb("sel", [GB, S_END])
        col = sb("col", [P, K_END])
        row = sb("row", [P, R_END])
        wqkv = sb("wqkv", [P, 3 * D])
        wo = sb("wo", [P, D])
        wf1 = sb("wf1", [P, FF])
        wf2 = sb("wf2", [P, FC, D])
        wdn0 = sb("wdn0", [P, FC, D])
        whi = sb("whi", [P, E + 1, FF], f32r)
        wlo = sb("wlo", [P, E + 1, FF], f32r)
        ident = cst[:, C_ID:C_ID + P]
        ones = sb("ones", [P, 1])
        half = sb("half", [P, 1])
        adaT = sb("adaT", [P, 4, B])
        adag = sb("adag", [B, 2 * D])
        gain = sb("gain", [P, TILES, 2 * D])
        silu = sb("silu", [P, B])
        mod = sb("mod", [GB, NG, 2 * E])
        xin = sb("xin", [P, TILES, D])
        x1 = sb("x1", [P, TILES, D])
        xn = sb("xn", [P, TILES, D])
        x3 = xn
        yT = sb("yT", [P, NG, GT])
        ysq = sb("ysq", [P, NG, GT])
        qkv = sb("qkv", [P, TILES, 3 * D])
        qk = sb("qk", [P, TILES, 2 * D])
        vs = sb("vs", [P, TILES, D])
        vrep = sb("vrep", [P, NG, TG * BT, D])
        qsq = [vrep[:, g].rearrange("p r d -> p (r d)")[:, 0:TG * 3 * D] for g in range(NG)]
        vexp = sb("vexp", [P, NG, TG * BT, NHG, VW])
        qT = sb("qT", [P, NG, GT])
        kexp = sb("kexp", [P, NG, TG * BT, HG, S])
        prob = sb("prob", [P, NG, NHG, GT])
        wada = prob[:, 1].rearrange("p n t -> p (n t)")[:, 0:6 * D]
        probT = sb("probT", [P, NG, NHG, GT])
        o = sb("o", [P, TILES, NHG, VW])
        osq = xn
        ain = ysq[:].rearrange("p g (t d) -> p (g t) d", d=D)
        ainT = sb("ainT", [P, NG, GT])
        ap, gt, tmp = (qkv[:, :, i * D:(i + 1) * D] for i in range(3))
        rsb = ainT
        hf = prob
        hsq = kexp[:].rearrange("p g r h s -> p g (r h s)").rearrange("p g (c t) -> p g c t", c=FC)
        hT = (probT, prob)
        x3hi = sb("x3hi", [P, NG, GT], f32r)
        x3lo = sb("x3lo", [P, NG, GT], f32r)
        bst = sb("bst", [P, 2, TILES, 6])
        mv = sb("mv", [P, 2, TILES, 2])
        st = sb("st", [P, 2, 24, TILES])
        heads = sb("heads", [P, NG, 4, 204])
        onrm = sb("onrm", [P, 4, TILES])
        seg = sb("seg", [P, NG, 3, GB])
        agg = sb("agg", [P, NG, 3, GB])
        gl = sb("gl", [GB, NG, 6, E])
        gp = sb("gp", [GB, NG, 2, E * E])
        gs = sb("gs", [GB, NG, 5])
        wtok = sb("wtok", [P, E, TILES])
        bacc = ain

        bank = [ctx.enter_context(nc.psum_tensor(f"bank{i}", [P, 512], f32)) for i in range(8)]

        gain_dram = nc.dram_tensor("gain_dram", (B, 2 * D), f32, kind="Internal").ap()
        v_dram = nc.dram_tensor("v_dram", (NG, P, TG, D), f32, kind="Internal").ap()

        both = """trans_mm xn_even xn_odd vals funcs rms_ready yT_ready ysq_ready yss_mm
        qkv_mm qkv_ready qsq_ready c_ready v_ready vexp_ready qk_ready qT_ready kexp_ready sc_mm p_ready
        pT_mm pT_even pT_odd o_mm o_ready osq_ready ain_ready ainT_ready ap_mm ap_ready gt_ready sq_done
        xtmp_mid xtmp_even xtmp_odd x1_ready x3_ready rs_ready rsb_mm rsb_ready up_mm hf_ready
        hsq_ready hpair_ready hsum_ready hss_mm f_mm x3hi_ready x3lo_ready agg_ready mod_ready gate_mm
        w_ready wtok_ready bias_ready moe_up moe_h moe_y moe_acc v_out""".split()
        s = {n: [sem(f"{n}{g}") for g in range(NG)] for n in both}
        once = """consts_in wada_in sels_in rows_in wqkv_in wmlp_in ones_ready ada_mm adaT_ready adag_ready
        gain_out gain_in silu_e silu_ready split stored vec_step pool_step""".split()
        s.update({n: sem(n) for n in once})
        x_in = [sem(f"x_in{g}") for g in range(NG)]
        vrep_in = [sem(f"vrep_in{g}") for g in range(NG)]
        w_in = [sem(f"w_in{e}") for e in range(E + 1)]

        TRANS = "xnT0 qT kT ainT xnT1 x3T".split()
        VALS = "mean0 m0 var0 nb0 head out tok n0 beta0 mean1 m1 var1 nb1 n1 beta1 logit".split()
        FUNCS = "ln0 rstd0 y0 head out tok a0 th0 ln1 rstd1 y1 h a1 th1 gexp".split()
        GATES = "logit token".split()

        def nth(names, name):
            return names.index(name) + 1

        nc_v, nc_a, nc_t, nc_p = nc.vector, nc.scalar, nc.tensor, nc.gpsimd

        def T(g):
            return slice(g * TG, (g + 1) * TG)

        def tiles(g):
            return range(g * TG, (g + 1) * TG)

        def bk(g, i):
            return bank[4 * g + i]

        BANKS = [0, 2, 3, 1]
        UPB = [3, 0, 1, 2]

        LAST = [3, 0]

        def half_tiles(g, i):
            return slice(g * TG + i * TG // 2, g * TG + (i + 1) * TG // 2)

        def oo(g, i):
            return heads[:, g].rearrange("p i w -> p (i w)")[:, i * TG * H:(i + 1) * TG * H]

        vslot = lambda i: vrep[:, i // 4].rearrange("p r d -> p (r d)")[:, (i % 4) * FF:(i % 4 + 1) * FF]
        wup = [vslot(i) for i in range(E + 1)]
        vflat = vexp[:, 0].rearrange("p r n w -> p (r n w)")
        wdn = [wdn0[:]] + [vflat[:, i * FF:(i + 1) * FF].rearrange("p (c d) -> p c d", c=FC) for i in range(E)]

        block = ctx.enter_context(nc.Block())

        @block.sync
        def _(sp):
            for g in range(NG):
                sp.dma_start(xin[:, T(g), :], x[T(g)].rearrange("t p d -> p t d")).then_inc(x_in[g], 16)
            sp.dma_start(row[:], rows.broadcast_to([P, R_END])).then_inc(s["rows_in"], 16)
            sp.dma_start(wqkv[:], w_qkv).then_inc(s["wqkv_in"], 16)
            sp.dma_start(wo[:], w_o).then_inc(s["wmlp_in"], 16)
            sp.dma_start(wf1[:], w_f1).then_inc(s["wmlp_in"], 16)
            sp.dma_start(wf2[:], w_f2.rearrange("p (c d) -> p c d", c=FC)).then_inc(s["wmlp_in"], 16)

            def load_up(e):
                sp.dma_start(wup[e], w_up[e]).then_inc(w_in[e], 16)

            def load_down(e):
                sp.dma_start(wdn[e], w_down[e].rearrange("p (c d) -> p c d", c=FC)).then_inc(w_in[e], 16)

            load_down(0)
            sp.wait_ge(s["adag_ready"], 1)
            sp.dma_start(gain_dram, adag[:]).then_inc(s["gain_out"], 16)
            sp.wait_ge(s["gain_out"], 16)
            for b in range(BT):
                sp.dma_start(gain[b * S:(b + 1) * S, :, :],
                             gain_dram.rearrange("(t b) d -> b t d", b=BT)[b:b + 1].broadcast_to([S, TILES, 2 * D])) \
                    .then_inc(s["gain_in"], 16)
            for g in range(NG):
                sp.wait_ge(s["v_ready"][g], 1)
                sp.dma_start(v_dram[g], vs[:, T(g), :]).then_inc(s["v_out"][g], 16)
                sp.wait_ge(s["v_out"][g], 16)
                for h in range(HG):
                    sp.dma_start(vrep[h * S:(h + 1) * S, g, :, :].rearrange("s (t b) d -> s t b d", b=BT),
                                 v_dram[g].rearrange("(b s) t d -> s t b d", b=BT)).then_inc(vrep_in[g], 16)
            sp.wait_ge(s["vexp_ready"][0], 1)
            for e in range(E):
                load_up(e)
            sp.wait_ge(s["o_mm"][0], 1)
            for e in range(1, E + 1):
                load_down(e)
            sp.wait_ge(s["vexp_ready"][1], 1)
            load_up(E)
            for g in range(NG):
                for i in range(2):
                    sp.wait_ge(s["moe_acc"][g], E + 2 + i)
                    sp.dma_start(out[half_tiles(g, i)].rearrange("t p d -> p t d"),
                                 x3[:, half_tiles(g, i), :]).then_inc(s["stored"], 16)
            sp.wait_ge(s["stored"], 16 * 2 * NG)

        @block.vector
        def _(v):
            steps = [0]

            def step(ins):
                ins.then_inc(s["vec_step"], 1)
                steps[0] += 1

            def settle():
                v.wait_ge(s["vec_step"], steps[0])

            def link(ins):
                step(ins)
                settle()

            def once_ones():
                nc_v.memset(ones[:], 1.0).then_inc(s["ones_ready"], 1)
                v.wait_ge(s["consts_in"], 32)

            def adaT_out():
                v.wait_ge(s["ada_mm"], 1)
                for j in range(4):
                    nc_v.tensor_scalar(adaT[:, j, :], bank[0][:, j * B:(j + 1) * B],
                                       col[:, K_BADA + j:K_BADA + j + 1], float(j % 2), ALU.add,
                                       ALU.add).then_inc(s["adaT_ready"], 1)

            def adag_out():
                v.wait_ge(s["rows_in"], 16)
                v.wait_ge(s["ada_mm"], 2)
                nc_v.tensor_tensor(adag[:], bank[4][0:B, 0:2 * D], row[0:B, R_BG:R_BG + 2 * D],
                                   ALU.add).then_inc(s["adag_ready"], 1)

            def silu_out():
                v.wait_ge(s["silu_e"], 1)
                link(nc_v.tensor_scalar(silu[:], silu[:], 1.0, None, ALU.add))
                link(nc_v.reciprocal(silu[:], silu[:]))
                nc_v.tensor_tensor(silu[:], silu[:], col[:, K_COND:K_COND + B], ALU.mult).then_inc(s["silu_ready"], 1)

            def stats(g, j, src):
                for t in tiles(g):
                    step(nc_v.bn_stats(bst[:, j, t, :], src[:, t, :]))

            def mean_square(g, j):
                q = lambda i: st[:, j, i, T(g)]
                settle()
                for t in tiles(g):
                    step(nc_v.bn_aggr(mv[:, j, t, :], bst[:, j, t, :]))
                settle()
                link(nc_v.tensor_tensor(q(0), mv[:, j, T(g), 0], mv[:, j, T(g), 0], ALU.mult))
                nc_v.scalar_tensor_tensor(q(1), q(0), TINY, mv[:, j, T(g), 1], ALU.add, ALU.add) \
                    .then_inc(s["vals"][g], 1)

            def log_small(g, j):
                q = lambda i: st[:, j, i, T(g)]
                v.wait_ge(s["rms_ready"][g], j + 1)
                nc_v.tensor_scalar(q(3), q(2), D ** 0.5, MAX_ARG, ALU.mult, ALU.min).then_inc(s["vals"][g], 1)
                link(nc_v.reciprocal(q(4), q(2)))
                v.wait_ge(s["vals"][g], nth(VALS, f"m{j}"))
                link(nc_v.tensor_tensor(q(5), q(3), q(3), ALU.mult))
                link(nc_v.tensor_scalar(q(6), q(5), 1.0 / 5, 1.0 / 3, ALU.mult, ALU.add))
                link(nc_v.tensor_tensor(q(6), q(6), q(5), ALU.mult))
                step(nc_v.tensor_scalar(q(6), q(6), 1.0, None, ALU.add))
                step(nc_v.tensor_scalar(q(7), q(3), 0.05, None, ALU.is_lt))

            def log_factor(g, j):
                q = lambda i: st[:, j, i, T(g)]
                v.wait_ge(s["funcs"][g], nth(FUNCS, f"ln{j}"))
                link(nc_v.tensor_tensor(q(10), q(8), q(9), ALU.subtract))
                link(nc_v.scalar_tensor_tensor(q(11), q(10), 0.5 * D ** -0.5, q(4), ALU.mult, ALU.mult))
                link(nc_v.copy_predicated(q(11), q(7).bitcast(u32), q(6)))
                link(nc_v.reciprocal(q(12), q(11)))
                link(nc_v.tensor_tensor(q(12), q(12), q(12), ALU.mult))
                nc_v.scalar_tensor_tensor(q(13), q(12), 1e-6, mv[:, j, T(g), 1], ALU.mult,
                                          ALU.add).then_inc(s["vals"][g], 1)

            def normalise(g, j, src):
                q = lambda i: st[:, j, i, T(g)]
                v.wait_ge(s["funcs"][g], nth(FUNCS, f"rstd{j}"))
                link(nc_v.reciprocal(q(15), q(14)))
                nc_v.scalar_tensor_tensor(q(16), mv[:, j, T(g), 0], -1.0, q(15), ALU.mult,
                                          ALU.mult).then_inc(s["vals"][g], 1)
                for t in tiles(g)[::2]:
                    nc_v.tensor_scalar(xn[:, t, :], src[:, t, :], mv[:, j, t, 0:1], st[:, j, 15, t:t + 1],
                                       ALU.subtract, ALU.mult).then_inc(s["xn_even"][g], 1)

            def modulate(g, j):
                v.wait_ge(s["trans_mm"][g], nth(TRANS, f"xnT{j}"))
                v.wait_ge(s["adaT_ready"], 4)
                b0 = g * GB
                y3 = yT[:, g, :].rearrange("p (b s) -> p b s", s=S)
                sc = adaT[:, 2 * j + 1, b0:b0 + GB].unsqueeze(2).broadcast_to([P, GB, S])
                sh = adaT[:, 2 * j, b0:b0 + GB].unsqueeze(2).broadcast_to([P, GB, S])
                link(nc_v.tensor_tensor(y3, bk(g, 0)[:, :].rearrange("p (b s) -> p b s", s=S), sc, ALU.mult))
                nc_v.tensor_tensor(y3, y3, sh, ALU.add).then_inc(s["yT_ready"][g], 1)

            def clamp_y(g, j):
                q = lambda i: st[:, j, i, T(g)]
                v.wait_ge(s["funcs"][g], nth(FUNCS, f"y{j}"))
                if j == 1:
                    nc_v.tensor_scalar(q(18), q(0), 1.0 / A, 1.0, ALU.mult, ALU.max).then_inc(s["rs_ready"][g], 1)
                link(nc_v.reciprocal(q(17), q(0)))
                link(nc_v.tensor_scalar(q(17), q(17), A, 1.0, ALU.mult, ALU.min))

            n_hd = TG * 3 * H

            def project(g):
                v.wait_ge(s["rows_in"], 16)
                for i, t in enumerate(tiles(g)):
                    v.wait_ge(s["qkv_mm"][g], i + 1)
                    nc_v.scalar_tensor_tensor(qkv[:, t, :], bk(g, (i + 2) % 4)[:, 0:3 * D], st[:, 0, 17, t:t + 1],
                                              row[:, R_QKV:R_QKV + 3 * D], ALU.mult, ALU.add).then_inc(s["qkv_ready"][g], 1)

            def head_sums(g):
                v.wait_ge(s["qsq_ready"][g], TG)
                h0 = heads[:, g, 0, :]
                link(nc_v.tensor_reduce(h0[:, 0:n_hd], qsq[g].rearrange("p (h d) -> p h d", d=HD), X, ALU.add))
                nc_v.tensor_reduce(h0[:, n_hd:n_hd + 3 * TG], h0[:, 0:n_hd].rearrange("p (w h) -> p w h", h=H),
                                   X, ALU.add).then_inc(s["vals"][g], 1)

            def head_clamps(g):
                hh = lambda i: heads[:, g, i, :]
                v.wait_ge(s["funcs"][g], nth(FUNCS, "head"))
                link(nc_v.reciprocal(hh(2), hh(1)))
                link(nc_v.tensor_scalar(hh(3)[:, n_hd:n_hd + 3 * TG], hh(2)[:, n_hd:n_hd + 3 * TG], A * RATIO, RATIO,
                                        ALU.mult, ALU.min))
                w3 = lambda z: z[:, 0:n_hd].rearrange("p (w h) -> p w h", h=H)
                nc_v.scalar_tensor_tensor(w3(hh(3)), w3(hh(2)), A,
                                          hh(3)[:, n_hd:n_hd + 3 * TG].unsqueeze(2).broadcast_to([P, 3 * TG, H]),
                                          ALU.mult, ALU.min).then_inc(s["c_ready"][g], 1)
                v.wait_ge(s["c_ready"][g], 1)
                c4 = hh(3)[:, 0:n_hd].rearrange("p (t h) -> p t h", t=TG)[:, :, 0:2 * H]
                nc_v.tensor_tensor(qk[:, T(g), :].rearrange("p t (h d) -> p t h d", d=HD),
                                   qkv[:, T(g), 0:2 * D].rearrange("p t (h d) -> p t h d", d=HD),
                                   c4.unsqueeze(3).broadcast_to([P, TG, 2 * H, HD]), ALU.mult).then_inc(s["qk_ready"][g], 1)

            def expand_k(g):
                v.wait_ge(s["trans_mm"][g], nth(TRANS, "kT"))
                hm = cst[:, C_HM:C_HM + HG].unsqueeze(1).broadcast_to([P, BT, HG]).unsqueeze(3).broadcast_to([P, BT, HG, S])
                for i in range(TG):
                    kk = bk(g, 1)[:, i * P:(i + 1) * P].rearrange("p (r s) -> p r s", s=S).unsqueeze(2) \
                        .broadcast_to([P, BT, HG, S])
                    nc_v.tensor_tensor(kexp[:, g, i * BT:(i + 1) * BT], kk, hm, ALU.mult).then_inc(s["kexp_ready"][g], 1)

            def copy_probs(g):
                for k in (0, 2):
                    i = BANKS[k]
                    v.wait_ge(s["pT_mm"][g], k + 1)
                    nc_v.tensor_copy(probT[:, g, i, :], bk(g, i)[:, :]).then_inc(s["pT_even"][g], 1)

            def head_squares(g):
                ov = o[:, T(g)].rearrange("p t n w -> p (t n) w")
                v.wait_ge(s["o_ready"][g], 2)
                step(nc_v.reciprocal(oo(g, 0).rearrange("p (n h) -> p n h", h=HG), ov[:, :, HG * HD:VW]))
                v.wait_ge(s["osq_ready"][g], 1)
                nc_v.tensor_reduce(oo(g, 1), osq[:, T(g), :].rearrange("p t (h d) -> p (t h) d", d=HD), X,
                                   ALU.add).then_inc(s["vals"][g], 1)

            def heads_out(g):
                v.wait_ge(s["funcs"][g], nth(FUNCS, "out"))
                link(nc_v.reciprocal(oo(g, 3), oo(g, 2)))
                link(nc_v.scalar_tensor_tensor(oo(g, 3), oo(g, 3), A, oo(g, 0), ALU.mult, ALU.min))
                n = TG * NHG
                c = oo(g, 3).rearrange("p (n h) -> p n h", h=HG).unsqueeze(3).broadcast_to([P, n, HG, HD])
                nc_v.tensor_tensor(ain[:, T(g), :].rearrange("p t (n h d) -> p (t n) h d", h=HG, d=HD),
                                   o[:, T(g)].rearrange("p t n w -> p (t n) w")[:, :, 0:HG * HD]
                                   .rearrange("p n (h d) -> p n h d", d=HD), c, ALU.mult).then_inc(s["ain_ready"][g], 1)
                link(nc_v.tensor_tensor(oo(g, 4), oo(g, 3), oo(g, 3), ALU.mult))
                link(nc_v.tensor_tensor(oo(g, 4), oo(g, 4), oo(g, 1), ALU.mult))
                nc_v.tensor_reduce(onrm[:, 0, T(g)], oo(g, 4).rearrange("p (t h) -> p t h", t=TG), X,
                                   ALU.add).then_inc(s["vals"][g], 1)

            def token_clamp(g):
                v.wait_ge(s["funcs"][g], nth(FUNCS, "tok"))
                link(nc_v.reciprocal(onrm[:, 2, T(g)], onrm[:, 1, T(g)]))
                link(nc_v.tensor_scalar(onrm[:, 2, T(g)], onrm[:, 2, T(g)], A, 1.0 / RATIO, ALU.mult, ALU.min))

            def branch_out(g, j, bnk, mm_done, bias, res):
                n0 = j * TG

                def project_out(t):
                    nc_v.scalar_tensor_tensor(ap[:, t, :], bk(g, bnk)[:, (t % TG) * D:(t % TG + 1) * D],
                                              onrm[:, 2, t:t + 1], row[:, bias:bias + D],
                                              ALU.mult, ALU.add).then_inc(s["ap_ready"][g], 1)

                def gained(t, i):
                    v.wait_ge(s["ap_ready"][g], n0 + i + 1)
                    nc_v.tensor_tensor(gt[:, t, :], ap[:, t, :], gain[:, t, j * D:(j + 1) * D],
                                       ALU.mult).then_inc(s["gt_ready"][g], 1)

                def dot(t, i):
                    v.wait_ge(s["gt_ready"][g], n0 + i + 1)
                    step(nc_v.tensor_tensor_reduce(out=tmp[:, t, :], in0=res[:, t, :], in1=gt[:, t, :], scale=1.0,
                                                   scalar=0.0, op0=ALU.mult, op1=ALU.add, accum_out=st[:, j, 19, t:t + 1]))

                v.wait_ge(s[mm_done][g], 1)
                v.wait_ge(s["gain_in"], 16 * BT)
                for i in range(TG + 2):
                    t = g * TG + i
                    if i < TG:
                        project_out(t)
                    if 0 <= i - 1 < TG:
                        gained(t - 1, i - 1)
                    if 0 <= i - 2:
                        dot(t - 2, i - 2)
                q = lambda i: st[:, j, i, T(g)]
                link(nc_v.tensor_scalar(q(0), q(1), float(D), None, ALU.mult))
                step(nc_v.tensor_scalar(q(3), q(0), -1.0, 1.0, ALU.mult, ALU.add))

            def branch_norm(g, j):
                q = lambda i: st[:, j, i, T(g)]
                v.wait_ge(s["funcs"][g], nth(FUNCS, f"a{j}"))
                step(nc_v.reciprocal(q(22), q(20)))
                step(nc_v.reciprocal(q(23), q(21)))
                settle()
                link(nc_v.tensor_scalar(q(22), q(22), A, 1.0, ALU.mult, ALU.min))
                nc_v.tensor_tensor(q(20), q(22), q(21), ALU.mult).then_inc(s["vals"][g], 1)

            def mobius(g, j, res, dst):
                q = lambda i: st[:, j, i, T(g)]
                v.wait_ge(s["funcs"][g], nth(FUNCS, f"th{j}"))
                step(nc_v.tensor_tensor(q(4), q(22), q(23), ALU.mult))
                step(nc_v.tensor_tensor(q(5), q(22), q(22), ALU.mult))
                settle()
                step(nc_v.tensor_tensor(q(6), q(4), q(19), ALU.mult))
                step(nc_v.tensor_tensor(q(3), q(3), q(4), ALU.mult))
                step(nc_v.tensor_tensor(q(8), q(0), q(5), ALU.mult))
                settle()
                link(nc_v.tensor_scalar(q(6), q(6), 2.0, 1.0, ALU.mult, ALU.add))
                step(nc_v.tensor_tensor(q(8), q(6), q(8), ALU.add))
                step(nc_v.tensor_tensor(q(5), q(6), q(5), ALU.add))
                settle()
                link(nc_v.tensor_scalar(q(8), q(8), EPS, None, ALU.max))
                link(nc_v.reciprocal(q(8), q(8)))
                nc_v.tensor_tensor(q(3), q(3), q(8), ALU.mult).then_inc(s["vals"][g], 1)
                link(nc_v.tensor_tensor(q(5), q(5), q(8), ALU.mult))
                if j == 1:
                    for t in tiles(g)[::2]:
                        nc_v.scalar_tensor_tensor(tmp[:, t, :], gt[:, t, :], st[:, j, 3, t:t + 1], xin[:, t, :],
                                                  ALU.mult, ALU.add).then_inc(s["xtmp_even"][g], 1)
                for i in range(TG + 1):
                    t = g * TG + i
                    if i < TG:
                        if j == 0:
                            v.wait_ge(s["xtmp_mid"][g], i + 1)
                        elif i % 2:
                            v.wait_ge(s["xtmp_odd"][g], i // 2 + 1)
                        else:
                            v.wait_ge(s["xtmp_even"][g], i // 2 + 1)
                        nc_v.scalar_tensor_tensor(dst[:, t, :], res[:, t, :], st[:, j, 5, t:t + 1], tmp[:, t, :],
                                                  ALU.mult, ALU.add).then_inc(s["x3_ready" if j else "x1_ready"][g], 1)
                    if j == 0 and i:
                        v.wait_ge(s["x1_ready"][g], i)
                        step(nc_v.bn_stats(bst[:, 1, t - 1, :], x1[:, t - 1, :]))

            def hidden(g):
                v.wait_ge(s["rsb_ready"][g], 1)
                for i, c in enumerate(UPB):
                    v.wait_ge(s["up_mm"][g], i + 1)
                    nc_v.scalar_tensor_tensor(hf[:, g, i, :], rsb[:, g, :], col[:, K_BF1 + i:K_BF1 + i + 1], bk(g, c)[:, :],
                                              ALU.mult, ALU.add).then_inc(s["hf_ready"][g], 1)

            def sum_hidden(g):
                v.wait_ge(s["hsq_ready"][g], FC)
                step(nc_v.tensor_tensor(hsq[:, g, 2, :], hsq[:, g, 2, :], hsq[:, g, 3, :], ALU.add))
                v.wait_ge(s["hpair_ready"][g], 1)
                settle()
                nc_v.tensor_tensor(hsq[:, g, 0, :], hsq[:, g, 0, :], hsq[:, g, 2, :], ALU.add).then_inc(s["hsum_ready"][g], 1)

            def hidden_clamp(g):
                v.wait_ge(s["funcs"][g], nth(FUNCS, "h"))
                link(nc_v.reciprocal(onrm[:, 1, T(g)], onrm[:, 3, T(g)]))
                link(nc_v.scalar_tensor_tensor(onrm[:, 2, T(g)], onrm[:, 1, T(g)], A, st[:, 1, 17, T(g)], ALU.mult, ALU.min))

            def modulation(g):
                v.wait_ge(s["funcs"][g], nth(FUNCS, "y1"))
                link(nc_v.tensor_tensor(mod[:, g, :], bk(g, 1)[0:GB, 8:8 + 2 * E], row[0:GB, R_TB:R_TB + 2 * E], ALU.add))
                nc_v.tensor_scalar(mod[:, g, 0:E], mod[:, g, 0:E], 1.0, None, ALU.add).then_inc(s["mod_ready"][g], 1)

            def x3_low(g):
                v.wait_ge(s["x3hi_ready"][g], 1)
                nc_v.tensor_tensor(x3lo[:, g, :], bk(g, 3)[:, :], x3hi[:, g, :].bitcast(f32),
                                   ALU.subtract).then_inc(s["x3lo_ready"][g], 1)

            def gate_inputs(g):
                v.wait_ge(s["x3hi_ready"][g], 1)
                xt = bk(g, 3)[:, :].rearrange("p (b s) -> p b s", s=S)
                for i, (a, b) in enumerate(((0, SEG), (SEG, 2 * SEG), (2 * SEG, S))):
                    step(nc_v.tensor_reduce(seg[:, g, i, :], xt[:, :, a:b], X, ALU.add))
                settle()
                step(nc_v.tensor_tensor(agg[:, g, 1, :], seg[:, g, 0, :], seg[:, g, 2, :], ALU.add))
                step(nc_v.tensor_tensor(agg[:, g, 2, :], seg[:, g, 1, :], seg[:, g, 2, :], ALU.add))
                settle()
                link(nc_v.tensor_tensor(agg[:, g, 0, :], agg[:, g, 1, :], seg[:, g, 1, :], ALU.add))
                step(nc_v.tensor_scalar(agg[:, g, 0, :], agg[:, g, 0, :], 1.0 / S, None, ALU.mult))
                nc_v.tensor_scalar(agg[:, g, 1:3, :], agg[:, g, 1:3, :], 1.0 / (SEG + TAIL), None,
                                   ALU.mult).then_inc(s["agg_ready"][g], 1)

            def gate_logits(g):
                L = lambda i: gl[:, g, i, :]
                v.wait_ge(s["gate_mm"][g], nth(GATES, "logit"))
                v.wait_ge(s["mod_ready"][g], 1)
                link(nc_v.tensor_tensor(L(0), bk(g, 3)[0:GB, 0:E], row[0:GB, R_GB:R_GB + E], ALU.add))
                link(nc_v.tensor_tensor(L(0), L(0), mod[:, g, 0:E], ALU.mult))
                link(nc_v.tensor_tensor(L(0), L(0), mod[:, g, E:2 * E], ALU.add))
                nc_v.tensor_reduce(gs[:, g, 0:1], L(0), X, ALU.max, negate=True).then_inc(s["vals"][g], 1)

            def gate_weights(g):
                L = lambda i: gl[:, g, i, :]
                v.wait_ge(s["funcs"][g], nth(FUNCS, "gexp"))
                link(nc_v.tensor_reduce(gs[:, g, 1:2], L(1), X, ALU.add))
                link(nc_v.reciprocal(gs[:, g, 2:3], gs[:, g, 1:2]))
                link(nc_v.tensor_scalar(L(2), L(1), gs[:, g, 2:3], None, ALU.mult))
                pj = L(2).unsqueeze(1).broadcast_to([GB, E, E])
                pi = L(2).unsqueeze(2).broadcast_to([GB, E, E])
                m = lambda i: gp[:, g, i, :].rearrange("p (i j) -> p i j", i=E)
                step(nc_v.tensor_tensor(m(0), pj, pi, ALU.is_gt))
                step(nc_v.tensor_tensor(m(1), pj, pi, ALU.is_equal))
                settle()
                link(nc_v.tensor_tensor(m(1), m(1), cst[0:GB, C_TRI:C_TRI + E * E].rearrange("p (i j) -> p i j", i=E),
                                        ALU.mult))
                link(nc_v.tensor_tensor(m(0), m(0), m(1), ALU.add))
                link(nc_v.tensor_reduce(L(3), m(0), X, ALU.add))
                link(nc_v.scalar_tensor_tensor(L(4), L(3), 1.5, L(2), ALU.is_lt, ALU.mult))
                link(nc_v.tensor_reduce(gs[:, g, 3:4], L(4), X, ALU.add))
                link(nc_v.tensor_scalar(gs[:, g, 3:4], gs[:, g, 3:4], 1e-8, None, ALU.add))
                link(nc_v.reciprocal(gs[:, g, 4:5], gs[:, g, 3:4]))
                nc_v.tensor_scalar(L(5), L(4), gs[:, g, 4:5], None, ALU.mult).then_inc(s["w_ready"][g], 1)

            def token_weights(g):
                v.wait_ge(s["gate_mm"][g], nth(GATES, "token"))
                nc_v.tensor_tensor(wtok[:, :, T(g)].rearrange("p e t -> p t e"),
                                   bk(g, 3)[:, 8:8 + E * TG].rearrange("p (t e) -> p t e", e=E),
                                   cst[:, C_WM:C_WM + E].unsqueeze(1).broadcast_to([P, TG, E]),
                                   ALU.mult).then_inc(s["wtok_ready"][g], 1)

            def accumulate(g, e):
                v.wait_ge(s["moe_y"][g], e + 1)
                if e == 0:
                    v.wait_ge(s["wtok_ready"][g], 1)
                else:
                    v.wait_ge(s["moe_acc"][g], e + (e > 2))
                if e < E:
                    for i, t in enumerate(tiles(g)):
                        last = nc_v.scalar_tensor_tensor(x3[:, t, :], bk(g, 3)[:, i * D:(i + 1) * D],
                                                         wtok[:, e, t:t + 1], x3[:, t, :], ALU.mult, ALU.add)
                    last.then_inc(s["moe_acc"][g], 1)
                else:
                    for i, b in enumerate(LAST):
                        v.wait_ge(s["moe_y"][g], E + 1 + i)
                        h = x3[:, half_tiles(g, i), :].rearrange("p t d -> p (t d)")
                        nc_v.tensor_tensor(h, bk(g, b)[:, 0:GT // 2], h, ALU.add).then_inc(s["moe_acc"][g], 1)

            def accumulate_biases(g):
                v.wait_ge(s["bias_ready"][g], 2 * E)
                v.wait_ge(s["moe_acc"][g], 3)
                x3g = x3[:, T(g), :].rearrange("p t d -> p (t d)")
                nc_v.tensor_tensor(x3g, bacc[:, T(g), :].rearrange("p t d -> p (t d)"), x3g,
                                   ALU.add).then_inc(s["moe_acc"][g], 1)

            def x_stats(g):
                v.wait_ge(x_in[g], 16)
                stats(g, 0, xin)

            once_ones()
            x_stats(0)
            x_stats(1)
            mean_square(1, 0)
            mean_square(0, 0)
            log_small(1, 0)
            log_small(0, 0)
            adaT_out()
            log_factor(0, 0)
            adag_out()
            normalise(0, 0, xin)
            modulate(0, 0)
            log_factor(1, 0)
            normalise(1, 0, xin)
            clamp_y(0, 0)
            project(0)
            modulate(1, 0)
            head_sums(0)
            head_clamps(0)
            silu_out()
            clamp_y(1, 0)
            expand_k(0)
            project(1)
            head_sums(1)
            head_clamps(1)
            copy_probs(0)
            expand_k(1)
            head_squares(0)
            heads_out(0)
            token_clamp(0)
            branch_out(0, 0, 3, "ap_mm", R_BO, xin)
            branch_norm(0, 0)
            mobius(0, 0, xin, x1)
            mean_square(0, 1)
            log_small(0, 1)
            copy_probs(1)
            log_factor(0, 1)
            normalise(0, 1, x1)
            modulate(0, 1)
            head_squares(1)
            heads_out(1)
            clamp_y(0, 1)
            modulation(0)
            token_clamp(1)
            branch_out(1, 0, 3, "ap_mm", R_BO, xin)
            branch_norm(1, 0)
            hidden(0)
            mobius(1, 0, xin, x1)
            mean_square(1, 1)
            sum_hidden(0)
            log_small(1, 1)
            log_factor(1, 1)
            hidden_clamp(0)
            normalise(1, 1, x1)
            branch_out(0, 1, 0, "f_mm", R_BF2, x1)
            modulate(1, 1)
            branch_norm(0, 1)
            mobius(0, 1, x1, x3)
            clamp_y(1, 1)
            modulation(1)
            x3_low(0)
            gate_inputs(0)
            hidden(1)
            gate_logits(0)
            gate_weights(0)
            sum_hidden(1)
            token_weights(0)
            hidden_clamp(1)
            branch_out(1, 1, 0, "f_mm", R_BF2, x1)
            branch_norm(1, 1)
            accumulate(0, 0)
            accumulate(0, 1)
            mobius(1, 1, x1, x3)
            accumulate(0, 2)
            x3_low(1)
            gate_inputs(1)
            gate_logits(1)
            gate_weights(1)
            token_weights(1)
            accumulate(1, 0)
            accumulate(1, 1)
            accumulate(1, 2)
            accumulate_biases(1)
            accumulate_biases(0)
            accumulate(0, 3)
            accumulate(1, 3)
            accumulate(0, 4)
            accumulate(1, 4)

        @block.scalar
        def _(a):
            act = nc_a.activation
            tiny = cst[:, C_TINY:C_TINY + 1]

            def logs(g, j):
                q = lambda i: st[:, j, i, T(g)]
                a.wait_ge(s["vals"][g], nth(VALS, f"m{j}"))
                act(q(8), q(3), ACT.Ln, scale=1.0, bias=1.0)
                act(q(9), q(3), ACT.Ln, scale=-1.0, bias=1.0).then_inc(s["funcs"][g], 1)

            def rstd(g, j):
                q = lambda i: st[:, j, i, T(g)]
                a.wait_ge(s["vals"][g], nth(VALS, f"var{j}"))
                act(q(14), q(13), ACT.Sqrt).then_inc(s["funcs"][g], 1)

            def normalise(g, j, src):
                a.wait_ge(s["vals"][g], nth(VALS, f"nb{j}"))
                for t in tiles(g)[1::2]:
                    act(xn[:, t, :], src[:, t, :], ACT.Identity, scale=st[:, j, 15, t:t + 1],
                        bias=st[:, j, 16, t:t + 1]).then_inc(s["xn_odd"][g], 1)

            def square_y(g, j):
                a.wait_ge(s["yT_ready"][g], j + 1)
                act(ysq[:, g, :], yT[:, g, :], ACT.Square).then_inc(s["ysq_ready"][g], 1)

            def norm_y(g, j):
                a.wait_ge(s["yss_mm"][g], j + 1)
                act(st[:, j, 0, T(g)], bk(g, 1)[:, 0:TG], ACT.Sqrt, bias=tiny).then_inc(s["funcs"][g], 1)

            def square_qkv(g):
                for i, t in enumerate(tiles(g)):
                    a.wait_ge(s["qkv_ready"][g], i + 1)
                    act(qsq[g][:, i * 3 * D:(i + 1) * 3 * D], qkv[:, t, :], ACT.Square).then_inc(s["qsq_ready"][g], 1)

            def head_norms(g):
                a.wait_ge(s["vals"][g], nth(VALS, "head"))
                act(heads[:, g, 1, :], heads[:, g, 0, :], ACT.Sqrt, bias=tiny).then_inc(s["funcs"][g], 1)

            def copy_qT(g):
                a.wait_ge(s["trans_mm"][g], nth(TRANS, "qT"))
                act(qT[:, g, :], bk(g, 0)[:, :], ACT.Copy).then_inc(s["qT_ready"][g], 1)

            def exps(g):
                for k, i in enumerate(BANKS):
                    a.wait_ge(s["sc_mm"][g], 1 if k < 3 else 2)
                    act(prob[:, g, i, :], bk(g, i)[:, :], ACT.Exp, scale=HD ** -0.5).then_inc(s["p_ready"][g], 1)

            def silu_exp():
                act(silu[:], col[:, K_COND:K_COND + B], ACT.Exp, scale=-1.0).then_inc(s["silu_e"], 1)

            def copy_probs(g):
                for k in (1, 3):
                    i = BANKS[k]
                    a.wait_ge(s["pT_mm"][g], k + 1)
                    act(probT[:, g, i, :], bk(g, i)[:, :], ACT.Copy).then_inc(s["pT_odd"][g], 1)

            def copy_o(g):
                a.wait_ge(s["o_mm"][g], 1)
                for i in range(2):
                    t = g * TG + 2 * i
                    act(o[:, t:t + 2].rearrange("p t n w -> p (t n w)"), bk(g, i)[:, 0:2 * NHG * VW],
                        ACT.Copy).then_inc(s["o_ready"][g], 1)
                a.wait_ge(s["o_ready"][g], 2)
                act(osq[:, T(g), :].rearrange("p t (n w) -> p (t n) w", w=HG * HD),
                    o[:, T(g)].rearrange("p t n w -> p (t n) w")[:, :, 0:HG * HD], ACT.Square).then_inc(s["osq_ready"][g], 1)

            def out_norms(g):
                a.wait_ge(s["vals"][g], nth(VALS, "out"))
                act(oo(g, 2), oo(g, 1), ACT.Sqrt, bias=tiny).then_inc(s["funcs"][g], 1)

            def copy_ainT(g):
                a.wait_ge(s["trans_mm"][g], nth(TRANS, "ainT"))
                act(ainT[:, g, :], bk(g, 2)[:, :], ACT.Copy).then_inc(s["ainT_ready"][g], 1)

            def token_norms(g):
                a.wait_ge(s["vals"][g], nth(VALS, "tok"))
                act(onrm[:, 1, T(g)], onrm[:, 0, T(g)], ACT.Sqrt, bias=tiny).then_inc(s["funcs"][g], 1)

            def branch_squares(g, j):
                n0 = j * TG

                def square(i, src, ready, lane, q):
                    t = g * TG + i
                    a.wait_ge(s[ready][g], n0 + i + 1)
                    act(qk[:, t, lane * D:(lane + 1) * D], src[:, t, :], ACT.Square,
                        accum_out=st[:, j, q, t:t + 1]).then_inc(s["sq_done"][g], 1)

                for i in range(TG + 1):
                    if i < TG:
                        square(i, ap, "ap_ready", 0, 20)
                    if i:
                        square(i - 1, gt, "gt_ready", 1, 21)
                a.wait_ge(s["sq_done"][g], 2 * (n0 + TG))
                act(st[:, j, 20:22, T(g)], st[:, j, 20:22, T(g)], ACT.Sqrt, bias=tiny).then_inc(s["funcs"][g], 1)

            def tanh_norm(g, j):
                a.wait_ge(s["vals"][g], nth(VALS, f"n{j}"))
                act(st[:, j, 22, T(g)], st[:, j, 20, T(g)], ACT.Tanh).then_inc(s["funcs"][g], 1)

            def branch_scaled(g, j):
                a.wait_ge(s["vals"][g], nth(VALS, f"beta{j}"))
                for t in tiles(g) if j == 0 else tiles(g)[1::2]:
                    act(tmp[:, t, :], gt[:, t, :], ACT.Copy, scale=st[:, j, 3, t:t + 1]).then_inc(s["xtmp_mid"][g], 1)

            def copy_rsb(g):
                a.wait_ge(s["rsb_mm"][g], 1)
                act(rsb[:, g, :], bk(g, 2)[:, :], ACT.Copy).then_inc(s["rsb_ready"][g], 1)

            def square_hidden(g):
                for c in range(FC):
                    a.wait_ge(s["hf_ready"][g], c + 1)
                    act(hsq[:, g, c, :], hf[:, g, c, :], ACT.Square).then_inc(s["hsq_ready"][g], 1)

            def hidden_norms(g):
                a.wait_ge(s["hss_mm"][g], 1)
                act(onrm[:, 3, T(g)], bk(g, 1)[:, 0:TG], ACT.Sqrt, bias=tiny).then_inc(s["funcs"][g], 1)

            def x3_high(g):
                a.wait_ge(s["trans_mm"][g], nth(TRANS, "x3T"))
                act(x3hi[:, g, :], bk(g, 3)[:, :], ACT.Copy).then_inc(s["x3hi_ready"][g], 1)

            def gate_exp(g):
                a.wait_ge(s["vals"][g], nth(VALS, "logit"))
                act(gl[:, g, 1, :], gl[:, g, 0, :], ACT.Exp, bias=gs[:, g, 0:1]).then_inc(s["funcs"][g], 1)

            def gelu(g, e):
                if e >= 2:
                    a.wait_ge(s["moe_y"][g], e - 1)
                for c in range(FC):
                    a.wait_ge(s["moe_up"][g], e * FC + c + 1)
                    act(hT[e % 2][:, g, c, :], bk(g, (e * FC + c) % 3)[:, :], ACT.Gelu_apprx_tanh,
                        bias=col[:, K_EB1 + e * FC + c:K_EB1 + e * FC + c + 1]).then_inc(s["moe_h"][g], 1)

            a.dma_start(cst[:], consts).then_inc(s["consts_in"], 16)
            a.dma_start(col[:], cols).then_inc(s["consts_in"], 16)
            a.dma_start(wada, w_ada).then_inc(s["wada_in"], 16)
            a.dma_start(sel[:], sels).then_inc(s["sels_in"], 16)
            a.wait_ge(s["consts_in"], 32)
            silu_exp()
            logs(0, 0)
            rstd(0, 0)
            normalise(0, 0, xin)
            logs(1, 0)
            square_y(0, 0)
            rstd(1, 0)
            normalise(1, 0, xin)
            norm_y(0, 0)
            square_qkv(0)
            square_y(1, 0)
            head_norms(0)
            norm_y(1, 0)
            copy_qT(0)
            square_qkv(1)
            head_norms(1)
            exps(0)
            copy_probs(0)
            copy_o(0)
            out_norms(0)
            copy_qT(1)
            copy_ainT(0)
            token_norms(0)
            branch_squares(0, 0)
            tanh_norm(0, 0)
            branch_scaled(0, 0)
            exps(1)
            logs(0, 1)
            copy_probs(1)
            rstd(0, 1)
            normalise(0, 1, x1)
            copy_o(1)
            out_norms(1)
            square_y(0, 1)
            norm_y(0, 1)
            copy_ainT(1)
            token_norms(1)
            branch_squares(1, 0)
            copy_rsb(0)
            tanh_norm(1, 0)
            square_hidden(0)
            branch_scaled(1, 0)
            logs(1, 1)
            hidden_norms(0)
            rstd(1, 1)
            normalise(1, 1, x1)
            branch_squares(0, 1)
            tanh_norm(0, 1)
            square_y(1, 1)
            branch_scaled(0, 1)
            norm_y(1, 1)
            x3_high(0)
            copy_rsb(1)
            gelu(0, 0)
            gate_exp(0)
            square_hidden(1)
            gelu(0, 1)
            hidden_norms(1)
            branch_squares(1, 1)
            gelu(0, 2)
            tanh_norm(1, 1)
            gelu(0, 3)
            branch_scaled(1, 1)
            x3_high(1)
            gelu(0, 4)
            gelu(1, 0)
            gate_exp(1)
            gelu(1, 1)
            gelu(1, 2)
            gelu(1, 3)
            gelu(1, 4)

        @block.gpsimd
        def _(p):
            vm = cst[:, C_VM:C_VM + HG]
            n = TG * BT * NHG

            def start():
                nc_p.memset(half[:], 0.5).then_inc(s["pool_step"], 1)
                p.wait_ge(s["pool_step"], 1)
                p.wait_ge(s["consts_in"], 32)
                for g in range(NG):
                    vd = vexp[:, g].rearrange("p r n w -> p (r n) w")
                    nc_p.tensor_copy(vd[:, :, HG * HD:VW], vm.unsqueeze(1).broadcast_to([P, n, HG]))

            def biases(g):
                p.wait_ge(s["rows_in"], 16)
                p.wait_ge(s["wtok_ready"][g], 1)
                b2 = lambda e: row[:, R_B2 + e * D:R_B2 + (e + 1) * D].unsqueeze(1).broadcast_to([P, TG, D])
                prod = yT[:, g, :].rearrange("p (t d) -> p t d", d=D)
                for e in range(E + 1):
                    if e < E:
                        w = wtok[:, e, T(g)].unsqueeze(2).broadcast_to([P, TG, D])
                        nc_p.tensor_tensor(prod if e else bacc[:, T(g), :], b2(e), w, ALU.mult) \
                            .then_inc(s["bias_ready"][g], 1)
                    if e:
                        p.wait_ge(s["bias_ready"][g], min(2 * e, 2 * E - 1))
                        nc_p.tensor_tensor(bacc[:, T(g), :], bacc[:, T(g), :], prod if e < E else b2(E), ALU.add) \
                            .then_inc(s["bias_ready"][g], 1)
                        if e < E - 1:
                            p.wait_ge(s["bias_ready"][g], 2 * e + 1)

            def root_mean_square(g, j):
                p.wait_ge(s["vals"][g], nth(VALS, f"mean{j}"))
                nc_p.tensor_tensor(st[:, j, 2, T(g)], st[:, j, 1, T(g)], half[:].broadcast_to([P, TG]), ALU.pow) \
                    .then_inc(s["rms_ready"][g], 1)

            def clamp_v(g):
                p.wait_ge(s["c_ready"][g], 1)
                c = heads[:, g, 3, 0:TG * 3 * H].rearrange("p (t h) -> p t h", t=TG)[:, :, 2 * H:3 * H]
                nc_p.tensor_tensor(vs[:, T(g), :].rearrange("p t (h d) -> p t h d", d=HD),
                                   qkv[:, T(g), 2 * D:3 * D].rearrange("p t (h d) -> p t h d", d=HD),
                                   c.unsqueeze(3).broadcast_to([P, TG, H, HD]), ALU.mult).then_inc(s["v_ready"][g], 1)

            def expand_v(g):
                vd = vexp[:, g].rearrange("p r n w -> p (r n) w")
                p.wait_ge(vrep_in[g], 16 * HG)
                nc_p.tensor_tensor(vd[:, :, 0:HG * HD].rearrange("p n (h d) -> p n h d", d=HD),
                                   vrep[:, g].rearrange("p r (n h d) -> p (r n) h d", h=HG, d=HD),
                                   vm.unsqueeze(1).broadcast_to([P, n, HG]).unsqueeze(3).broadcast_to([P, n, HG, HD]),
                                   ALU.mult).then_inc(s["vexp_ready"][g], 1)

            def split_up(e):
                p.wait_ge(w_in[e], 32)
                nc_p.tensor_copy(whi[:, e, :], wup[e]).then_inc(s["pool_step"], 1)
                p.wait_ge(s["pool_step"], e + 2)
                nc_p.tensor_tensor(wlo[:, e, :], wup[e], whi[:, e, :].bitcast(f32), ALU.subtract).then_inc(s["split"], 1)

            def pair_squares(g):
                p.wait_ge(s["hsq_ready"][g], 2)
                nc_p.tensor_tensor(hsq[:, g, 0, :], hsq[:, g, 0, :], hsq[:, g, 1, :], ALU.add).then_inc(s["hpair_ready"][g], 1)

            def add_x(g):
                for i, t in enumerate(tiles(g)[1::2]):
                    p.wait_ge(s["xtmp_mid"][g], TG + i + 1)
                    nc_p.tensor_tensor(tmp[:, t, :], tmp[:, t, :], xin[:, t, :], ALU.add).then_inc(s["xtmp_odd"][g], 1)

            start()
            root_mean_square(1, 0)
            root_mean_square(0, 0)
            clamp_v(0)
            expand_v(0)
            clamp_v(1)
            expand_v(1)
            split_up(0)
            split_up(1)
            split_up(2)
            root_mean_square(0, 1)
            pair_squares(0)
            root_mean_square(1, 1)
            add_x(0)
            split_up(3)
            split_up(4)
            pair_squares(1)
            add_x(1)
            biases(1)
            biases(0)

        @block.tensor
        def _(pe):
            mm, tr = nc_t.matmul, nc_t.transpose

            def ada():
                cond = col[:, K_COND:K_COND + B]
                pe.wait_ge(s["consts_in"], 32)
                pe.wait_ge(s["wada_in"], 16)
                for j, c in enumerate((0, 1, 3, 4)):
                    last = mm(bank[0][:, j * B:(j + 1) * B], wada[:, c * D:(c + 1) * D], cond, start=True, stop=True)
                last.then_inc(s["ada_mm"], 1)
                for i, c in enumerate((2, 5)):
                    last = mm(bank[4][0:B, i * D:(i + 1) * D], cond, wada[:, c * D:(c + 1) * D], start=True, stop=True)
                last.then_inc(s["ada_mm"], 1)

            def transpose_group(dst, src, g):
                for i, t in enumerate(tiles(g)):
                    last = tr(dst[:, i * P:(i + 1) * P], src[:, t, :], ident)
                last.then_inc(s["trans_mm"][g], 1)

            def norm_rows(g, j):
                pe.wait_ge(s["ones_ready"], 1)
                pe.wait_ge(s["ysq_ready"][g], j + 1)
                if j == 1:
                    pe.wait_ge(s["silu_ready"], 1)
                    mm(bk(g, 1)[0:GB, 8:8 + 2 * E], silu[:, g * GB:(g + 1) * GB], col[:, K_TW:K_TW + 2 * E],
                       start=True, stop=True)
                for i in range(TG):
                    last = mm(bk(g, 1)[:, i:i + 1], ysq[:, g, i * P:(i + 1) * P], ones[:], start=True, stop=True)
                last.then_inc(s["yss_mm"][g], 1)

            def xn_transposed(g, j):
                pe.wait_ge(s["xn_even"][g], (j + 1) * TG // 2)
                pe.wait_ge(s["xn_odd"][g], (j + 1) * TG // 2)
                if j == 0:
                    if g == 0:
                        pe.wait_ge(s["adaT_ready"], 4)
                    else:
                        pe.wait_ge(s["adag_ready"], 1)
                transpose_group(bk(g, 0), xn, g)

            def project(g, ts):
                pe.wait_ge(s["wqkv_in"], 16)
                for t in ts:
                    if (t + 2) % 4 == 1:
                        pe.wait_ge(s["funcs"][g], nth(FUNCS, "y0"))
                    mm(bk(g, (t + 2) % 4)[:, 0:3 * D], yT[:, g, t * P:(t + 1) * P], wqkv[:],
                       start=True, stop=True).then_inc(s["qkv_mm"][g], 1)

            def project_first(g):
                pe.wait_ge(s["yT_ready"][g], 1)
                project(g, range(TG - 1))

            def project_last(g):
                project(g, (TG - 1,))

            def transpose_qk(g):
                pe.wait_ge(s["qk_ready"][g], 1)
                for half in range(2):
                    transpose_group(bk(g, half), qk[:, :, half * D:(half + 1) * D], g)

            def scores(g):
                pe.wait_ge(s["qT_ready"][g], 1)
                for heads4 in (BANKS[:3], BANKS[3:]):
                    for t in range(TG):
                        pe.wait_ge(s["kexp_ready"][g], t + 1 if len(heads4) > 1 else TG)
                        for n in heads4:
                            for b in range(BT):
                                r = t * BT + b
                                last = mm(bk(g, n)[b * S:(b + 1) * S, t * P:(t + 1) * P],
                                          qT[n * 32:(n + 1) * 32, g, r * S:(r + 1) * S],
                                          kexp[n * 32:(n + 1) * 32, g, r].rearrange("p h s -> p (h s)"),
                                          start=True, stop=True)
                    last.then_inc(s["sc_mm"][g], 1)

            def transpose_probs(g):
                for k, n in enumerate(BANKS):
                    pe.wait_ge(s["p_ready"][g], k + 1)
                    for t in range(TG):
                        last = tr(bk(g, n)[:, t * P:(t + 1) * P], prob[:, g, n, t * P:(t + 1) * P], ident)
                    last.then_inc(s["pT_mm"][g], 1)

            def weigh_v(g):
                pe.wait_ge(s["pT_even"][g], 2)
                pe.wait_ge(s["pT_odd"][g], 2)
                pe.wait_ge(s["vexp_ready"][g], 1)
                for t in range(TG):
                    for n in range(NHG):
                        c = ((t % 2) * NHG + n) * VW
                        for b in range(BT):
                            last = mm(bk(g, t // 2)[b * S:(b + 1) * S, c:c + VW],
                                      probT[:, g, n, t * P + b * S:t * P + (b + 1) * S],
                                      vexp[:, g, t * BT + b, n, :], start=True, stop=True)
                last.then_inc(s["o_mm"][g], 1)

            def transpose_ain(g):
                pe.wait_ge(s["ain_ready"][g], 1)
                transpose_group(bk(g, 2), ain, g)

            def project_out(g):
                pe.wait_ge(s["wmlp_in"], 48)
                pe.wait_ge(s["ainT_ready"][g], 1)
                for t in range(TG):
                    last = mm(bk(g, 3)[:, t * D:(t + 1) * D], ainT[:, g, t * P:(t + 1) * P], wo[:], start=True, stop=True)
                last.then_inc(s["ap_mm"][g], 1)

            def up_mlp(g, chunks):
                pe.wait_ge(s["yT_ready"][g], 2)
                for i in chunks:
                    mm(bk(g, UPB[i])[:, :], wf1[:, i * P:(i + 1) * P], yT[:, g, :], start=True, stop=True) \
                        .then_inc(s["up_mm"][g], 1)

            def spread_rs(g):
                pe.wait_ge(s["rs_ready"][g], 1)
                for t in range(TG):
                    tt = g * TG + t
                    last = mm(bk(g, 2)[:, t * P:(t + 1) * P], st[:, 1, 18, tt:tt + 1].broadcast_to([P, P]), ident,
                              start=True, stop=True)
                last.then_inc(s["rsb_mm"][g], 1)

            def up_mlp2(g):
                pe.wait_ge(s["mod_ready"][g], 1)
                up_mlp(g, (2,))

            def up_mlp3(g):
                pe.wait_ge(s["rsb_ready"][g], 1)
                up_mlp(g, (3,))

            def hidden_norms(g):
                pe.wait_ge(s["hsum_ready"][g], 1)
                for t in range(TG):
                    last = mm(bk(g, 1)[:, t:t + 1], hsq[:, g, 0, t * P:(t + 1) * P], ones[:], start=True, stop=True)
                last.then_inc(s["hss_mm"][g], 1)

            def mlp_out(g):
                pe.wait_ge(s["hf_ready"][g], FC)
                for t in range(TG):
                    for c in range(FC):
                        last = mm(bk(g, 0)[:, t * D:(t + 1) * D], hf[:, g, c, t * P:(t + 1) * P], wf2[:, c, :],
                                  start=c == 0, stop=c == FC - 1)
                last.then_inc(s["f_mm"][g], 1)

            def transpose_x3(g):
                pe.wait_ge(s["x3_ready"][g], TG)
                transpose_group(bk(g, 3), x3, g)

            def gate(g):
                pe.wait_ge(s["agg_ready"][g], 1)
                pe.wait_ge(s["x3lo_ready"][g], 1)
                for j in range(3):
                    last = mm(bk(g, 3)[0:GB, 0:E], agg[:, g, j, :], col[:, K_GW + j * E:K_GW + (j + 1) * E],
                              start=j == 0, stop=j == 2)
                last.then_inc(s["gate_mm"][g], 1)

            def token_weights(g):
                pe.wait_ge(s["sels_in"], 16)
                pe.wait_ge(s["w_ready"][g], 1)
                for t in range(TG):
                    last = mm(bk(g, 3)[:, 8 + E * t:8 + E * (t + 1)], sel[0:GB, S_SEL + t * P:S_SEL + (t + 1) * P],
                              gl[:, g, 5, :], start=True, stop=True)
                last.then_inc(s["gate_mm"][g], 1)

            def up(g, e):
                pe.wait_ge(s["x3lo_ready"][g], 1)
                pe.wait_ge(s["split"], e + 1)
                lo, hi, xlo, xhi = wlo[:, e, :], whi[:, e, :], x3lo[:, g, :], x3hi[:, g, :]
                for c in range(FC):
                    k = e * FC + c
                    if k >= 3:
                        pe.wait_ge(s["moe_h"][g], k - 2)
                    z = bk(g, k % 3)[:, :]
                    mm(z, hi[:, c * P:(c + 1) * P], xhi, start=True, stop=False)
                    mm(z, lo[:, c * P:(c + 1) * P], xhi, start=False, stop=False)
                    mm(z, hi[:, c * P:(c + 1) * P], xlo, start=False, stop=True).then_inc(s["moe_up"][g], 1)

            def down(g, e):
                pe.wait_ge(s["moe_h"][g], FC * (e + 1))
                pe.wait_ge(w_in[e], 32)
                if e == 0:
                    pe.wait_ge(s["wtok_ready"][g], 1)
                else:
                    pe.wait_ge(s["moe_acc"][g], e + (e > 3))
                for t in range(TG):
                    d = bk(g, 3)[:, t * D:(t + 1) * D]
                    if e == E:
                        d = bk(g, LAST[t // 2])[:, t % 2 * D:(t % 2 + 1) * D]
                    for c in range(FC):
                        last = mm(d, hT[e % 2][:, g, c, t * P:(t + 1) * P], wdn[e][:, c, :],
                                  start=c == 0, stop=c == FC - 1)
                    if t == TG - 1 or (e == E and t == TG // 2 - 1):
                        last.then_inc(s["moe_y"][g], 1)

            ada()
            xn_transposed(0, 0)
            norm_rows(0, 0)
            project_first(0)
            project_last(0)
            xn_transposed(1, 0)
            norm_rows(1, 0)
            project_first(1)
            project_last(1)
            transpose_qk(0)
            scores(0)
            transpose_probs(0)
            transpose_qk(1)
            weigh_v(0)
            transpose_ain(0)
            project_out(0)
            scores(1)
            transpose_probs(1)
            weigh_v(1)
            xn_transposed(0, 1)
            up_mlp(0, (0,))
            up_mlp(0, (1,))
            norm_rows(0, 1)
            transpose_ain(1)
            project_out(1)
            spread_rs(0)
            up_mlp2(0)
            up_mlp3(0)
            mlp_out(0)
            hidden_norms(0)
            xn_transposed(1, 1)
            up_mlp(1, (0,))
            norm_rows(1, 1)
            up_mlp(1, (1,))
            transpose_x3(0)
            spread_rs(1)
            up_mlp2(1)
            up(0, 0)
            up_mlp3(1)
            gate(0)
            mlp_out(1)
            up(0, 1)
            token_weights(0)
            hidden_norms(1)
            down(0, 0)
            up(0, 2)
            down(0, 1)
            up(0, 3)
            down(0, 2)
            transpose_x3(1)
            up(0, 4)
            up(1, 0)
            gate(1)
            down(0, 3)
            up(1, 1)
            token_weights(1)
            down(1, 0)
            up(1, 2)
            down(1, 1)
            up(1, 3)
            down(1, 2)
            up(1, 4)
            down(1, 3)
            down(0, 4)
            down(1, 4)


_OUT = (B, S, D)


def _constants(np):
    c = np.zeros((P, C_END), np.float32)
    i = np.arange(P)
    c[:, C_ID:C_ID + P] = np.eye(P)
    c[:, C_HM:C_HM + HG] = (i[:, None] // HD) % HG == np.arange(HG)
    c[:, C_VM:C_VM + HG] = i[:, None] // S == np.arange(HG)
    keep = np.ones((S, E))
    keep[SEG:2 * SEG, 1] = 0
    keep[0:SEG, 2] = 0
    c[:, C_WM:C_WM + E] = np.tile(keep, (BT, 1))
    c[:, C_TRI:C_TRI + E * E] = np.tril(np.ones((E, E)), -1).reshape(1, -1)
    c[:, C_TINY] = TINY
    m = np.zeros((GB, S_END), np.float32)
    m[:, S_SEL:S_SEL + GT] = np.arange(GT)[None, :] // S == np.arange(GB)[:, None]
    return c, m


def kernel(**inputs):
    import numpy as np
    import concourse.bacc as bacc
    from concourse.bass_utils import run_bass_kernel_spmd

    a = {k: np.asarray(v) for k, v in inputs.items()}
    L0 = lambda n: a["L0_cond_" + n]
    L1 = lambda n: a["L1_cond_" + n]
    chunks = lambda w: np.ascontiguousarray(w.reshape(FC, P, D).transpose(1, 0, 2).reshape(P, FC * D))
    bada = L0("b_ada").reshape(6, D)
    eb1 = np.concatenate([L1("eb1"), L1("sb1")[None]]).reshape((E + 1) * FC, P)
    consts, sels = _constants(np)
    arrays = {
        "x": a["x"].reshape(TILES, P, D),
        "consts": consts,
        "sels": sels,
        "cols": np.concatenate([a["cond_1024"].T, bada[[0, 1, 3, 4]].T, L0("b_f1").reshape(FC, P).T, eb1.T,
                                L1("gate_w").reshape(3, D, E).transpose(1, 0, 2).reshape(D, 3 * E), L1("time_w")], axis=1),
        "rows": np.concatenate([L0("b_q"), L0("b_k"), L0("b_v"), L0("b_o"), L0("b_f2"), bada[2], bada[5],
                                L1("gate_b"), L1("time_b"), *L1("eb2"), L1("sb2")])[None],
        "w_ada": L0("w_ada"),
        "w_qkv": np.concatenate([L0("w_q"), L0("w_k"), L0("w_v")], axis=1),
        "w_o": L0("w_o"),
        "w_f1": L0("w_f1"),
        "w_f2": chunks(L0("w_f2")),
        "w_up": np.concatenate([L1("ew1"), L1("sw1")[None]]),
        "w_down": np.stack([chunks(w) for w in [*L1("ew2"), L1("sw2")]]),
    }
    nc = bacc.Bacc("TRN2", target_bir_lowering=False, num_devices=1)
    aps = []
    for name in arrays:
        arrays[name] = np.ascontiguousarray(arrays[name])
        aps.append(nc.dram_tensor(name, arrays[name].shape, mybir.dt.from_np(arrays[name].dtype),
                                  kind="ExternalInput").ap())
    out = nc.dram_tensor("out", (TILES, P, D), mybir.dt.float32, kind="ExternalOutput").ap()
    cond_resid_kernel(nc, *aps, out)
    r = run_bass_kernel_spmd(nc, [arrays], core_ids=[0])
    return r.results[0]["out"].reshape(_OUT)
```
